# Optimizing a Trainium2 kernel written in Bass

```python
import numpy as np
import jax
import jax.numpy as jnp

def _softmax(x, axis=-1):
    return jax.nn.softmax(x, axis=axis)

def _gelu(x):
    return jax.nn.gelu(x, approximate=True)

def _silu(x):
    return jax.nn.silu(x)

def _sigmoid(x):
    return jax.nn.sigmoid(x)

def _layernorm(x, axis=-1, eps=1e-05):
    m = jnp.mean(x, axis=axis, keepdims=True)
    v = jnp.var(x, axis=axis, keepdims=True)
    return (x - m) / jnp.sqrt(v + eps)

def _scatter_add(tgt, idx, src, axis=0):
    return tgt.at[idx].add(src)

def _segment_sum(src, seg, n):
    return jax.ops.segment_sum(src, seg, n)
kernel_name = 'mk_hybrid_d1_jaxref_r8_9e6b59'

def setup_inputs(seed: int=0):
    np.random.seed(seed)
    _w = jnp.asarray

    def _L0_attn_a_setup():
        import jax, jax.numpy as jnp
        import numpy as np
        NUM_HEADS = 16
        ROPE_BASE = 10000.0
        QK_GAIN_INIT = 12.0
        EPS = 1e-06
        ROPE_MASK = jnp.asarray(np.tile([1.0, 0.0], NUM_HEADS // 2), dtype=jnp.float32)

        def _rope_cos_sin(seqlen, head_dim, dtype):
            half = head_dim // 2
            inv_freq = ROPE_BASE ** (-jnp.arange(0, half, dtype=jnp.float32) / half)
            theta = jnp.arange(seqlen, dtype=jnp.float32)[:, None] * inv_freq[None, :]
            return (jnp.cos(theta).astype(dtype), jnp.sin(theta).astype(dtype))

        def _apply_rope(t, cos, sin):
            d2 = t.shape[-1] // 2
            t1, t2 = (t[..., :d2], t[..., d2:])
            c = cos[None, :, None, :]
            s = sin[None, :, None, :]
            return jnp.concatenate([t1 * c - t2 * s, t1 * s + t2 * c], axis=-1)

        def _unit_norm(t):
            return t * jax.lax.rsqrt(jnp.sum(t * t, axis=-1, keepdims=True) + EPS)
        key = jax.random.key(seed)
        k0, k1, k2 = jax.random.split(key, 3)
        B, S, Dm = (2, 256, 256)
        x = jax.random.normal(k0, (B, S, Dm), dtype=jnp.float32)
        w_qkv = jax.random.normal(k1, (Dm, 3 * Dm), dtype=jnp.float32) * Dm ** (-0.5)
        w_out = jax.random.normal(k2, (Dm, Dm), dtype=jnp.float32) * Dm ** (-0.5)
        q_gain = jnp.full((NUM_HEADS,), QK_GAIN_INIT, dtype=jnp.float32)
        return {'x': x, 'w_qkv': w_qkv, 'w_out': w_out, 'q_gain': q_gain}
    _L0_attn_a_in = _L0_attn_a_setup()

    def _L0_attn_b_setup():
        import jax, jax.numpy as jnp
        import numpy as np
        B, SQ, H = (2, 256, 256)
        NH = 16
        HN = H // NH
        key = jax.random.key(seed)
        ks = jax.random.split(key, 6)
        query = jax.random.normal(ks[0], (B, SQ, H), dtype=jnp.float32)
        k_in = jax.random.normal(ks[1], (B, SQ, H), dtype=jnp.float32)
        v_in = jax.random.normal(ks[2], (B, SQ, H), dtype=jnp.float32)
        Wqkv = jax.random.normal(ks[3], (3 * H, H), dtype=jnp.float32) * (1.0 / np.sqrt(H))
        Wproj = jax.random.normal(ks[4], (H, H), dtype=jnp.float32) * (1.0 / np.sqrt(H))
        bproj = jnp.zeros((H,), dtype=jnp.float32)
        return {'query': query, 'key': k_in, 'value': v_in, 'Wqkv': Wqkv, 'Wproj': Wproj, 'bproj': bproj}
    _L0_attn_b_in = _L0_attn_b_setup()

    def _L0_ffn_setup():
        import jax, jax.numpy as jnp
        import numpy as np
        B, T, D = (2, 128, 256)
        E, F, K = (64, 64, 4)
        S, HS = (2, 64 * 4)
        key = jax.random.key(seed)
        ks = jax.random.split(key, 9)
        s = 0.02
        f32 = jnp.float32
        return {'x': jax.random.normal(ks[0], (B, T, D), f32), 'router_w': jax.random.normal(ks[1], (D, E), f32) * s, 'router_bias': jnp.zeros((E,), f32), 'wg': jax.random.normal(ks[2], (E, D, F), f32) * s, 'wu': jax.random.normal(ks[3], (E, D, F), f32) * s, 'wd': jax.random.normal(ks[4], (E, F, D), f32) * s, 'swg': jax.random.normal(ks[5], (S, D, HS), f32) * s, 'swu': jax.random.normal(ks[6], (S, D, HS), f32) * s, 'swd': jax.random.normal(ks[7], (S, HS, D), f32) * s}
    _L0_ffn_in = _L0_ffn_setup()
    _d = {'L0_attn_a_x': _L0_attn_a_in['x'], 'L0_attn_a_w_qkv': _L0_attn_a_in['w_qkv'], 'L0_attn_a_w_out': _L0_attn_a_in['w_out'], 'L0_attn_a_q_gain': _L0_attn_a_in['q_gain'], 'L0_attn_b_key': _L0_attn_b_in['key'], 'L0_attn_b_value': _L0_attn_b_in['value'], 'L0_attn_b_Wqkv': _L0_attn_b_in['Wqkv'], 'L0_attn_b_Wproj': _L0_attn_b_in['Wproj'], 'L0_attn_b_bproj': _L0_attn_b_in['bproj'], 'L0_ffn_router_w': _L0_ffn_in['router_w'], 'L0_ffn_router_bias': _L0_ffn_in['router_bias'], 'L0_ffn_wg': _L0_ffn_in['wg'], 'L0_ffn_wu': _L0_ffn_in['wu'], 'L0_ffn_wd': _L0_ffn_in['wd'], 'L0_ffn_swg': _L0_ffn_in['swg'], 'L0_ffn_swu': _L0_ffn_in['swu'], 'L0_ffn_swd': _L0_ffn_in['swd']}
    _x0 = _d['L0_attn_a_x']
    _d['L0_attn_a_x'] = jax.random.normal(jax.random.fold_in(jax.random.key(seed), 1), (8, 256, 256), dtype=_x0.dtype)
    del _x0
    return _d

def reference(L0_attn_a_x, L0_attn_a_w_qkv, L0_attn_a_w_out, L0_attn_a_q_gain, L0_attn_b_key, L0_attn_b_value, L0_attn_b_Wqkv, L0_attn_b_Wproj, L0_attn_b_bproj, L0_ffn_router_w, L0_ffn_router_bias, L0_ffn_wg, L0_ffn_wu, L0_ffn_wd, L0_ffn_swg, L0_ffn_swu, L0_ffn_swd):

    def _L0_attn_a_ref(x, w_qkv, w_out, q_gain):
        import jax, jax.numpy as jnp
        import numpy as np
        NUM_HEADS = 16
        ROPE_BASE = 10000.0
        QK_GAIN_INIT = 12.0
        EPS = 1e-06
        ROPE_MASK = jnp.asarray(np.tile([1.0, 0.0], NUM_HEADS // 2), dtype=jnp.float32)

        def _rope_cos_sin(seqlen, head_dim, dtype):
            half = head_dim // 2
            inv_freq = ROPE_BASE ** (-jnp.arange(0, half, dtype=jnp.float32) / half)
            theta = jnp.arange(seqlen, dtype=jnp.float32)[:, None] * inv_freq[None, :]
            return (jnp.cos(theta).astype(dtype), jnp.sin(theta).astype(dtype))

        def _apply_rope(t, cos, sin):
            d2 = t.shape[-1] // 2
            t1, t2 = (t[..., :d2], t[..., d2:])
            c = cos[None, :, None, :]
            s = sin[None, :, None, :]
            return jnp.concatenate([t1 * c - t2 * s, t1 * s + t2 * c], axis=-1)

        def _unit_norm(t):
            return t * jax.lax.rsqrt(jnp.sum(t * t, axis=-1, keepdims=True) + EPS)
        B, S, Dm = x.shape
        H = NUM_HEADS
        D = Dm // H
        qkv = (x @ w_qkv).reshape(B, S, 3, H, D)
        q, k, v = (qkv[:, :, 0], qkv[:, :, 1], qkv[:, :, 2])
        q = _unit_norm(q)
        k = _unit_norm(k)
        cos, sin = _rope_cos_sin(S, D, x.dtype)
        m = ROPE_MASK[None, None, :, None]
        q = m * _apply_rope(q, cos, sin) + (1.0 - m) * q
        k = m * _apply_rope(k, cos, sin) + (1.0 - m) * k
        logits = jnp.einsum('bshd,bthd->bhst', q, k) * q_gain[None, :, None, None]
        causal = jnp.tril(jnp.ones((S, S), dtype=bool))
        logits = jnp.where(causal[None, None], logits, jnp.finfo(logits.dtype).min)
        attn = jax.nn.softmax(logits, axis=-1)
        y = jnp.einsum('bhst,bthd->bshd', attn, v).reshape(B, S, Dm)
        return y @ w_out

    def _L0_attn_b_ref(query, key, value, Wqkv, Wproj, bproj):
        import jax, jax.numpy as jnp
        import numpy as np
        B, SQ, H = (2, 256, 256)
        NH = 16
        HN = H // NH
        b, sq, h = query.shape
        nh, hn = (NH, HN)
        norm = 1.0 / jnp.sqrt(jnp.asarray(hn, query.dtype))
        x = jnp.transpose(query, (1, 0, 2)).reshape(sq * b, h)
        mixed = x @ Wqkv.T
        mixed = mixed.reshape(sq, b, nh, 3, hn)
        q = mixed[..., 0, :]
        k = mixed[..., 1, :]
        v = mixed[..., 2, :]
        q = q.reshape(sq, b * nh, hn).transpose(1, 0, 2)
        k = k.reshape(sq, b * nh, hn).transpose(1, 0, 2)
        v = v.reshape(sq, b * nh, hn).transpose(1, 0, 2)
        attn = jnp.einsum('gqd,gkd->gqk', q, k) * norm
        attn = jax.nn.softmax(attn, axis=-1)
        ctx = jnp.einsum('gqk,gkd->gqd', attn, v)
        ctx = ctx.reshape(nh, b, sq, hn)
        ctx = jnp.transpose(ctx, (2, 1, 0, 3)).reshape(sq * b, h)
        out = ctx @ Wproj.T + bproj
        out = out.reshape(sq, b, h)
        return jnp.transpose(out, (1, 0, 2))

    def _L0_ffn_ref(x, router_w, router_bias, wg, wu, wd, swg, swu, swd):
        import jax, jax.numpy as jnp
        import numpy as np
        B, T, D = (2, 128, 256)
        E, F, K = (64, 64, 4)
        S, HS = (2, 64 * 4)
        b, t, d = x.shape
        flat = x.reshape(b * t, d)
        n = flat.shape[0]
        logits = flat @ router_w
        scores = jax.nn.softmax(logits, axis=-1)
        _, topk_idx = jax.lax.top_k(logits + router_bias, K)
        topk_scores = jnp.take_along_axis(scores, topk_idx, axis=-1)
        topk_scores = topk_scores / topk_scores.sum(axis=-1, keepdims=True)
        comb = jnp.zeros((n, E), dtype=flat.dtype).at[jnp.arange(n)[:, None], topk_idx].set(topk_scores)
        g = jax.nn.silu(jnp.einsum('nd,edf->nef', flat, wg))
        u = jnp.einsum('nd,edf->nef', flat, wu)
        routed = jnp.einsum('ne,nef,efd->nd', comb, g * u, wd)
        sg = jax.nn.silu(jnp.einsum('nd,sdh->nsh', flat, swg))
        su = jnp.einsum('nd,sdh->nsh', flat, swu)
        shared = jnp.einsum('nsh,shd->nd', sg * su, swd)
        return (routed + shared).reshape(b, t, d)
    x = L0_attn_a_x
    x = x + _L0_attn_a_ref(_layernorm(x, axis=-1), L0_attn_a_w_qkv, L0_attn_a_w_out, L0_attn_a_q_gain)
    x = x + _L0_ffn_ref(_layernorm(x, axis=-1), L0_ffn_router_w, L0_ffn_router_bias, L0_ffn_wg, L0_ffn_wu, L0_ffn_wd, L0_ffn_swg, L0_ffn_swu, L0_ffn_swd)
    x = x + _L0_attn_b_ref(_layernorm(x, axis=-1), L0_attn_b_key, L0_attn_b_value, L0_attn_b_Wqkv, L0_attn_b_Wproj, L0_attn_b_bproj)
    x = x + _L0_ffn_ref(_layernorm(x, axis=-1), L0_ffn_router_w, L0_ffn_router_bias, L0_ffn_wg, L0_ffn_wu, L0_ffn_wd, L0_ffn_swg, L0_ffn_swu, L0_ffn_swd)
    return x

_drawn_inputs = setup_inputs


def setup_inputs(seed=0):
    import zlib

    import numpy as np

    out = dict(_drawn_inputs(seed))
    spreads = {'L0_attn_a_q_gain': (12.0, 0.2),
     'L0_attn_b_bproj': (0.0, 0.1),
     'L0_ffn_router_bias': (0.0, 0.8)}
    factors = {'L0_ffn_router_w': 8.0, 'L0_ffn_wg': 7.804, 'L0_ffn_wu': 7.742, 'L0_ffn_wd': 7.718}
    for name, (base, spread) in spreads.items():
        noise = np.random.default_rng([zlib.crc32(name.encode()), seed]).standard_normal(out[name].shape)
        drawn = base * np.exp(spread * noise) if base else spread * noise
        out[name] = jnp.asarray(drawn.astype(out[name].dtype))
    for name, factor in factors.items():
        out[name] = (out[name] * factor).astype(out[name].dtype)
    return out
```

```python
from contextlib import ExitStack

import numpy as np
import concourse.bass as bass
from concourse import mybir

F32 = mybir.dt.float32
BF16 = mybir.dt.bfloat16
I32 = mybir.dt.int32
U32 = mybir.dt.uint32
ALU = mybir.AluOpType
ACT = mybir.ActivationFunctionType
AX = mybir.AxisListType

P = 128
B, S, D = 8, 256, 256
NT = B * S // P
TB = S // P
KC = D // P
H, HD = 16, 16
VW = 32
E, FF, K = 64, 64, 4
SH = 512
SC = SH // P
TERMS = [(0, 0), (0, 1), (1, 0), (1, 1), (0, 2), (2, 0)]
KR = len(TERMS) * HD
NTILE = B * S * K // P + E
SLOTS = NTILE * P
EPS_LN, EPS_UNIT = 1e-5, 1e-6
GRING, ERING, YRING = 8, 8, 4


class Signal:

    def __init__(self, sem, per_run):
        self.sem, self.per_run = sem, per_run

    def __call__(self, run, count):
        value = count + run * self.per_run
        return self.sem, (max(value, 0) if isinstance(value, int) else value)


def pipeline(eng, items, depth, unroll, step):
    first = 8 if depth > 1 else depth + 1
    loops = (items - first) // unroll
    flags = lambda s: [0 <= s - d < items for d in range(depth + 1)]
    for s in range(first):
        step(s, s % unroll, flags(s))
    with eng.Fori(0, loops) as i:
        for j in range(unroll):
            step(i * unroll + (first + j), (first + j) % unroll, [True] * (depth + 1))
    for s in range(first + loops * unroll, items + depth):
        step(s, s % unroll, flags(s))


def build(nc, t):
    with ExitStack() as ctx:
        def sb(name, shape, dt=F32):
            return ctx.enter_context(nc.sbuf_tensor(name, shape, dt))

        def signal(name, per_run=0):
            return Signal(ctx.enter_context(nc.semaphore(name)), per_run)

        X = sb("X", [P, NT, D])
        stats = sb("stats", [P, NT, 6])
        mv = sb("mv", [P, NT, 2])
        ve = sb("ve", [P, NT])
        rstd = sb("rstd", [P, NT])
        mhalf = sb("mhalf", [P, NT])
        xn = sb("xn", [P, TB, D])
        xt = sb("xt", [P, KC, S])
        ident = sb("ident", [P, P])
        cb = sb("cb", [P, 2048 + 5 * P], BF16)
        esel = cb[:, 0:2048].rearrange("p (h k) -> p h k", h=H)
        identb, mask_s, mask_t, ltri, onesb = (cb[:, 2048 + i * P:2048 + (i + 1) * P] for i in range(5))
        rotm = sb("rotm", [P, P])
        blk = sb("blk", [P, P])
        cs = sb("cs", [P, 2, S])
        gain = sb("gain", [P, KC])
        wqk = [sb(f"wqk{r}", [P, KC, 2 * D]) for r in range(2)]
        wv = [sb(f"wv{r}", [P, KC, D]) for r in range(2)]
        wo = [sb(f"wo{r}", [P, KC, D]) for r in range(2)]
        bproj = sb("bproj", [P, D])
        rw = sb("rw", [P, KC, E])
        rb = sb("rb", [P, E])
        iot = sb("iot", [P, E])
        jcol = sb("jcol", [P, 1])
        swg = sb("swg", [P, KC, SH])
        swu = sb("swu", [P, KC, SH])
        swd = sb("swd", [P, SC, D])
        oh = sb("oh", [P, NT, K, E], BF16)
        rank = sb("rank", [P, NT, E])
        comb = sb("comb", [P, NT, K])
        slot = sb("slot", [P, NT, K], I32)
        te = sb("te", [1, P], I32)

        big = sb("big", [P, 2 * NT * D])
        v_all = big[:, 0:NT * D].rearrange("p (i h d) -> p i h d", i=NT, h=H)
        xn_all = big[:, 0:NT * D].rearrange("p (i d) -> p i d", i=NT)
        xnt_all = big[:, NT * D:].rearrange("p (c n) -> p c n", c=KC)
        y_all = big[:, NT * D:].rearrange("p (i d) -> p i d", i=NT)
        arena = sb("arena", [P, 12288])
        qs = [arena[:, 4096 * i:4096 * i + 2048].bitcast(BF16).rearrange("p (h n) -> p h n", h=H) for i in range(3)]
        ks = [arena[:, 4096 * i + 2048:4096 * i + 4096].bitcast(BF16).rearrange("p (h n) -> p h n", h=H) for i in range(3)]
        cload = arena[:, 0:2048 + 5 * P]
        wring = [arena[:, 384 * i:384 * i + 384] for i in range(ERING)]
        xring = [arena[:, 3072 + 256 * i:3328 + 256 * i] for i in range(ERING)]
        yring = [arena[:, 5120 + 256 * i:5376 + 256 * i] for i in range(YRING)]
        xdt = [arena[:, 6144 + 256 * i:6400 + 256 * i].rearrange("p (c n) -> p c n", c=KC) for i in range(2)]
        eth = [arena[:, 6656 + 64 * i:6720 + 64 * i] for i in range(2)]
        eg = [arena[:, 6784 + 64 * i:6848 + 64 * i] for i in range(2)]
        eh = [arena[:, 6912 + 128 * i:7040 + 128 * i] for i in range(2)]
        eht = [arena[:, 7168 + 128 * i:7296 + 128 * i] for i in range(2)]
        sth = arena[:, 7680:8704]
        sga = arena[:, 8704:9728]
        sg = [arena[:, 9728 + 1024 * i:10752 + 1024 * i].rearrange("p (c n) -> p c n", c=SC) for i in range(2)]
        gring = [arena[:, 7680 + 256 * i:7936 + 256 * i] for i in range(GRING)]
        tmp = sb("tmp", [P, 8192])
        qr = [tmp[:, 0:1024], tmp[:, 1024:2048]]
        sq = tmp[:, 2048:3072]
        nrm = tmp[:, 3072:4096]
        rinv = tmp[:, 4096:5120]
        qf = tmp[:, 5120:6144]
        res = tmp[:, 6144:7168]
        rt = tmp[:, 7168:7680]
        pt = sb("pt", [P, 3, 4 * S], BF16)
        prob = [tmp[:, 512 * i:512 * i + 512] for i in range(4)]
        vb = [tmp[:, 2048 + 1024 * i:3072 + 1024 * i].rearrange("p (t h w) -> p t h w", t=TB, h=H) for i in range(3)]
        ot = [tmp[:, 5120 + 256 * i:5376 + 256 * i] for i in range(2)]
        yrow = tmp[:, 5632:6144]
        yt = tmp[:, 6144:6656]
        ybuf = [arena[:, 512 * i:512 * i + 512] for i in range(2)]
        ytb = [arena[:, 1024 + 512 * i:1536 + 512 * i] for i in range(2)]
        mx = tmp[:, 6656:6688]
        rs = tmp[:, 6688:6696]
        rm = tmp[:, 6720:6976]
        nm = tmp[:, 7168:7296].bitcast(BF16)
        nm2 = tmp[:, 7296:7424].bitcast(BF16)
        lb = tmp[:, 0:128]
        nmx = tmp[:, 128:130]
        m8 = tmp[:, 144:160]
        i8 = tmp[:, 160:176].bitcast(U32)
        idxf = tmp[:, 176:184]
        gk = tmp[:, 184:192]
        gs = tmp[:, 192:194]
        gr = tmp[:, 194:196]
        ex = tmp[:, 256:384]
        prod = tmp[:, 512:1536]
        msk = tmp[:, 1536:1600].bitcast(BF16)
        cum = tmp[:, 1600:1632].bitcast(BF16)
        cnt_i = tmp[:, 1664:1728].bitcast(I32)
        ntf = tmp[:, 1728:1792]
        incl = tmp[:, 1792:1856]
        base = tmp[:, 1856:1920]
        one64 = tmp[:, 1920:1984]
        cmp = tmp[:, 1984:2048]
        tef = tmp[:, 2048:2049]
        slotf = tmp[:, 2052:2068]
        slotmap = tmp[:, 4096:5120]
        zero = sb("zero", [P, D])

        ps = [ctx.enter_context(nc.psum_tensor(f"ps{i}", [P, 512], F32)) for i in range(8)]

        consts_in, x_in = signal("consts_in"), signal("x_in")
        cast_done, setup_done = signal("cast_done"), signal("setup_done")
        phase_end = signal("phase_end")
        stat_done = signal("stat_done")
        ve_ready, rstd_ready = signal("ve_ready", 2), signal("rstd_ready", 2)
        xn_ready, xT_done, xt_ready = signal("xn_ready", 16), signal("xT_done", 8), signal("xt_ready", 8)
        qk_done, qk_raw = signal("qk_done", 16), signal("qk_raw", 16)
        v_done, v_out = signal("v_done", 8), signal("v_out", 8)
        sq_ready, ss_done, nrm_ready = signal("sq_ready"), signal("ss_done"), signal("nrm_ready")
        rinv_ready, qn_ready, rot_done = signal("rinv_ready"), signal("qn_ready"), signal("rot_done")
        rope_ready, qf_ready = signal("rope_ready"), signal("qf_ready")
        p1_ready, res_ready, p2_ready, p3_ready = (signal(n, 8) for n in ("p1_ready", "res_ready", "p2_ready", "p3_ready"))
        parts_stored = signal("parts_stored", 128)
        stack_in = [signal(f"stack_in{i}", 16 * len(TERMS) * 2 * (3 if i < 2 else 2)) for i in range(3)]
        vb_ready, vpad = signal("vb_ready", 8), signal("vpad", 1)
        s1_done, mx_ready, mT_done = signal("s1_done", 128), signal("mx_ready", 128), signal("mT_done", 8)
        nm1_ready, rm_ready, nm2_ready, nm_ready = (signal(n, 8) for n in ("nm1_ready", "rm_ready", "nm2_ready", "nm_ready"))
        s2_done, exp_ready, pv_done = signal("s2_done", 128), signal("exp_ready", 128), signal("pv_done", 128)
        ot_ready, oT_done, rs_ready, y_ready = (signal(n, 32) for n in ("ot_ready", "oT_done", "rs_ready", "y_ready"))
        yT_done, yt_ready, op_done, x_added = (signal(n) for n in ("yT_done", "yt_ready", "op_done", "x_added"))
        rn_ready, rT_done, rt_ready, rcopy_done = signal("rn_ready", 16), signal("rT_done", 8), signal("rt_ready", 8), signal("rcopy_done", 16)
        lg_done, nmx_ready, ex_ready = signal("lg_done", 8), signal("nmx_ready", 8), signal("ex_ready", 8)
        topk = signal("topk")
        msk_ready, rank_done, rank_out = signal("msk_ready", 8), signal("rank_done", 8), signal("rank_out", 8)
        cum_ready, cnt_done = signal("cum_ready", 8), signal("cnt_done", 1)
        slot_ready, tef_ready, teT_done, te_ready = signal("slot_ready", 4), signal("tef_ready", 1), signal("teT_done", 1), signal("te_ready", 1)
        zeroed, scattered = signal("zeroed"), signal("scattered", 16 * NT * K)
        gu_done, sth_ready, sga_ready, sg_ready = signal("gu_done", 16), signal("sth_ready", 16), signal("sga_ready", 16), signal("sg_ready", 16)
        sd_done, sx_added = signal("sd_done", 8), signal("sx_added", 8)
        w_in = [signal(f"w_in{i}", 16 * NTILE // ERING) for i in range(ERING)]
        xd_in = [signal(f"xd_in{i}", 16 * NTILE // ERING) for i in range(ERING)]
        y_out = [signal(f"y_out{i}", 16 * NTILE // YRING) for i in range(YRING)]
        eT_done, ext_ready, egu_done, eth_ready = (signal(n, NTILE) for n in ("eT_done", "ext_ready", "egu_done", "eth_ready"))
        eg_ready, eh_ready, hT_done, eht_ready = (signal(n, NTILE) for n in ("eg_ready", "eh_ready", "hT_done", "eht_ready"))
        ed_done, ya_ready, yv_ready = (signal(n, NTILE) for n in ("ed_done", "ya_ready", "yv_ready"))
        g_in = [signal(f"g_in{i}", 16 * NT * K // GRING) for i in range(GRING)]
        g_used = signal("g_used", NT * K)
        tile_final, stored = signal("tile_final", NT), signal("stored")

        CONSTS = [(cload, "cload"), (ident[:, :], "ident"), (rotm[:, :], "rotm"), (blk[:, :], "blk"),
                  (cs[:, :, :], "cs"), (gain[:, :], "gain"), (bproj[:, :], "bproj"), (rw[:, :, :], "rw"),
                  (rb[:, :], "rb"), (iot[:, :], "iot"), (jcol[:, :], "jcol"), (swg[:, :, :], "swg"),
                  (swu[:, :, :], "swu"), (swd[:, :, :], "swd")]
        for r in range(2):
            CONSTS += [(wqk[r][:, :, :], f"wqk{r}"), (wv[r][:, :, :], f"wv{r}"), (wo[r][:, :, :], f"wo{r}")]
        x_tiles = t["x"].rearrange("b (t p) d -> p (b t) d", p=P)
        out_tiles = t["out"].rearrange("b (t p) d -> p (b t) d", p=P)
        parts = t["parts"]
        xd, yd = t["xd"], t["yd"]

        epsu = sb("epsu", [P, 1])[:, :]
        nm_zero, bias_added, stat_a = signal("nm_zero"), signal("bias_added"), signal("stat_a", 2 * B)
        yb_ready, yT1_done, yt1_ready, op1_done, x1_added = (signal(n) for n in ("yb_ready", "yT1_done", "yt1_ready", "op1_done", "x1_added"))
        stat_b, settled = signal("stat_b"), signal("settled")
        cum0, cum_half, disp = signal("cum0"), signal("cum_half", 8), signal("disp")
        disp_base = [0]

        block = ctx.enter_context(nc.Block())

        barriers = {}

        def barrier(e, name):
            barriers[name] = barriers.get(name, 0) + 1
            e.drain().then_inc(phase_end.sem, 1)
            e.wait_ge(phase_end.sem, 3 * barriers[name])

        def stored_count(j, i):
            return 16 * max(j // YRING, 0) if isinstance(j, int) else (j - i) * (16 // YRING)

        def causal(r):
            return r == 0

        @block.sync
        def _(sp):
            sp.dma_start(X[:, :, :], x_tiles).then_inc(x_in.sem, 16)
            for dst, name in CONSTS:
                sp.dma_start(dst, t[name]).then_inc(consts_in.sem, 16)
            sp.wait_ge(setup_done.sem, 1)
            zsrc = zero[:, :].rearrange("p (a d) -> p a d", a=1).broadcast_to([P, NTILE, D])
            sp.dma_start(xd.rearrange("(p a) d -> p a d", a=NTILE), zsrc).then_inc(zeroed.sem, 16)

            for r in range(2):
                with sp.Fori(0, B) as b:
                    sp.wait_ge(*p3_ready(r, b + 1))
                    sp.dma_start(parts[bass.ds(b, 1)].rearrange("a s (c p) n -> p (a s) c n", p=P),
                                 pt[:, :, :].rearrange("p s (c n) -> p s c n", c=4)).then_inc(parts_stored.sem, 16)

                def load_stack(b, i):
                    for side, dst in ((0, qs[i]), (1, ks[i])):
                        for n, term in enumerate(TERMS):
                            src = parts[bass.ds(b, 1), term[side], side * D:(side + 1) * D, :].rearrange(
                                "a (h d) n -> d (a h) n", d=HD)
                            sp.dma_start(dst[HD * n:HD * n + HD, :, :], src).then_inc(stack_in[i].sem, 16)

                sp.wait_ge(*parts_stored(r, 16 * B))
                load_stack(0, 0)
                load_stack(1, 1)
                with sp.Fori(0, 2) as it:
                    for j in range(3):
                        b = it * 3 + (2 + j)
                        sp.wait_ge(*s2_done(r, (b - 2) * H + 1))
                        load_stack(b, (2 + j) % 3)

                def load_weights(j, i):
                    ev = sp.value_load(te[0:1, bass.ds(j, 1)], min_val=0, max_val=E - 1)
                    sp.dma_start(wring[i], t["we"][bass.ds(ev, 1)].rearrange("a p n -> p (a n)")).then_inc(w_in[i].sem, 16)

                def load_rows(j, i):
                    sp.dma_start(xring[i], xd[bass.ds(j * P, P), :]).then_inc(xd_in[i].sem, 16)
                sp.wait_ge(*te_ready(r, 1))
                for j in range(ERING):
                    load_weights(j, j)
                sp.wait_ge(*scattered(r, 16 * NT * K))
                sp.wait_ge(zeroed.sem, 16)
                for j in range(ERING):
                    load_rows(j, j)
                with sp.Fori(0, NTILE // ERING - 1) as it:
                    for i in range(ERING):
                        j = it * ERING + (ERING + i)
                        sp.wait_ge(*eT_done(r, j - (ERING - 1)))
                        load_rows(j, i)
                        sp.wait_ge(*ed_done(r, j - (ERING - 1)))
                        load_weights(j, i)
            for i in range(0, NT, TB):
                sp.wait_ge(tile_final.sem, NT + i + TB)
                sp.dma_start(out_tiles[:, i:i + TB, :], X[:, i:i + TB, :]).then_inc(stored.sem, 16)
            sp.wait_ge(stored.sem, 16 * NT // TB)

        @block.gpsimd
        def _(pool):
            pool.memset(mhalf[:, :], -0.5).then_inc(vpad.sem, 1)
            pool.wait_ge(vpad.sem, 1)

            def rsqrt_variance(run, n):
                pool.wait_ge(*ve_ready(run, n))
                pool.tensor_tensor(rstd[:, :], ve[:, :], mhalf[:, :], ALU.pow).then_inc(rstd_ready.sem, 1)

            for r in range(2):
                rsqrt_variance(r, 1)
                pool.wait_ge(*v_out(r, 8))
                pool.wait_ge(*parts_stored(r, 128))
                for i in range(3):
                    pool.memset(vb[i][:, :, :, HD:HD + 1], 1.0)
                    pool.memset(vb[i][:, :, :, HD + 1:VW], 0.0).then_inc(vpad.sem, 1)
                pool.wait_ge(vpad.sem, 1 + 3 * (r + 1))

                def copy_v(b, i):
                    pool.tensor_copy(vb[i][:, :, :, 0:HD], v_all[:, bass.ds(b * TB, TB), :, :]).then_inc(vb_ready.sem, 1)

                copy_v(0, 0)
                copy_v(1, 1)
                with pool.Fori(0, 2) as it:
                    for j in range(3):
                        b = it * 3 + (2 + j)
                        pool.wait_ge(*pv_done(r, (b - 2) * H + 1))
                        copy_v(b, (2 + j) % 3)

                if r == 1:
                    pool.wait_ge(*y_ready(r, 32))
                    for b in range(2):
                        pool.tensor_copy(ybuf[b].rearrange("p (t d) -> p t d", t=TB), y_all[:, b * TB:b * TB + TB, :]).then_inc(yb_ready.sem, 1)
                    with pool.Fori(0, (B - 2) // 2) as it:
                        for j in range(2):
                            b = it * 2 + (2 + j)
                            pool.wait_ge(yT1_done.sem, b - 1)
                            pool.tensor_copy(ybuf[j].rearrange("p (t d) -> p t d", t=TB), y_all[:, bass.ds(b * TB, TB), :]).then_inc(yb_ready.sem, 1)
                rsqrt_variance(r, 2)
                with pool.Fori(0, B) as b:
                    pool.wait_ge(*rn_ready(r, 2 * b + 2))
                    pool.tensor_copy(xn_all[:, bass.ds(b * TB, TB), :], xn[:, :, :]).then_inc(rcopy_done.sem, 1)
                    pool.wait_ge(*rt_ready(r, b + 1))
                    pool.tensor_copy(xnt_all[:, :, bass.ds(b * S, S)], xt[:, :, :]).then_inc(rcopy_done.sem, 1)

                pool.wait_ge(zeroed.sem, 16)
                pool.wait_ge(*rcopy_done(r, 2 * B))
                for i in range(NT):
                    if i % 4 == 0:
                        pool.wait_ge(*slot_ready(r, i // 4 + 1))
                    for k in range(K):
                        pool.indirect_dma_start(xd[:, :], bass.IndirectOffsetOnAxis(ap=slot[:, i, k:k + 1], axis=0),
                                                xn_all[:, i, :], None).then_inc(scattered.sem, 16)

                def store_tile(j, i):
                    pool.wait_ge(*ya_ready(r, j + 1))
                    pool.wait_ge(*yv_ready(r, j + 1))
                    pool.dma_start(yd[bass.ds(j * P, P), :], yring[i]).then_inc(y_out[i].sem, 16)
                with pool.Fori(0, NTILE // YRING) as it:
                    for i in range(YRING):
                        store_tile(it * YRING + i, i)

                for i in range(YRING):
                    pool.wait_ge(*y_out[i](r, 16 * NTILE // YRING))
                for i in range(NT):
                    for k in range(K):
                        n = i * K + k
                        if n >= GRING:
                            pool.wait_ge(*g_used(r, n - GRING + 1))
                        pool.indirect_dma_start(gring[n % GRING], None, yd[:, :],
                                                bass.IndirectOffsetOnAxis(ap=slot[:, i, k:k + 1], axis=0)).then_inc(g_in[n % GRING].sem, 16)

        @block.tensor
        def _(pe):
            pe.wait_ge(consts_in.sem, 16 * len(CONSTS))
            pe.wait_ge(cast_done.sem, 1)

            for r in range(2):
                barrier(pe, "pe")

                def project_step(s, i, has):
                    if has[0]:
                        pe.wait_ge(*xn_ready(r, s * 2 + 2))
                        pe.wait_ge(*xt_ready(r, s))
                        for tt in range(TB):
                            for c in range(KC):
                                mm = pe.transpose(ps[0][:, c * S + tt * P:c * S + tt * P + P],
                                                  xn[:, tt, c * P:(c + 1) * P], ident[:, :])
                        mm.then_inc(xT_done.sem, 1)
                        pe.wait_ge(*xt_ready(r, s + 1))
                        for side in range(2):
                            pe.wait_ge(*qk_raw(r, s * 2))
                            for j in range(2):
                                col = side * D + j * P
                                for c in range(KC):
                                    mm = pe.matmul(ps[1 + side][:, j * S:(j + 1) * S], wqk[r][:, c, col:col + P],
                                                   xt[:, c, :], start=(c == 0), stop=(c == KC - 1))
                            mm.then_inc(qk_done.sem, 1)
                        pe.wait_ge(*v_out(r, s))
                        for tt in range(TB):
                            for c in range(KC):
                                mm = pe.matmul(ps[3][:, tt * D:(tt + 1) * D], xt[:, c, tt * P:(tt + 1) * P],
                                               wv[r][:, c, :], start=(c == 0), stop=(c == KC - 1))
                        mm.then_inc(v_done.sem, 1)
                    if has[1] and r == 0:
                        pe.wait_ge(sq_ready.sem, s)
                        for side in range(2):
                            pe.wait_ge(nrm_ready.sem, (s - 1) * 2)
                            pe.matmul(ps[4 + side][:, :], blk[:, :], sq[:, side * 512:(side + 1) * 512],
                                      start=True, stop=True).then_inc(ss_done.sem, 1)
                        pe.wait_ge(qn_ready.sem, s * 3)
                        pe.wait_ge(rope_ready.sem, (s - 1) * 2)
                        for side in range(2):
                            mm = pe.matmul(ps[6][:, side * S:(side + 1) * S], rotm[:, :],
                                           qf[:, side * 512:side * 512 + S], start=True, stop=True)
                        mm.then_inc(rot_done.sem, 1)
                pipeline(pe, B, 1, 2, project_step)
                barrier(pe, "pe")

                def scores(s, i, h):
                    if h == 0:
                        n = 16 * len(TERMS) * 2
                        b3 = s // 3 if isinstance(s, int) else None
                        pe.wait_ge(*stack_in[i](r, n * (b3 + 1) if b3 is not None else stack_count(s, i, n)))
                    pe.wait_ge(*mx_ready(r, s * H + max(h - 1, 0)))
                    if h == 1:
                        pe.wait_ge(*nm_ready(r, s))
                    bank = ps[h % 2]
                    for tt in range(TB):
                        keys = (tt + 1) * P if causal(r) else S
                        pe_last = pe.matmul(bank[:, tt * S:tt * S + keys], qs[i][0:KR, h, tt * P:(tt + 1) * P],
                                            ks[i][0:KR, h, 0:keys], start=True, stop=not causal(r))
                        if causal(r):
                            pe_last = pe.matmul(bank[:, tt * S + tt * P:tt * S + (tt + 1) * P], identb, mask_s,
                                                start=False, stop=True)
                    pe_last.then_inc(s1_done.sem, 1)

                def stack_count(s, i, n):
                    return (s - i + 3) * (n // 3)

                def probs(s, i, h):
                    b = s - 1
                    if h == 0:
                        pe.wait_ge(*nm_ready(r, s))
                    pe.wait_ge(*exp_ready(r, b * H + max(h - 1, 0)))
                    bank = ps[2 + h % 2]
                    for kb in range(TB):
                        q0 = kb * P if causal(r) else 0
                        out = bank[:, kb * S:kb * S + S - q0]
                        pe.matmul(out, ks[i][0:KR, h, kb * P:(kb + 1) * P], qs[i][0:KR, h, q0:S],
                                  start=True, stop=False)
                        mm = pe.matmul(out, esel[0:96, h, :], nm[0:96, q0:S], start=False, stop=not causal(r))
                        if causal(r):
                            mm = pe.matmul(bank[:, kb * S:kb * S + P], identb, mask_t, start=False, stop=True)
                    mm.then_inc(s2_done.sem, 1)

                def weigh(s, i, h):
                    b, g, j = s - 1, h // 4, h % 4
                    if h == 0:
                        pe.wait_ge(*vb_ready(r, s))
                    pe.wait_ge(*exp_ready(r, b * H + h + 1))
                    if j == 0:
                        pe.wait_ge(*ot_ready(r, b * 4 + max(g - 1, 0)))
                    bank = ps[4 + g % 2]
                    for kb in range(TB):
                        q0 = kb * P if causal(r) else 0
                        mm = pe.matmul(bank[32 * j:32 * j + VW, q0:S], vb[i][:, kb, h, :],
                                       prob[h % 4][:, kb * S:kb * S + S - q0], start=(kb == 0), stop=(kb == TB - 1))
                    mm.then_inc(pv_done.sem, 1)

                def turn_group(s, g):
                    b = s - 1
                    pe.wait_ge(*ot_ready(r, b * 4 + g + 1))
                    pe.wait_ge(*y_ready(r, b * 4 + g))
                    for tt in range(TB):
                        mm = pe.transpose(ps[6][:, tt * P:(tt + 1) * P], ot[g % 2][:, tt * P:(tt + 1) * P], ident[:, :])
                    mm.then_inc(oT_done.sem, 1)

                def attend_step(s, i, has):
                    iprev = (i - 1) % 3
                    for h in range(H + 2):
                        if h < H and has[0]:
                            scores(s, i, h)
                        if has[1]:
                            if h < H:
                                probs(s, iprev, h)
                            if h >= 2:
                                weigh(s, iprev, h - 2)
                            if h >= 8 and h % 4 == 0:
                                turn_group(s, h // 4 - 2)
                    if has[0]:
                        pe.wait_ge(*mx_ready(r, s * H + H))
                        for tt in range(TB):
                            mm = pe.transpose(ps[1][0:H, tt * P:(tt + 1) * P], mx[:, tt * H:(tt + 1) * H], ident[:, :])
                        mm.then_inc(mT_done.sem, 1)
                    if has[1]:
                        turn_group(s, 3)
                    if has[1] and r == 0:
                        pe.wait_ge(*y_ready(r, s * 4))
                        for tt in range(TB):
                            for c in range(KC):
                                mm = pe.transpose(ps[6][:, c * S + tt * P:c * S + tt * P + P],
                                                  yrow[:, tt * D + c * P:tt * D + (c + 1) * P], ident[:, :])
                        mm.then_inc(yT_done.sem, 1)
                        pe.wait_ge(*yt_ready(r, s))
                        pe.wait_ge(*x_added(r, s - 1))
                        for tt in range(TB):
                            for c in range(KC):
                                mm = pe.matmul(ps[7][:, tt * D:(tt + 1) * D], yt[:, c * S + tt * P:c * S + tt * P + P],
                                               wo[r][:, c, :], start=(c == 0), stop=(c == KC - 1))
                        mm.then_inc(op_done.sem, 1)
                pipeline(pe, B, 1, 3, attend_step)
                if r == 1:
                    def output_step(s, i, has):
                        if has[0]:
                            pe.wait_ge(yb_ready.sem, s + 1)
                            pe.wait_ge(yt1_ready.sem, s)
                            for tt in range(TB):
                                for c in range(KC):
                                    mm = pe.transpose(ps[0][:, c * S + tt * P:c * S + tt * P + P],
                                                      ybuf[i][:, tt * D + c * P:tt * D + (c + 1) * P], ident[:, :])
                            mm.then_inc(yT1_done.sem, 1)
                        if has[1]:
                            pe.wait_ge(yt1_ready.sem, s)
                            pe.wait_ge(x1_added.sem, s - 1)
                            for tt in range(TB):
                                for c in range(KC):
                                    mm = pe.matmul(ps[7][:, tt * D:(tt + 1) * D], ytb[1 - i][:, c * S + tt * P:c * S + tt * P + P],
                                                   wo[r][:, c, :], start=(c == 0), stop=(c == KC - 1))
                            mm.then_inc(op1_done.sem, 1)
                    barrier(pe, "pe")
                    pipeline(pe, B, 1, 2, output_step)
                barrier(pe, "pe")

                def route_step(s, i, has):
                    if has[0]:
                        pe.wait_ge(*rn_ready(r, s * 2 + 2))
                        pe.wait_ge(*rt_ready(r, s))
                        for tt in range(TB):
                            for c in range(KC):
                                mm = pe.transpose(ps[0][:, c * S + tt * P:c * S + tt * P + P],
                                                  xn[:, tt, c * P:(c + 1) * P], ident[:, :])
                        mm.then_inc(rT_done.sem, 1)
                        pe.wait_ge(*rt_ready(r, s + 1))
                        pe.wait_ge(*nmx_ready(r, s - 1 if not isinstance(s, int) or s else 0))
                        pe.wait_ge(*ex_ready(r, s - 1 if not isinstance(s, int) or s else 0))
                        for tt in range(TB):
                            for c in range(KC):
                                mm = pe.matmul(ps[1 + i][:, tt * E:(tt + 1) * E], xt[:, c, tt * P:(tt + 1) * P],
                                               rw[:, c, :], start=(c == 0), stop=(c == KC - 1))
                        mm.then_inc(lg_done.sem, 1)
                    if has[1]:
                        pe.wait_ge(*msk_ready(r, s))
                        pe.wait_ge(*cum_ready(r, s - 1))
                        pe.wait_ge(*rank_out(r, s - 1))
                        pe.matmul(ps[3][:, 0:E], ltri, msk[:, 0:E], start=True, stop=False)
                        pe.matmul(ps[3][:, 0:E], onesb, cum, start=False, stop=True)
                        pe.matmul(ps[3][:, E:2 * E], ltri, msk[:, E:2 * E], start=True, stop=False)
                        pe.matmul(ps[3][:, E:2 * E], onesb, msk[:, 0:E], start=False, stop=False)
                        pe.matmul(ps[3][:, E:2 * E], onesb, cum, start=False, stop=True).then_inc(rank_done.sem, 1)
                pipeline(pe, B, 1, 2, route_step)
                pe.wait_ge(*cum_ready(r, B))
                pe.matmul(ps[4][:, 0:E], onesb, cum, start=True, stop=True).then_inc(cnt_done.sem, 1)
                pe.wait_ge(*tef_ready(r, 1))
                pe.transpose(ps[5][0:1, 0:P], tef, ident[:, :]).then_inc(teT_done.sem, 1)
                barrier(pe, "pe")

                pe.wait_ge(*rcopy_done(r, 2 * B))

                def shared_step(s, i, has):
                    for half in range(2):
                        if has[0]:
                            pe.wait_ge(*sg_ready(r, s * 2 + half if half == 0 else s * 2))
                            for w, bank in ((swg, ps[half]), (swu, ps[2 + half])):
                                for j in range(2):
                                    ch = half * 2 + j
                                    for c in range(KC):
                                        mm = pe.matmul(bank[:, j * S:(j + 1) * S], w[:, c, ch * P:(ch + 1) * P],
                                                       xnt_all[:, c, bass.ds(s * S, S)], start=(c == 0), stop=(c == KC - 1))
                            mm.then_inc(gu_done.sem, 1)
                    if has[1]:
                        pe.wait_ge(*sg_ready(r, s * 2))
                        pe.wait_ge(*sx_added(r, s - 1))
                        for tt in range(TB):
                            for ch in range(SC):
                                mm = pe.matmul(ps[4][:, tt * D:(tt + 1) * D], sg[1 - i][:, ch, tt * P:(tt + 1) * P],
                                               swd[:, ch, :], start=(ch == 0), stop=(ch == SC - 1))
                        mm.then_inc(sd_done.sem, 1)
                pipeline(pe, B, 1, 2, shared_step)
                barrier(pe, "pe")

                def expert_step(s, i, has):
                    if has[0]:
                        j = s
                        pe.wait_ge(*xd_in[i](r, ring_count(j, i)))
                        pe.wait_ge(*ext_ready(r, j - 1 if not isinstance(j, int) or j else 0))
                        for c in range(KC):
                            mm = pe.transpose(ps[i % 2][:, c * P:(c + 1) * P], xring[i][:, c * P:(c + 1) * P], ident[:, :])
                        mm.then_inc(eT_done.sem, 1)
                    if has[1]:
                        j, i1 = s - 1, (i - 1) % ERING
                        pe.wait_ge(*w_in[i1](r, ring_count(j, i1)))
                        pe.wait_ge(*ext_ready(r, j + 1))
                        pe.wait_ge(*eh_ready(r, j - 1 if not isinstance(j, int) or j else 0))
                        for c in range(KC):
                            mm = pe.matmul(ps[2 + i1 % 2][:, 0:2 * FF], xdt[i1 % 2][:, c, :], wring[i1][:, c * 128:(c + 1) * 128],
                                           start=(c == 0), stop=(c == KC - 1))
                        mm.then_inc(egu_done.sem, 1)
                    if has[2]:
                        j, i2 = s - 2, (i - 2) % ERING
                        pe.wait_ge(*eh_ready(r, j + 1))
                        pe.wait_ge(*eht_ready(r, j))
                        pe.transpose(ps[4][:, 0:P], eh[i2 % 2], ident[:, :]).then_inc(hT_done.sem, 1)
                    if has[3]:
                        j, i3 = s - 3, (i - 3) % ERING
                        pe.wait_ge(*eht_ready(r, j + 1))
                        pe.wait_ge(*ya_ready(r, j))
                        pe.wait_ge(*yv_ready(r, j))
                        for half in range(2):
                            mm = pe.matmul(ps[5 + half][:, 0:P], eht[i3 % 2][64 * half:64 * half + 64, :],
                                           wring[i3][64 * half:64 * half + 64, 256:384], start=True, stop=True)
                        mm.then_inc(ed_done.sem, 1)

                def ring_count(j, i):
                    return 16 * (j // ERING + 1) if isinstance(j, int) else (j - i + ERING) * (16 // ERING)
                pipeline(pe, NTILE, 3, ERING, expert_step)

        @block.scalar
        def _(act):
            def copy(dst, src):
                return act.activation(dst, src, ACT.Copy)

            act.wait_ge(setup_done.sem, 2)
            for r in range(2):
                barrier(act, "act")

                def project_step(s, i, has):
                    if has[0]:
                        act.wait_ge(*xT_done(r, s + 1))
                        act.wait_ge(*v_done(r, s))
                        copy(xt[:, :, :].rearrange("p c n -> p (c n)"), ps[0][:, :]).then_inc(xt_ready.sem, 1)
                        if r == 0:
                            act.wait_ge(qn_ready.sem, max((s - 1) * 3, 0) if isinstance(s, int) else (s - 1) * 3)
                        else:
                            act.wait_ge(*res_ready(r, s - 1))
                        for side in range(2):
                            act.wait_ge(*qk_done(r, s * 2 + side + 1))
                            act.activation(qr[i][:, side * 512:(side + 1) * 512], ps[1 + side][:, :], ACT.Copy,
                                           scale=HD ** -0.5 if r == 1 and side == 0 else 1.0).then_inc(qk_raw.sem, 1)
                    if has[1]:
                        raw = qr[1 - i]
                        act.wait_ge(*qk_raw(r, s * 2))
                        if r == 0:
                            act.wait_ge(ss_done.sem, (s - 1) * 2)
                            act.activation(sq, raw, ACT.Square).then_inc(sq_ready.sem, 1)
                            act.wait_ge(rinv_ready.sem, s - 1)
                            for side in range(2):
                                act.wait_ge(ss_done.sem, s * 2 - 1 + side)
                                act.activation(nrm[:, side * 512:(side + 1) * 512], ps[4 + side][:, :], ACT.Sqrt,
                                               bias=epsu).then_inc(nrm_ready.sem, 1)
                            act.wait_ge(qf_ready.sem, s)
                        act.wait_ge(*parts_stored(r, (s - 1) * 16))
                        src = qf if r == 0 else raw
                        copy(pt[:, 0, :], src).then_inc(p1_ready.sem, 1)
                        act.wait_ge(*res_ready(r, s))
                        copy(pt[:, 1, :], res).then_inc(p2_ready.sem, 1)
                pipeline(act, B, 1, 2, project_step)
                barrier(act, "act")

                def attend_step(s, i, has):
                    if has[1]:
                        for h in range(H):
                            b = s - 1
                            act.wait_ge(*s2_done(r, b * H + h + 1))
                            act.wait_ge(*pv_done(r, b * H + max(h - 3, 0)))
                            n = S + P if causal(r) else 2 * S
                            act.activation(prob[h % 4][:, 0:n], ps[2 + h % 2][:, 0:n], ACT.Exp).then_inc(exp_ready.sem, 1)
                    if has[0]:
                        act.wait_ge(*mT_done(r, s + 1))
                        copy(nm[0:H, :], ps[1][0:H, 0:S]).then_inc(nm1_ready.sem, 1)
                        act.wait_ge(*rm_ready(r, s + 1))
                        copy(nm[32:32 + H, :], rm[0:H, :])
                        copy(nm2[0:H, :], rm[0:H, :]).then_inc(nm2_ready.sem, 1)
                    if has[1] and r == 0:
                        act.wait_ge(*yT_done(r, s))
                        copy(yt, ps[6][:, :]).then_inc(yt_ready.sem, 1)
                pipeline(act, B, 1, 3, attend_step)
                if r == 1:
                    def output_step(s, i, has):
                        if has[0]:
                            act.wait_ge(yT1_done.sem, s + 1)
                            act.wait_ge(op1_done.sem, s - 1 if not isinstance(s, int) or s else 0)
                            copy(ytb[i], ps[0][:, :]).then_inc(yt1_ready.sem, 1)
                    barrier(act, "act")
                    pipeline(act, B, 1, 2, output_step)
                barrier(act, "act")

                def route_step(s, i, has):
                    if has[0]:
                        act.wait_ge(*rT_done(r, s + 1))
                        act.wait_ge(*lg_done(r, s))
                        act.wait_ge(*rcopy_done(r, s * 2))
                        copy(xt[:, :, :].rearrange("p c n -> p (c n)"), ps[0][:, :]).then_inc(rt_ready.sem, 1)
                    if has[1]:
                        act.wait_ge(*nmx_ready(r, s))
                        for tt in range(TB):
                            ins = act.activation(ex[:, tt * E:(tt + 1) * E], ps[1 + (1 - i)][:, tt * E:(tt + 1) * E],
                                                 ACT.Exp, bias=nmx[:, tt:tt + 1])
                        ins.then_inc(ex_ready.sem, 1)
                        act.wait_ge(*rank_done(r, s))
                        copy(rank[:, bass.ds((s - 1) * TB, TB), :],
                             ps[3][:, 0:2 * E].rearrange("p (t e) -> p t e", t=TB)).then_inc(rank_out.sem, 1)
                pipeline(act, B, 1, 2, route_step)
                barrier(act, "act")

                def shared_step(s, i, has):
                    if has[0]:
                        for half in range(2):
                            act.wait_ge(*gu_done(r, s * 2 + half + 1))
                            act.wait_ge(*sga_ready(r, s * 2))
                            act.activation(sth[:, half * 512:(half + 1) * 512], ps[half][:, :], ACT.Tanh,
                                           scale=0.5).then_inc(sth_ready.sem, 1)
                pipeline(act, B, 1, 2, shared_step)
                barrier(act, "act")

                def expert_step(s, i, has):
                    if has[0]:
                        act.wait_ge(*eT_done(r, s + 1))
                        act.wait_ge(*egu_done(r, s - 1 if not isinstance(s, int) or s else 0))
                        copy(xdt[i % 2].rearrange("p c n -> p (c n)"), ps[i % 2][:, 0:D]).then_inc(ext_ready.sem, 1)
                    if has[1]:
                        j, i1 = s - 1, (i - 1) % ERING
                        act.wait_ge(*egu_done(r, j + 1))
                        act.wait_ge(*eg_ready(r, j - 1 if not isinstance(j, int) or j else 0))
                        act.activation(eth[i1 % 2], ps[2 + i1 % 2][:, 0:FF], ACT.Tanh, scale=0.5).then_inc(eth_ready.sem, 1)
                    if has[3]:
                        j, i3 = s - 3, (i - 3) % ERING
                        act.wait_ge(*ed_done(r, j + 1))
                        act.wait_ge(*y_out[i3 % YRING](r, stored_count(j, i3 % YRING)))
                        copy(yring[i3 % YRING][:, 0:P], ps[5][:, 0:P]).then_inc(ya_ready.sem, 1)
                pipeline(act, NTILE, 3, ERING, expert_step)

        @block.vector
        def _(dve):
            dve.memset(zero[:, :], 0.0).then_inc(setup_done.sem, 1)
            dve.memset(epsu, EPS_UNIT).then_inc(setup_done.sem, 1)
            dve.wait_ge(consts_in.sem, 16 * len(CONSTS))
            dve.tensor_copy(cb[:, :], cload).then_inc(cast_done.sem, 1)
            dve.wait_ge(x_in.sem, 16)
            for i in range(NT):
                dve.bn_stats(stats[:, i % 2, :], X[:, i, :]).then_inc(stat_done.sem, 1)
                dve.wait_ge(stat_done.sem, i + 1)
                dve.bn_aggr(mv[:, i, :], stats[:, i % 2, :]).then_inc(stat_b.sem, 1)
            dve.wait_ge(stat_b.sem, NT)
            stat_at = NT

            def settle():
                dve.sem_inc(settled.sem, 1)

            def make_rstd(r, n):
                dve.tensor_scalar(ve[:, :], mv[:, :, 1], EPS_LN, None, ALU.add).then_inc(ve_ready.sem, 1)
                dve.wait_ge(*rstd_ready(r, n))

            def normalise(b, done):
                for tt in range(TB):
                    at = bass.ds(b * TB + tt, 1)
                    dve.tensor_scalar(xn[:, tt, :], X[:, at, :].rearrange("p a d -> p (a d)"),
                                      mv[:, at, 0:1].rearrange("p a o -> p (a o)"), rstd[:, at],
                                      ALU.subtract, ALU.mult).then_inc(done.sem, 1)

            for r in range(2):
                barrier(dve, "dve")
                make_rstd(r, 1)
                if r == 0:
                    dve.wait_ge(consts_in.sem, 16 * len(CONSTS))

                def project_step(s, i, has):
                    if has[0]:
                        dve.wait_ge(*xT_done(r, s))
                        normalise(s, xn_ready)
                    if has[1]:
                        src = qf if r == 0 else qr[1 - i]
                        if r == 0:
                            raw = qr[1 - i]
                            dve.wait_ge(nrm_ready.sem, s * 2)
                            dve.reciprocal(rinv, nrm).then_inc(rinv_ready.sem, 1)
                            dve.wait_ge(rinv_ready.sem, s)
                            dve.wait_ge(*p1_ready(r, s - 1))
                            for c in range(KC):
                                dve.scalar_tensor_tensor(out=qf[:, c * S:(c + 1) * S], in0=raw[:, c * S:(c + 1) * S],
                                                         scalar=gain[:, c:c + 1], in1=rinv[:, c * S:(c + 1) * S],
                                                         op0=ALU.mult, op1=ALU.mult).then_inc(qn_ready.sem, 1)
                            dve.tensor_tensor(qf[:, 512:1024], raw[:, 512:1024], rinv[:, 512:1024], ALU.mult).then_inc(qn_ready.sem, 1)
                            roped = qf.rearrange("p (a n) -> p a n", a=2)[:, :, 0:S]
                            cos = cs[:, 0:1, :].broadcast_to([P, 2, S])
                            sin = cs[:, 1:2, :].broadcast_to([P, 2, S])
                            rt2 = rt.rearrange("p (a n) -> p a n", a=2)
                            dve.wait_ge(rot_done.sem, s)
                            dve.tensor_tensor(rt2, ps[6][:, :].rearrange("p (a n) -> p a n", a=2), sin, ALU.mult).then_inc(rope_ready.sem, 1)
                            dve.wait_ge(qn_ready.sem, s * 3)
                            dve.tensor_tensor(roped, roped, cos, ALU.mult).then_inc(rope_ready.sem, 1)
                            dve.wait_ge(rope_ready.sem, s * 2)
                            dve.tensor_tensor(roped, roped, rt2, ALU.add).then_inc(qf_ready.sem, 1)
                        dve.wait_ge(*p1_ready(r, s))
                        dve.wait_ge(*p2_ready(r, s - 1))
                        dve.tensor_tensor(res, src, pt[:, 0, :], ALU.subtract).then_inc(res_ready.sem, 1)
                        dve.wait_ge(*p2_ready(r, s))
                        dve.tensor_tensor(pt[:, 2, :], res, pt[:, 1, :], ALU.subtract).then_inc(p3_ready.sem, 1)
                    if has[0]:
                        dve.wait_ge(*v_done(r, s + 1))
                        dve.tensor_copy(v_all[:, bass.ds(s * TB, TB), :, :],
                                        ps[3][:, :].rearrange("p (t h d) -> p t h d", t=TB, h=H)).then_inc(v_out.sem, 1)
                pipeline(dve, B, 1, 2, project_step)
                barrier(dve, "dve")
                dve.memset(nm, 0.0).then_inc(nm_zero.sem, 1)
                dve.wait_ge(nm_zero.sem, r + 1)

                def group(s, g):
                    b = s - 1
                    if g == 0 and r == 0:
                        dve.wait_ge(yT_done.sem, s - 1)
                    dve.wait_ge(*oT_done(r, b * 4 + g + 1))
                    o4 = ps[6][:, 0:2 * P].rearrange("p (t j w) -> p t j w", t=TB, j=4)
                    rs3 = rs.rearrange("p (t j o) -> p t j o", t=TB, o=1)
                    dve.reciprocal(rs3, o4[:, :, :, HD:HD + 1]).then_inc(rs_ready.sem, 1)
                    dve.wait_ge(*rs_ready(r, b * 4 + g + 1))
                    if r == 0:
                        y4 = yrow.rearrange("p (t g j d) -> p t g j d", t=TB, g=4, j=4)[:, :, g, :, :]
                    else:
                        y4 = y_all.rearrange("p (b t) d -> p t b d", t=TB)[
                            :, :, (4 * g) % B:(4 * g) % B + 4, bass.ds(b * (2 * HD) + HD * (g // 2), HD)]
                    dve.tensor_tensor(y4, o4[:, :, :, 0:HD], rs3.broadcast_to([P, TB, 4, HD]), ALU.mult).then_inc(y_ready.sem, 1)

                def take_group(s, g):
                    b = s - 1
                    dve.wait_ge(*pv_done(r, b * H + 4 * g + 4))
                    dve.wait_ge(*oT_done(r, b * 4 + max(g - 1, 0)))
                    dve.tensor_copy(ot[g % 2], ps[4 + g % 2][:, 0:S]).then_inc(ot_ready.sem, 1)

                def attend_step(s, i, has):
                    if has[0]:
                        dve.wait_ge(*mT_done(r, s))
                    for h in range(H):
                        if has[0]:
                            dve.wait_ge(*s1_done(r, s * H + h + 1))
                            mx2 = mx.rearrange("p (t h) -> p t h", t=TB)[:, :, h]
                            if causal(r):
                                dve.tensor_reduce(mx[:, h:h + 1], ps[h % 2][:, 0:P], AX.X, ALU.max, negate=True)
                                ins = dve.tensor_reduce(mx[:, H + h:H + h + 1], ps[h % 2][:, S:2 * S], AX.X, ALU.max, negate=True)
                            else:
                                ins = dve.tensor_reduce(mx2, ps[h % 2][:, :].rearrange("p (t n) -> p t n", t=TB), AX.X, ALU.max, negate=True)
                            ins.then_inc(mx_ready.sem, 1)
                        if has[1]:
                            if h >= 6 and (h - 6) % 4 == 0:
                                take_group(s, (h - 6) // 4)
                            if h >= 9 and (h - 9) % 4 == 0:
                                group(s, (h - 9) // 4)
                    if has[1]:
                        take_group(s, 3)
                    if has[0]:
                        dve.wait_ge(*nm1_ready(r, s + 1))
                        dve.tensor_tensor(rm[0:H, :], ps[1][0:H, 0:S], nm[0:H, :], ALU.subtract).then_inc(rm_ready.sem, 1)
                        dve.wait_ge(*nm2_ready(r, s + 1))
                        dve.tensor_tensor(nm[64:64 + H, :], rm[0:H, :], nm2[0:H, :], ALU.subtract).then_inc(nm_ready.sem, 1)
                    if has[1]:
                        group(s, 2)
                        group(s, 3)
                        if r == 0:
                            dve.wait_ge(op_done.sem, s)
                            add_out(s, x_added)

                def add_out(s, added):
                    b = s - 1
                    xb = X[:, bass.ds(b * TB, TB), :]
                    dve.tensor_tensor(xb, xb, ps[7][:, :].rearrange("p (t d) -> p t d", t=TB), ALU.add).then_inc(added.sem, 1)
                    dve.wait_ge(added.sem, s)
                    if r == 1:
                        dve.tensor_tensor(xb, xb, bproj[:, :].rearrange("p (a d) -> p a d", a=1).broadcast_to([P, TB, D]),
                                          ALU.add).then_inc(bias_added.sem, 1)
                        dve.wait_ge(bias_added.sem, s)
                    settle()
                    for tt in range(TB):
                        dve.bn_stats(stats[:, bass.ds(b * TB + tt, 1), :].rearrange("p a o -> p (a o)"),
                                     X[:, bass.ds(b * TB + tt, 1), :].rearrange("p a d -> p (a d)")).then_inc(stat_a.sem, 1)
                pipeline(dve, B, 1, 3, attend_step)
                if r == 1:
                    def output_step(s, i, has):
                        if has[1]:
                            dve.wait_ge(op1_done.sem, s)
                            add_out(s, x1_added)
                    barrier(dve, "dve")
                    pipeline(dve, B, 1, 2, output_step)
                barrier(dve, "dve")
                dve.wait_ge(*stat_a(r, 2 * B))
                for i in range(NT):
                    dve.bn_aggr(mv[:, i, :], stats[:, i, :]).then_inc(stat_done.sem, 1)
                stat_at += NT
                dve.wait_ge(stat_done.sem, stat_at)
                make_rstd(r, 2)

                dve.memset(cum, 0.0).then_inc(cum0.sem, 1)
                dve.memset(one64, 1.0).then_inc(cum0.sem, 1)
                dve.wait_ge(cum0.sem, 2 * r + 2)
                CH = 11

                def route_step(s, i, has):
                    if has[0]:
                        dve.wait_ge(*rT_done(r, s))
                        dve.wait_ge(*rcopy_done(r, s * 2))
                        normalise(s, rn_ready)
                    if has[1]:
                        b, c0 = s - 1, (s - 1) * CH + r * (CH * B)
                        lg = ps[1 + (1 - i)][:, 0:2 * E].rearrange("p (t e) -> p t e", t=TB)
                        lb2 = lb.rearrange("p (t e) -> p t e", t=TB)
                        ohb = oh[:, bass.ds(b * TB, TB), :, :].rearrange("p t k e -> p (t k) e")
                        pr = prod[:, 0:TB * K * E]
                        dve.wait_ge(*lg_done(r, s))
                        dve.tensor_tensor(lb2, lg, rb[:, :].rearrange("p (a e) -> p a e", a=1).broadcast_to([P, TB, E]),
                                          ALU.add).then_inc(topk.sem, 1)
                        dve.tensor_reduce(nmx, lg, AX.X, ALU.max, negate=True).then_inc(nmx_ready.sem, 1)
                        dve.wait_ge(topk.sem, c0 + 1)
                        settle()
                        for tt in range(TB):
                            dve.max(m8[:, 8 * tt:8 * tt + 8], lb[:, tt * E:(tt + 1) * E]).then_inc(topk.sem, 1)
                        dve.wait_ge(topk.sem, c0 + 3)
                        settle()
                        for tt in range(TB):
                            dve.max_index(i8[:, 8 * tt:8 * tt + 8], m8[:, 8 * tt:8 * tt + 8], lb[:, tt * E:(tt + 1) * E]).then_inc(topk.sem, 1)
                        dve.wait_ge(topk.sem, c0 + 5)
                        dve.tensor_copy(idxf.rearrange("p (t k) -> p t k", t=TB),
                                        i8.rearrange("p (t k) -> p t k", t=TB)[:, :, 0:K]).then_inc(topk.sem, 1)
                        dve.wait_ge(topk.sem, c0 + 6)
                        dve.tensor_tensor(ohb, iot[:, :].rearrange("p (a e) -> p a e", a=1).broadcast_to([P, TB * K, E]),
                                          idxf.rearrange("p (a o) -> p a o", o=1).broadcast_to([P, TB * K, E]),
                                          ALU.is_equal).then_inc(topk.sem, 1)
                        dve.wait_ge(topk.sem, c0 + 7)
                        settle()
                        with nc.allow_low_precision("counts up to 4 are exact in bf16"):
                            dve.tensor_reduce(msk.rearrange("p (t e) -> p t e", t=TB),
                                              oh[:, bass.ds(b * TB, TB), :, :].rearrange("p t k e -> p t e k"),
                                              AX.X, ALU.add).then_inc(msk_ready.sem, 1)
                        dve.wait_ge(*ex_ready(r, s))
                        for tt in range(TB):
                            prt = pr[:, tt * K * E:(tt + 1) * K * E].rearrange("p (k e) -> p k e", k=K)
                            ins = dve.tensor_tensor(prt, ohb[:, tt * K:(tt + 1) * K, :],
                                                    ex[:, tt * E:(tt + 1) * E].rearrange("p (a e) -> p a e", a=1).broadcast_to([P, K, E]),
                                                    ALU.mult)
                        ins.then_inc(topk.sem, 1)
                        dve.wait_ge(topk.sem, c0 + 8)
                        dve.tensor_reduce(gk, pr.rearrange("p (a e) -> p a e", e=E), AX.X, ALU.add).then_inc(topk.sem, 1)
                        dve.wait_ge(topk.sem, c0 + 9)
                        dve.tensor_reduce(gs, gk.rearrange("p (t k) -> p t k", t=TB), AX.X, ALU.add).then_inc(topk.sem, 1)
                        dve.wait_ge(topk.sem, c0 + 10)
                        dve.reciprocal(gr, gs).then_inc(topk.sem, 1)
                        dve.wait_ge(topk.sem, c0 + 11)
                        dve.tensor_tensor(comb[:, bass.ds(b * TB, TB), :], gk.rearrange("p (t k) -> p t k", t=TB),
                                          gr.rearrange("p (t o) -> p t o", o=1).broadcast_to([P, TB, K]), ALU.mult)
                        dve.wait_ge(*rank_done(r, s))
                        dve.tensor_tensor(cum, cum, msk[:, 0:E], ALU.add).then_inc(cum_half.sem, 1)
                        dve.wait_ge(*cum_half(r, s))
                        dve.tensor_tensor(cum, cum, msk[:, E:2 * E], ALU.add).then_inc(cum_ready.sem, 1)
                pipeline(dve, B, 1, 2, route_step)

                d = [0]

                def link(ins):
                    d[0] += 1
                    ins.then_inc(disp.sem, 1)
                    dve.wait_ge(disp.sem, disp_base[0] + d[0])
                dve.wait_ge(*cnt_done(r, 1))
                link(dve.tensor_scalar(cnt_i, ps[4][:, 0:E], float(P - 1), None, ALU.add))
                link(dve.tensor_single_scalar(cnt_i, cnt_i, 7, ALU.arith_shift_right))
                link(dve.tensor_copy(ntf, cnt_i))
                link(dve.tensor_tensor_scan(incl, one64, ntf, 0.0, ALU.mult, ALU.add))
                link(dve.tensor_tensor(base, incl, ntf, ALU.subtract))
                link(dve.tensor_scalar(base, base, float(P), None, ALU.mult))
                dve.wait_ge(*rank_out(r, B))
                sm = slotmap.rearrange("p (i e) -> p i e", i=NT)
                link(dve.tensor_tensor(sm, rank[:, :, :], base.rearrange("p (a e) -> p a e", a=1).broadcast_to([P, NT, E]), ALU.add))
                for q in range(4):
                    for i in range(4):
                        ii = 4 * q + i
                        ins = dve.tensor_tensor(prod[:, i * 256:(i + 1) * 256].rearrange("p (k e) -> p k e", k=K), oh[:, ii, :, :],
                                                sm[:, ii:ii + 1, :].broadcast_to([P, K, E]), ALU.mult)
                    link(ins)
                    link(dve.tensor_reduce(slotf, prod.rearrange("p (a e) -> p a e", e=E), AX.X, ALU.add))
                    dve.tensor_copy(slot[:, 4 * q:4 * q + 4, :].rearrange("p i k -> p (i k)"), slotf).then_inc(slot_ready.sem, 1)
                    dve.wait_ge(*slot_ready(r, q + 1))
                link(dve.tensor_scalar(cmp, incl, jcol[:, 0:1], None, ALU.is_le))
                link(dve.tensor_reduce(tef, cmp, AX.X, ALU.add))
                dve.tensor_scalar(tef, tef, float(E - 1), None, ALU.min).then_inc(tef_ready.sem, 1)
                dve.wait_ge(*teT_done(r, 1))
                dve.tensor_copy(te[:, :], ps[5][0:1, 0:P]).then_inc(te_ready.sem, 1)
                disp_base[0] += d[0]
                barrier(dve, "dve")

                def shared_step(s, i, has):
                    if has[0]:
                        for half in range(2):
                            lo, hi = half * 512, (half + 1) * 512
                            dve.wait_ge(*sth_ready(r, s * 2 + half + 1))
                            dve.scalar_tensor_tensor(out=sga[:, lo:hi], in0=sth[:, lo:hi], scalar=1.0, in1=ps[half][:, :],
                                                     op0=ALU.add, op1=ALU.mult).then_inc(sga_ready.sem, 1)
                            dve.wait_ge(*sga_ready(r, s * 2 + half + 1))
                            if half == 0:
                                dve.wait_ge(*sd_done(r, s - 1 if not isinstance(s, int) or s else 0))
                            dve.scalar_tensor_tensor(out=sg[i][:, 2 * half:2 * half + 2, :].rearrange("p c n -> p (c n)"),
                                                     in0=sga[:, lo:hi], scalar=0.5, in1=ps[2 + half][:, :],
                                                     op0=ALU.mult, op1=ALU.mult).then_inc(sg_ready.sem, 1)
                    if has[1]:
                        dve.wait_ge(*sd_done(r, s))
                        xb = X[:, bass.ds((s - 1) * TB, TB), :]
                        dve.tensor_tensor(xb, xb, ps[4][:, :].rearrange("p (t d) -> p t d", t=TB), ALU.add).then_inc(sx_added.sem, 1)
                pipeline(dve, B, 1, 2, shared_step)
                barrier(dve, "dve")

                def expert_step(s, i, has):
                    if has[1]:
                        j, i1 = s - 1, (i - 1) % ERING
                        dve.wait_ge(*eth_ready(r, j + 1))
                        dve.scalar_tensor_tensor(out=eg[i1 % 2], in0=eth[i1 % 2], scalar=1.0, in1=ps[2 + i1 % 2][:, 0:FF],
                                                 op0=ALU.add, op1=ALU.mult).then_inc(eg_ready.sem, 1)
                        dve.wait_ge(*eg_ready(r, j + 1))
                        dve.wait_ge(*hT_done(r, j - 1 if not isinstance(j, int) or j else 0))
                        dve.scalar_tensor_tensor(out=eh[i1 % 2].rearrange("p (a f) -> p a f", a=2),
                                                 in0=eg[i1 % 2].rearrange("p (a f) -> p a f", a=1).broadcast_to([P, 2, FF]), scalar=0.5,
                                                 in1=ps[2 + i1 % 2][:, FF:2 * FF].rearrange("p (a f) -> p a f", a=1).broadcast_to([P, 2, FF]),
                                                 op0=ALU.mult, op1=ALU.mult).then_inc(eh_ready.sem, 1)
                    if has[2]:
                        j, i2 = s - 2, (i - 2) % ERING
                        dve.wait_ge(*hT_done(r, j + 1))
                        dve.wait_ge(*ed_done(r, j - 1 if not isinstance(j, int) or j else 0))
                        dve.tensor_copy(eht[i2 % 2], ps[4][:, 0:P]).then_inc(eht_ready.sem, 1)
                    if has[3]:
                        j, i3 = s - 3, (i - 3) % ERING
                        dve.wait_ge(*ed_done(r, j + 1))
                        dve.wait_ge(*y_out[i3 % YRING](r, stored_count(j, i3 % YRING)))
                        dve.tensor_copy(yring[i3 % YRING][:, P:D], ps[6][:, 0:P]).then_inc(yv_ready.sem, 1)
                pipeline(dve, NTILE, 3, ERING, expert_step)

                for i in range(NT):
                    for k in range(K):
                        n = i * K + k
                        dve.wait_ge(*g_in[n % GRING](r, 16 * (n // GRING + 1)))
                        if k:
                            dve.wait_ge(*g_used(r, n))
                        dve.scalar_tensor_tensor(out=X[:, i, :], in0=gring[n % GRING], scalar=comb[:, i, k:k + 1],
                                                 in1=X[:, i, :], op0=ALU.mult, op1=ALU.add).then_inc(g_used.sem, 1)
                    dve.wait_ge(*g_used(r, i * K + K))
                    dve.bn_stats(stats[:, i % 2, :], X[:, i, :]).then_inc(stat_done.sem, 1)
                    stat_at += 1
                    dve.wait_ge(stat_done.sem, stat_at)
                    dve.bn_aggr(mv[:, i, :], stats[:, i % 2, :]).then_inc(tile_final.sem, 1)
                dve.drain()


EVEN_FIRST = list(range(0, H, 2)) + list(range(1, H, 2))


def constants():
    eye = np.eye(P, dtype=np.float32)
    cload = np.zeros((P, 2048 + 5 * P), np.float32)
    sel = cload[:, 0:2048].reshape(P, H, P)
    for part in range(3):
        for h in range(H):
            sel[32 * part + h, h, :] = 1.0
    row, col = np.arange(P)[:, None], np.arange(P)[None, :]
    for i, m in enumerate((eye, np.where(col > row, -1e30, 0.0), np.where(row > col, -1e30, 0.0), row < col, np.ones((P, P)))):
        cload[:, 2048 + i * P:2048 + (i + 1) * P] = m
    half = HD // 2
    rotm = np.zeros((P, P), np.float32)
    for m in range(P):
        rotm[m + half if m % HD < half else m - half, m] = -1.0 if m % HD < half else 1.0
    inv = np.float32(10000.0) ** (-np.arange(half, dtype=np.float32) / np.float32(half))
    theta = (np.arange(S, dtype=np.float32)[:, None] * inv[None, :]).astype(np.float32)
    cs = np.stack([np.cos(theta), np.sin(theta)]).astype(np.float32)
    cs = np.ascontiguousarray(cs[:, :, np.arange(P) % half].transpose(2, 0, 1))
    return dict(cload=cload, ident=eye, rotm=rotm, cs=cs, blk=(row // HD == col // HD).astype(np.float32),
                iot=np.tile(np.arange(E, dtype=np.float32), (P, 1)), jcol=np.arange(P, dtype=np.float32)[:, None])


def chunked(w):
    return w.reshape(-1, P, w.shape[1]).transpose(1, 0, 2)


def layout(v):
    g = {k: np.asarray(a) for k, a in v.items()}
    a = dict(constants())
    a["x"] = g["L0_attn_a_x"]
    w = g["L0_attn_a_w_qkv"].reshape(D, 3, H, HD)[:, :, EVEN_FIRST, :].reshape(D, 3 * D)
    a["wqk0"], a["wv0"] = chunked(w[:, :2 * D]), chunked(w[:, 2 * D:])
    a["wo0"] = chunked(g["L0_attn_a_w_out"].reshape(H, HD, D)[EVEN_FIRST].reshape(D, D))
    a["gain"] = np.repeat(g["L0_attn_a_q_gain"][EVEN_FIRST], HD).reshape(KC, P).T
    w = g["L0_attn_b_Wqkv"].reshape(H, 3, HD, D).transpose(3, 1, 0, 2).reshape(D, 3 * D)
    a["wqk1"], a["wv1"] = chunked(w[:, :2 * D]), chunked(w[:, 2 * D:])
    a["wo1"] = chunked(g["L0_attn_b_Wproj"].T)
    a["bproj"] = np.tile(g["L0_attn_b_bproj"], (P, 1))
    a["rw"], a["rb"] = chunked(g["L0_ffn_router_w"]), np.tile(g["L0_ffn_router_bias"], (P, 1))
    a["swg"] = chunked(g["L0_ffn_swg"].transpose(1, 0, 2).reshape(D, SH))
    a["swu"] = chunked(g["L0_ffn_swu"].transpose(1, 0, 2).reshape(D, SH))
    a["swd"] = chunked(g["L0_ffn_swd"].reshape(SH, D))
    gu = np.concatenate([g["L0_ffn_wg"], g["L0_ffn_wu"]], axis=2).reshape(E, KC, P, 2 * FF).transpose(0, 2, 1, 3).reshape(E, P, 4 * FF)
    wd = g["L0_ffn_wd"].reshape(E, FF, 2, P).transpose(0, 2, 1, 3).reshape(E, P, P)
    a["we"] = np.concatenate([gu, wd], axis=2)
    return {k: np.ascontiguousarray(x) for k, x in a.items()}


def kernel(**inputs):
    import concourse.bacc as bacc
    from concourse.bass_utils import run_bass_kernel_spmd

    nc = bacc.Bacc("TRN2", target_bir_lowering=False, num_devices=1)
    arrays = {f"in_{k}": a for k, a in layout(inputs).items()}
    t = {k[3:]: nc.dram_tensor(k, a.shape, F32, kind="ExternalInput").ap() for k, a in arrays.items()}
    t["out"] = nc.dram_tensor("out", (B, S, D), F32, kind="ExternalOutput").ap()
    t["parts"] = nc.dram_tensor("parts", (B, 3, 2 * D, S), BF16, kind="Internal").ap()
    t["xd"] = nc.dram_tensor("xd", (SLOTS, D), F32, kind="Internal").ap()
    t["yd"] = nc.dram_tensor("yd", (SLOTS, D), F32, kind="Internal").ap()
    build(nc, t)
    r = run_bass_kernel_spmd(nc, [arrays], core_ids=[0])
    return r.results[0]["out"]
```

```python
from contextlib import ExitStack

import numpy as np
import concourse.bass as bass
from concourse import mybir

F32 = mybir.dt.float32
BF16 = mybir.dt.bfloat16
I32 = mybir.dt.int32
U32 = mybir.dt.uint32
ALU = mybir.AluOpType
ACT = mybir.ActivationFunctionType
AX = mybir.AxisListType

P = 128
B, S, D = 8, 256, 256
NT = B * S // P
TB = S // P
KC = D // P
H, HD = 16, 16
VW = 32
E, FF, K = 64, 64, 4
SH = 512
SC = SH // P
TERMS = [(0, 0), (0, 1), (1, 0), (1, 1), (0, 2), (2, 0)]
KR = len(TERMS) * HD
NTILE = B * S * K // P + E
SLOTS = NTILE * P
EPS_LN, EPS_UNIT = 1e-5, 1e-6
GRING, ERING = 8, 8


class Signal:

    def __init__(self, sem, per_run):
        self.sem, self.per_run = sem, per_run

    def __call__(self, run, count):
        value = count + run * self.per_run
        return self.sem, (max(value, 0) if isinstance(value, int) else value)


def pipeline(eng, items, depth, unroll, step):
    first = 2 * depth
    loops = (items - first) // unroll
    flags = lambda s: [0 <= s - d < items for d in range(depth + 1)]
    for s in range(first):
        step(s, s % unroll, flags(s))
    with eng.Fori(0, loops) as i:
        for j in range(unroll):
            step(i * unroll + (first + j), (first + j) % unroll, [True] * (depth + 1))
    for s in range(first + loops * unroll, items + depth):
        step(s, s % unroll, flags(s))


def build(nc, t):
    with ExitStack() as ctx:
        def sb(name, shape, dt=F32):
            return ctx.enter_context(nc.sbuf_tensor(name, shape, dt))

        def signal(name, per_run=0):
            return Signal(ctx.enter_context(nc.semaphore(name)), per_run)

        X = sb("X", [P, NT, D])
        stats = sb("stats", [P, NT, 6])
        mv = sb("mv", [P, NT, 2])
        ve = sb("ve", [P, NT])
        rstd = sb("rstd", [P, NT])
        mhalf = sb("mhalf", [P, NT])
        xn = sb("xn", [P, TB, D])
        xt = sb("xt", [P, KC, S])
        ident = sb("ident", [P, P])
        cb = sb("cb", [P, 2048 + 5 * P], BF16)
        esel = cb[:, 0:2048].rearrange("p (h k) -> p h k", h=H)
        identb, mask_s, mask_t, ltri, onesb = (cb[:, 2048 + i * P:2048 + (i + 1) * P] for i in range(5))
        rotm = sb("rotm", [P, P])
        headsum = sb("headsum", [P, 32])
        headsel = sb("headsel", [P, 2 * KC, P])
        cs = sb("cs", [P, 2, S])
        gain = sb("gain", [P, KC])
        wqk = [sb(f"wqk{r}", [P, KC, 2 * D]) for r in range(2)]
        wv = [sb(f"wv{r}", [P, KC, D]) for r in range(2)]
        wo = [sb(f"wo{r}", [P, KC, D]) for r in range(2)]
        bproj = sb("bproj", [P, D])
        rw = sb("rw", [P, KC, E])
        rb = sb("rb", [P, E])
        iot = sb("iot", [P, E])
        jcol = sb("jcol", [P, 1])
        swg = sb("swg", [P, KC, SH])
        swu = sb("swu", [P, KC, SH])
        swd = sb("swd", [P, SC, D])
        oh = sb("oh", [P, NT, K, E], BF16)
        rank = sb("rank", [P, NT, E])
        comb = sb("comb", [P, NT, K])
        slot = sb("slot", [P, NT, K], I32)
        te = sb("te", [1, P], I32)

        big = sb("big", [P, 2 * NT * D])
        v_all = big[:, 0:NT * D].rearrange("p (i h d) -> p i h d", i=NT, h=H)
        xn_all = big[:, 0:NT * D].rearrange("p (i d) -> p i d", i=NT)
        xnt_all = big[:, NT * D:].rearrange("p (c n) -> p c n", c=KC)
        y_all = big[:, NT * D:].rearrange("p (i d) -> p i d", i=NT)
        arena = sb("arena", [P, 12288])
        qs = [arena[:, 4096 * i:4096 * i + 2048].bitcast(BF16).rearrange("p (h n) -> p h n", h=H) for i in range(3)]
        ks = [arena[:, 4096 * i + 2048:4096 * i + 4096].bitcast(BF16).rearrange("p (h n) -> p h n", h=H) for i in range(3)]
        cload = arena[:, 0:2048 + 5 * P]
        wring = [arena[:, 384 * i:384 * i + 384] for i in range(ERING)]
        xpair = [arena[:, 3072 + 512 * i:3584 + 512 * i].rearrange("p (t d) -> p t d", t=2) for i in range(ERING // 2)]
        ypair = [arena[:, 5120 + 512 * i:5632 + 512 * i].rearrange("p (t d) -> p t d", t=2) for i in range(ERING // 2)]
        sth = arena[:, 7680:8704]
        sga = arena[:, 8704:9728]
        sg = [arena[:, 9728 + 1024 * i:10752 + 1024 * i].rearrange("p (c n) -> p c n", c=SC) for i in range(2)]
        gring = [arena[:, 7680 + 256 * i:7936 + 256 * i] for i in range(GRING)]
        tmp = sb("tmp", [P, 8192])
        qr = [tmp[:, 0:1024], tmp[:, 1024:2048]]
        sq = tmp[:, 2048:3072]
        nrm = tmp[:, 3072:3328]
        rinv = tmp[:, 3328:3584]
        qf = [tmp[:, 3584:4608], tmp[:, 4608:5632]]
        res = tmp[:, 5632:6656]
        rt = tmp[:, 6656:7168]
        pt = [arena[:, 8192 + 1536 * i:9728 + 1536 * i].bitcast(BF16).rearrange("p (s n) -> p s n", s=3) for i in range(2)]
        prob = [tmp[:, 512 * i:512 * i + 512] for i in range(4)]
        vb = [tmp[:, 2048 + 1024 * i:3072 + 1024 * i].rearrange("p (t h w) -> p t h w", t=TB, h=H) for i in range(3)]
        ot = [tmp[:, 5120 + 256 * i:5376 + 256 * i] for i in range(2)]
        yrow = tmp[:, 5632:6144]
        yt = tmp[:, 6144:6656]
        ybuf = [arena[:, 512 * i:512 * i + 512] for i in range(2)]
        ytb = [arena[:, 1024 + 512 * i:1536 + 512 * i] for i in range(2)]
        mx = tmp[:, 6656:6688]
        rs = tmp[:, 6688:6696]
        rm = tmp[:, 6720:6976]
        nm = tmp[:, 7168:7296].bitcast(BF16)
        nm2 = tmp[:, 7296:7424].bitcast(BF16)
        lb = tmp[:, 0:128]
        nmx = tmp[:, 128:130]
        m8 = tmp[:, 144:160]
        i8 = tmp[:, 160:176].bitcast(U32)
        idxf = tmp[:, 176:184]
        gk = tmp[:, 184:192]
        gs = tmp[:, 192:194]
        gr = tmp[:, 194:196]
        ex = tmp[:, 256:384]
        prod = tmp[:, 512:1536]
        msk = tmp[:, 1536:1600].bitcast(BF16)
        cum = tmp[:, 1600:1632].bitcast(BF16)
        cnt_i = tmp[:, 1664:1728].bitcast(I32)
        ntf = tmp[:, 1728:1792]
        incl = tmp[:, 1792:1856]
        base = tmp[:, 1856:1920]
        one64 = tmp[:, 1920:1984]
        cmp = tmp[:, 1984:2048]
        tef = tmp[:, 2048:2049]
        slotf = tmp[:, 2052:2068]
        slotmap = tmp[:, 4096:5120]
        xdt = [tmp[:, 5120 + 256 * i:5376 + 256 * i].rearrange("p (c n) -> p c n", c=KC) for i in range(2)]
        eth = [tmp[:, 5632 + 64 * i:5696 + 64 * i] for i in range(2)]
        eg = [tmp[:, 5760 + 64 * i:5824 + 64 * i] for i in range(2)]
        eh = [tmp[:, 5888 + 128 * i:6016 + 128 * i] for i in range(4)]
        eht = [tmp[:, 6400 + 128 * i:6528 + 128 * i] for i in range(2)]
        zero = sb("zero", [P, D])

        ps = [ctx.enter_context(nc.psum_tensor(f"ps{i}", [P, 512], F32)) for i in range(8)]

        consts_in, x_in = signal("consts_in"), signal("x_in")
        cast_done, setup_done = signal("cast_done"), signal("setup_done")
        phase_end = signal("phase_end")
        stat_done = signal("stat_done")
        ve_ready, rstd_ready = signal("ve_ready", 2), signal("rstd_ready", 2)
        xn_ready, xT_done, xt_ready = signal("xn_ready", 16), signal("xT_done", 8), signal("xt_ready", 8)
        qk_done, qk_raw = signal("qk_done", 16), signal("qk_raw", 16)
        v_done, v_out = signal("v_done", 8), signal("v_out", 8)
        sq_ready, ss_done, nrm_ready = signal("sq_ready"), signal("ss_done"), signal("nrm_ready")
        rinv_ready, spread_done, qn_ready, rot_done = signal("rinv_ready"), signal("spread_done"), signal("qn_ready"), signal("rot_done")
        rope_ready, qf_ready = signal("rope_ready"), signal("qf_ready")
        p1_ready, res_ready, p2_ready, p3_ready = (signal(n, 8) for n in ("p1_ready", "res_ready", "p2_ready", "p3_ready"))
        parts_stored = [signal(f"parts_stored{i}", 16 * B // 2) for i in range(2)]
        stack_in = [signal(f"stack_in{i}", 16 * len(TERMS) * 2 * (3 if i < 2 else 2)) for i in range(3)]
        vb_ready, vpad = signal("vb_ready", 8), signal("vpad", 1)
        s1_done, mx_ready, mT_done = signal("s1_done", 128), signal("mx_ready", 128), signal("mT_done", 8)
        nm3_ready = signal("nm3_ready", 8)
        nm1_ready, rm_ready, nm2_ready, nm_ready = (signal(n, 8) for n in ("nm1_ready", "rm_ready", "nm2_ready", "nm_ready"))
        s2_done, exp_ready, pv_done = signal("s2_done", 128), signal("exp_ready", 128), signal("pv_done", 128)
        ot_ready, oT_done, rs_ready, y_ready = (signal(n, 32) for n in ("ot_ready", "oT_done", "rs_ready", "y_ready"))
        yT_done, yt_ready, op_done, x_added = (signal(n) for n in ("yT_done", "yt_ready", "op_done", "x_added"))
        rn_ready, rT_done, rt_ready, rcopy_done = signal("rn_ready", 16), signal("rT_done", 8), signal("rt_ready", 8), signal("rcopy_done", 16)
        lg_done, nmx_ready, ex_ready = signal("lg_done", 8), signal("nmx_ready", 8), signal("ex_ready", 8)
        topk = signal("topk")
        msk_ready, rank_done, rank_out = signal("msk_ready", 8), signal("rank_done", 8), signal("rank_out", 8)
        cum_ready, cnt_done = signal("cum_ready", 8), signal("cnt_done", 1)
        slot_ready, tef_ready, teT_done, te_ready = signal("slot_ready", 4), signal("tef_ready", 1), signal("teT_done", 1), signal("te_ready", 1)
        zeroed, scattered = signal("zeroed"), signal("scattered", 16 * NT * K)
        gu_done, sth_ready, sga_ready, sg_ready = signal("gu_done", 16), signal("sth_ready", 16), signal("sga_ready", 16), signal("sg_ready", 16)
        sd_done, sx_added = signal("sd_done", 8), signal("sx_added", 8)
        w_in = [signal(f"w_in{i}", 16 * NTILE // ERING) for i in range(ERING)]
        xd_in = [signal(f"xd_in{i}", 16 * NTILE // ERING) for i in range(ERING // 2)]
        y_out = [signal(f"y_out{i}", 16 * NTILE // ERING) for i in range(ERING // 2)]
        eT_done, ext_ready, egu_done, eth_ready = (signal(n, NTILE) for n in ("eT_done", "ext_ready", "egu_done", "eth_ready"))
        eg_ready, eh_ready, hT_done, eht_ready = (signal(n, NTILE) for n in ("eg_ready", "eh_ready", "hT_done", "eht_ready"))
        ed_done, ya_ready, yv_ready = (signal(n, NTILE) for n in ("ed_done", "ya_ready", "yv_ready"))
        g_in = [signal(f"g_in{i}", 16 * NT * K // GRING) for i in range(GRING)]
        g_used = signal("g_used", NT * K)
        tile_final, stored = signal("tile_final", NT), signal("stored")

        CONSTS = [(cload, "cload"), (ident[:, :], "ident"), (rotm[:, :], "rotm"), (headsum[:, :], "headsum"), (headsel[:, :, :], "headsel"),
                  (cs[:, :, :], "cs"), (gain[:, :], "gain"), (bproj[:, :], "bproj"), (rw[:, :, :], "rw"),
                  (rb[:, :], "rb"), (iot[:, :], "iot"), (jcol[:, :], "jcol"), (swg[:, :, :], "swg"),
                  (swu[:, :, :], "swu"), (swd[:, :, :], "swd")]
        for r in range(2):
            CONSTS += [(wqk[r][:, :, :], f"wqk{r}"), (wv[r][:, :, :], f"wv{r}"), (wo[r][:, :, :], f"wo{r}")]
        x_tiles = t["x"].rearrange("b (t p) d -> p (b t) d", p=P)
        out_tiles = t["out"].rearrange("b (t p) d -> p (b t) d", p=P)
        parts = t["parts"]
        xd, yd = t["xd"], t["yd"]

        epsu = sb("epsu", [P, 1])[:, :]
        nm_zero, bias_added, stat_a = signal("nm_zero"), signal("bias_added"), signal("stat_a", 2 * B)
        yb_ready, yT1_done, yt1_ready, op1_done, x1_added = (signal(n) for n in ("yb_ready", "yT1_done", "yt1_ready", "op1_done", "x1_added"))
        stat_b, settled = signal("stat_b"), signal("settled")
        cum0, cum_half, disp = signal("cum0"), signal("cum_half", 8), signal("disp")
        disp_base = [0]

        block = ctx.enter_context(nc.Block())

        barriers = {}

        def barrier(e, name):
            barriers[name] = barriers.get(name, 0) + 1
            e.drain().then_inc(phase_end.sem, 1)
            e.wait_ge(phase_end.sem, 3 * barriers[name])

        def stored_count(j, i):
            return 16 * max(j // ERING, 0) if isinstance(j, int) else (j - i) * (16 // ERING)

        def down_bank(i, half):
            return ps[((5, 6), (7, 1))[i % 2][half]]

        def causal(r):
            return r == 0

        @block.sync
        def _(sp):
            sp.dma_start(X[:, :, :], x_tiles).then_inc(x_in.sem, 16)
            for dst, name in CONSTS:
                sp.dma_start(dst, t[name]).then_inc(consts_in.sem, 16)
            sp.wait_ge(setup_done.sem, 1)
            zsrc = zero[:, :].rearrange("p (a d) -> p a d", a=1).broadcast_to([P, NTILE, D])
            sp.dma_start(xd.rearrange("(p a) d -> p a d", a=NTILE), zsrc).then_inc(zeroed.sem, 16)

            for r in range(2):
                def store_parts(b, j):
                    sp.wait_ge(*p3_ready(r, b + 1))
                    sp.dma_start(parts[bass.ds(b, 1)].rearrange("a s (c p) n -> p (a s) c n", p=P),
                                 pt[j].rearrange("p s (c n) -> p s c n", c=4)).then_inc(parts_stored[j].sem, 16)

                def load_stack(b, i):
                    for side, dst in ((0, qs[i]), (1, ks[i])):
                        for n, term in enumerate(TERMS):
                            src = parts[bass.ds(b, 1), term[side], side * D:(side + 1) * D, :].rearrange(
                                "a (h d) n -> d (a h) n", d=HD)
                            sp.dma_start(dst[HD * n:HD * n + HD, :, :], src).then_inc(stack_in[i].sem, 16)

                store_parts(0, 0)
                store_parts(1, 1)
                for b in range(2):
                    sp.wait_ge(*parts_stored[b](r, 16))
                    load_stack(b, b)
                with sp.Fori(0, B // 2 - 1) as it:
                    for j in range(2):
                        store_parts(it * 2 + (2 + j), j)
                for i in range(2):
                    sp.wait_ge(*parts_stored[i](r, 16 * B // 2))
                with sp.Fori(0, 2) as it:
                    for j in range(3):
                        b = it * 3 + (2 + j)
                        sp.wait_ge(*s2_done(r, (b - 2) * H + 1))
                        load_stack(b, (2 + j) % 3)

                def load_weights(j, i):
                    ev = sp.value_load(te[0:1, bass.ds(j, 1)], min_val=0, max_val=E - 1)
                    sp.dma_start(wring[i], t["we"][bass.ds(ev, 1)].rearrange("a p n -> p (a n)")).then_inc(w_in[i].sem, 16)
                sp.wait_ge(*te_ready(r, 1))
                for j in range(ERING):
                    load_weights(j, j)
                with sp.Fori(0, NTILE // ERING - 1) as it:
                    for i in range(ERING):
                        j = it * ERING + (ERING + i)
                        sp.wait_ge(*ed_done(r, j - (ERING - 1)))
                        load_weights(j, i)
            for i in range(0, NT, TB):
                sp.wait_ge(tile_final.sem, NT + i + TB)
                sp.dma_start(out_tiles[:, i:i + TB, :], X[:, i:i + TB, :]).then_inc(stored.sem, 16)
            sp.wait_ge(stored.sem, 16 * NT // TB)

        @block.gpsimd
        def _(pool):
            pool.memset(mhalf[:, :], -0.5).then_inc(vpad.sem, 1)
            pool.wait_ge(vpad.sem, 1)

            def rsqrt_variance(run, n):
                pool.wait_ge(*ve_ready(run, n))
                pool.tensor_tensor(rstd[:, :], ve[:, :], mhalf[:, :], ALU.pow).then_inc(rstd_ready.sem, 1)

            for r in range(2):
                rsqrt_variance(r, 1)
                pool.wait_ge(*v_out(r, 8))
                pool.wait_ge(*p3_ready(r, B))
                for i in range(3):
                    pool.memset(vb[i][:, :, :, HD:HD + 1], 1.0)
                    pool.memset(vb[i][:, :, :, HD + 1:VW], 0.0).then_inc(vpad.sem, 1)
                pool.wait_ge(vpad.sem, 1 + 3 * (r + 1))

                def copy_v(b, i):
                    pool.tensor_copy(vb[i][:, :, :, 0:HD], v_all[:, bass.ds(b * TB, TB), :, :]).then_inc(vb_ready.sem, 1)

                copy_v(0, 0)
                copy_v(1, 1)
                with pool.Fori(0, 2) as it:
                    for j in range(3):
                        b = it * 3 + (2 + j)
                        pool.wait_ge(*pv_done(r, (b - 2) * H + 1))
                        copy_v(b, (2 + j) % 3)

                if r == 1:
                    pool.wait_ge(*y_ready(r, 32))
                    for b in range(2):
                        pool.tensor_copy(ybuf[b].rearrange("p (t d) -> p t d", t=TB), y_all[:, b * TB:b * TB + TB, :]).then_inc(yb_ready.sem, 1)
                    with pool.Fori(0, (B - 2) // 2) as it:
                        for j in range(2):
                            b = it * 2 + (2 + j)
                            pool.wait_ge(yT1_done.sem, b - 1)
                            pool.tensor_copy(ybuf[j].rearrange("p (t d) -> p t d", t=TB), y_all[:, bass.ds(b * TB, TB), :]).then_inc(yb_ready.sem, 1)
                rsqrt_variance(r, 2)
                with pool.Fori(0, B) as b:
                    pool.wait_ge(*rn_ready(r, 2 * b + 2))
                    pool.tensor_copy(xn_all[:, bass.ds(b * TB, TB), :], xn[:, :, :]).then_inc(rcopy_done.sem, 1)
                    pool.wait_ge(*rt_ready(r, b + 1))
                    pool.tensor_copy(xnt_all[:, :, bass.ds(b * S, S)], xt[:, :, :]).then_inc(rcopy_done.sem, 1)

                pool.wait_ge(zeroed.sem, 16)
                pool.wait_ge(*rcopy_done(r, 2 * B))
                for i in range(NT):
                    if i % 4 == 0:
                        pool.wait_ge(*slot_ready(r, i // 4 + 1))
                    for k in range(K):
                        pool.indirect_dma_start(xd[:, :], bass.IndirectOffsetOnAxis(ap=slot[:, i, k:k + 1], axis=0),
                                                xn_all[:, i, :], None).then_inc(scattered.sem, 16)

                PAIRS, PR = NTILE // 2, ERING // 2

                def load_rows(q, i):
                    pool.dma_start(xpair[i], xd[bass.ds(q * 2 * P, 2 * P), :].rearrange("(t p) d -> p t d", p=P)).then_inc(xd_in[i].sem, 16)

                def store_results(q, i):
                    pool.wait_ge(*ya_ready(r, q * 2 + 2))
                    pool.wait_ge(*yv_ready(r, q * 2 + 2))
                    pool.dma_start(yd[bass.ds(q * 2 * P, 2 * P), :].rearrange("(t p) d -> p t d", p=P), ypair[i]).then_inc(y_out[i].sem, 16)
                pool.wait_ge(*scattered(r, 16 * NT * K))
                for q in range(PR):
                    load_rows(q, q)
                with pool.Fori(0, PAIRS // PR - 1) as it:
                    for i in range(PR):
                        q = it * PR + i
                        pool.wait_ge(*eT_done(r, q * 2 + 2))
                        load_rows(q + PR, i)
                        store_results(q, i)
                for i in range(PR):
                    store_results(PAIRS - PR + i, i)

                for i in range(ERING // 2):
                    pool.wait_ge(*y_out[i](r, 16 * NTILE // ERING))
                for i in range(NT):
                    for k in range(K):
                        n = i * K + k
                        if n >= GRING:
                            pool.wait_ge(*g_used(r, n - GRING + 1))
                        pool.indirect_dma_start(gring[n % GRING], None, yd[:, :],
                                                bass.IndirectOffsetOnAxis(ap=slot[:, i, k:k + 1], axis=0)).then_inc(g_in[n % GRING].sem, 16)

        @block.tensor
        def _(pe):
            pe.wait_ge(consts_in.sem, 16 * len(CONSTS))
            pe.wait_ge(cast_done.sem, 1)

            for r in range(2):
                barrier(pe, "pe")

                def project_step(s, i, has):
                    if has[0]:
                        pe.wait_ge(*xn_ready(r, s * 2 + 2))
                        pe.wait_ge(*xt_ready(r, s))
                        for tt in range(TB):
                            for c in range(KC):
                                mm = pe.transpose(ps[0][:, c * S + tt * P:c * S + tt * P + P],
                                                  xn[:, tt, c * P:(c + 1) * P], ident[:, :])
                        mm.then_inc(xT_done.sem, 1)
                    if has[1] and r == 0:
                        pe.wait_ge(sq_ready.sem, s)
                        pe.wait_ge(nrm_ready.sem, s - 1)
                        for c in range(2 * KC):
                            mm = pe.matmul(ps[4][32 * c:32 * c + 32, 0:S], headsum[:, :], sq[:, c * S:(c + 1) * S],
                                           start=True, stop=True)
                        mm.then_inc(ss_done.sem, 1)
                    if has[0]:
                        pe.wait_ge(*xt_ready(r, s + 1))
                        for side in range(2):
                            pe.wait_ge(*qk_raw(r, s * 2))
                            for j in range(2):
                                col = side * D + j * P
                                for c in range(KC):
                                    mm = pe.matmul(ps[1 + side][:, j * S:(j + 1) * S], wqk[r][:, c, col:col + P],
                                                   xt[:, c, :], start=(c == 0), stop=(c == KC - 1))
                            mm.then_inc(qk_done.sem, 1)
                    if has[1] and r == 0:
                        pe.wait_ge(rinv_ready.sem, s)
                        pe.wait_ge(qn_ready.sem, (s - 1) * 3)
                        for c in range(2 * KC):
                            mm = pe.matmul(ps[5 + c // 2 * 2][:, c % 2 * S:c % 2 * S + S], headsel[:, c, :], rinv,
                                           start=True, stop=True)
                        mm.then_inc(spread_done.sem, 1)
                    if has[0]:
                        pe.wait_ge(*v_out(r, s))
                        for tt in range(TB):
                            for c in range(KC):
                                mm = pe.matmul(ps[3][:, tt * D:(tt + 1) * D], xt[:, c, tt * P:(tt + 1) * P],
                                               wv[r][:, c, :], start=(c == 0), stop=(c == KC - 1))
                        mm.then_inc(v_done.sem, 1)
                    if has[1] and r == 0:
                        pe.wait_ge(qn_ready.sem, s * 3)
                        pe.wait_ge(rope_ready.sem, (s - 1) * 2)
                        for side in range(2):
                            mm = pe.matmul(ps[6][:, side * S:(side + 1) * S], rotm[:, :],
                                           qf[1 - i][:, side * 512:side * 512 + S], start=True, stop=True)
                        mm.then_inc(rot_done.sem, 1)
                pipeline(pe, B, 2 - r, 2, project_step)
                barrier(pe, "pe")

                def scores(s, i, h):
                    if h == 0:
                        n = 16 * len(TERMS) * 2
                        b3 = s // 3 if isinstance(s, int) else None
                        pe.wait_ge(*stack_in[i](r, n * (b3 + 1) if b3 is not None else stack_count(s, i, n)))
                    pe.wait_ge(*mx_ready(r, s * H + max(h - 1, 0)))
                    bank = ps[h % 2]
                    for tt in range(TB):
                        keys = (tt + 1) * P if causal(r) else S
                        pe_last = pe.matmul(bank[:, tt * S:tt * S + keys], qs[i][0:KR, h, tt * P:(tt + 1) * P],
                                            ks[i][0:KR, h, 0:keys], start=True, stop=not causal(r))
                        if causal(r):
                            pe_last = pe.matmul(bank[:, tt * S + tt * P:tt * S + (tt + 1) * P], identb, mask_s,
                                                start=False, stop=True)
                    pe_last.then_inc(s1_done.sem, 1)

                def stack_count(s, i, n):
                    return (s - i + 3) * (n // 3)

                def probs(s, i, h):
                    b = s - 1
                    if h == 0:
                        pe.wait_ge(*nm_ready(r, s))
                        pe.wait_ge(*nm3_ready(r, s))
                    pe.wait_ge(*exp_ready(r, b * H + max(h - 1, 0)))
                    bank = ps[2 + h % 2]
                    for kb in range(TB):
                        q0 = kb * P if causal(r) else 0
                        out = bank[:, kb * S:kb * S + S - q0]
                        pe.matmul(out, ks[i][0:KR, h, kb * P:(kb + 1) * P], qs[i][0:KR, h, q0:S],
                                  start=True, stop=False)
                        mm = pe.matmul(out, esel[0:96, h, :], nm[0:96, q0:S], start=False, stop=not causal(r))
                        if causal(r):
                            mm = pe.matmul(bank[:, kb * S:kb * S + P], identb, mask_t, start=False, stop=True)
                    mm.then_inc(s2_done.sem, 1)

                def weigh(s, i, h):
                    b, g, j = s - 1, h // 4, h % 4
                    if h == 0:
                        pe.wait_ge(*vb_ready(r, s))
                    pe.wait_ge(*exp_ready(r, b * H + h + 1))
                    if j == 0:
                        pe.wait_ge(*ot_ready(r, b * 4 + max(g - 1, 0)))
                    bank = ps[4 + g % 2]
                    for kb in range(TB):
                        q0 = kb * P if causal(r) else 0
                        mm = pe.matmul(bank[32 * j:32 * j + VW, q0:S], vb[i][:, kb, h, :],
                                       prob[h % 4][:, kb * S:kb * S + S - q0], start=(kb == 0), stop=(kb == TB - 1))
                    mm.then_inc(pv_done.sem, 1)

                def turn_group(s, g):
                    b = s - 1
                    pe.wait_ge(*ot_ready(r, b * 4 + g + 1))
                    pe.wait_ge(*y_ready(r, b * 4 + g))
                    for tt in range(TB):
                        mm = pe.transpose(ps[6][:, tt * P:(tt + 1) * P], ot[g % 2][:, tt * P:(tt + 1) * P], ident[:, :])
                    mm.then_inc(oT_done.sem, 1)

                def turn_output(s):
                    pe.wait_ge(*y_ready(r, s * 4))
                    for tt in range(TB):
                        for c in range(KC):
                            mm = pe.transpose(ps[6][:, c * S + tt * P:c * S + tt * P + P],
                                              yrow[:, tt * D + c * P:tt * D + (c + 1) * P], ident[:, :])
                    mm.then_inc(yT_done.sem, 1)

                def output(s):
                    pe.wait_ge(*yt_ready(r, s))
                    for tt in range(TB):
                        for c in range(KC):
                            mm = pe.matmul(ps[7][:, tt * D:(tt + 1) * D], yt[:, c * S + tt * P:c * S + tt * P + P],
                                           wo[r][:, c, :], start=(c == 0), stop=(c == KC - 1))
                    mm.then_inc(op_done.sem, 1)

                def turn_maxima(s):
                    pe.wait_ge(*mx_ready(r, s * H + H))
                    if r == 0:
                        pe.wait_ge(x_added.sem, s - 1 if not isinstance(s, int) or s else 0)
                    for tt in range(TB):
                        mm = pe.transpose(ps[7][0:H, tt * P:(tt + 1) * P], mx[:, tt * H:(tt + 1) * H], ident[:, :])
                    mm.then_inc(mT_done.sem, 1)

                def attend_step(s, i, has):
                    iprev = (i - 1) % 3
                    finish = has[1] and not (isinstance(s, int) and s == 1)
                    for h in range(H + 2):
                        if h < H and has[0]:
                            scores(s, i, h)
                        if h == H and has[0]:
                            turn_maxima(s)
                        if finish and h == 1:
                            turn_group(s - 1, 3)
                        if finish and h == 3 and r == 0:
                            turn_output(s - 1)
                        if finish and h == 5 and r == 0:
                            output(s - 1)
                        if has[1]:
                            if h < H:
                                probs(s, iprev, h)
                            if h >= 2:
                                weigh(s, iprev, h - 2)
                            if h >= 8 and h % 4 == 0:
                                turn_group(s, h // 4 - 2)
                pipeline(pe, B, 1, 3, attend_step)
                turn_group(B, 3)
                if r == 0:
                    turn_output(B)
                    output(B)
                if r == 1:
                    def output_step(s, i, has):
                        if has[0]:
                            pe.wait_ge(yb_ready.sem, s + 1)
                            pe.wait_ge(yt1_ready.sem, s)
                            for tt in range(TB):
                                for c in range(KC):
                                    mm = pe.transpose(ps[0][:, c * S + tt * P:c * S + tt * P + P],
                                                      ybuf[i][:, tt * D + c * P:tt * D + (c + 1) * P], ident[:, :])
                            mm.then_inc(yT1_done.sem, 1)
                        if has[1]:
                            pe.wait_ge(yt1_ready.sem, s)
                            pe.wait_ge(x1_added.sem, s - 1)
                            for tt in range(TB):
                                for c in range(KC):
                                    mm = pe.matmul(ps[7][:, tt * D:(tt + 1) * D], ytb[1 - i][:, c * S + tt * P:c * S + tt * P + P],
                                                   wo[r][:, c, :], start=(c == 0), stop=(c == KC - 1))
                            mm.then_inc(op1_done.sem, 1)
                    barrier(pe, "pe")
                    pipeline(pe, B, 1, 2, output_step)
                barrier(pe, "pe")

                def route_step(s, i, has):
                    if has[0]:
                        pe.wait_ge(*rn_ready(r, s * 2 + 2))
                        pe.wait_ge(*rt_ready(r, s))
                        for tt in range(TB):
                            for c in range(KC):
                                mm = pe.transpose(ps[0][:, c * S + tt * P:c * S + tt * P + P],
                                                  xn[:, tt, c * P:(c + 1) * P], ident[:, :])
                        mm.then_inc(rT_done.sem, 1)
                        pe.wait_ge(*rt_ready(r, s + 1))
                        pe.wait_ge(*nmx_ready(r, s - 1 if not isinstance(s, int) or s else 0))
                        pe.wait_ge(*ex_ready(r, s - 1 if not isinstance(s, int) or s else 0))
                        for tt in range(TB):
                            for c in range(KC):
                                mm = pe.matmul(ps[1 + i][:, tt * E:(tt + 1) * E], xt[:, c, tt * P:(tt + 1) * P],
                                               rw[:, c, :], start=(c == 0), stop=(c == KC - 1))
                        mm.then_inc(lg_done.sem, 1)
                    if has[1]:
                        pe.wait_ge(*msk_ready(r, s))
                        pe.wait_ge(*cum_ready(r, s - 1))
                        pe.wait_ge(*rank_out(r, s - 1))
                        pe.matmul(ps[3][:, 0:E], ltri, msk[:, 0:E], start=True, stop=False)
                        pe.matmul(ps[3][:, 0:E], onesb, cum, start=False, stop=True)
                        pe.matmul(ps[3][:, E:2 * E], ltri, msk[:, E:2 * E], start=True, stop=False)
                        pe.matmul(ps[3][:, E:2 * E], onesb, msk[:, 0:E], start=False, stop=False)
                        pe.matmul(ps[3][:, E:2 * E], onesb, cum, start=False, stop=True).then_inc(rank_done.sem, 1)
                pipeline(pe, B, 1, 2, route_step)
                pe.wait_ge(*cum_ready(r, B))
                pe.matmul(ps[4][:, 0:E], onesb, cum, start=True, stop=True).then_inc(cnt_done.sem, 1)
                pe.wait_ge(*tef_ready(r, 1))
                pe.transpose(ps[5][0:1, 0:P], tef, ident[:, :]).then_inc(teT_done.sem, 1)
                barrier(pe, "pe")

                pe.wait_ge(*rcopy_done(r, 2 * B))

                def shared_step(s, i, has):
                    for half in range(2):
                        if has[0]:
                            pe.wait_ge(*sg_ready(r, s * 2 + half if half == 0 else s * 2))
                            for w, bank in ((swg, ps[half]), (swu, ps[2 + half])):
                                for j in range(2):
                                    ch = half * 2 + j
                                    for c in range(KC):
                                        mm = pe.matmul(bank[:, j * S:(j + 1) * S], w[:, c, ch * P:(ch + 1) * P],
                                                       xnt_all[:, c, bass.ds(s * S, S)], start=(c == 0), stop=(c == KC - 1))
                            mm.then_inc(gu_done.sem, 1)
                    if has[1]:
                        pe.wait_ge(*sg_ready(r, s * 2))
                        pe.wait_ge(*sx_added(r, s - 1))
                        for tt in range(TB):
                            for ch in range(SC):
                                mm = pe.matmul(ps[4][:, tt * D:(tt + 1) * D], sg[1 - i][:, ch, tt * P:(tt + 1) * P],
                                               swd[:, ch, :], start=(ch == 0), stop=(ch == SC - 1))
                        mm.then_inc(sd_done.sem, 1)
                pipeline(pe, B, 1, 2, shared_step)
                barrier(pe, "pe")

                def expert_step(s, i, has):
                    if has[0]:
                        j = s
                        pe.wait_ge(*xd_in[i // 2](r, ring_count(j, i)))
                        pe.wait_ge(*ext_ready(r, j))
                        for c in range(KC):
                            mm = pe.transpose(ps[0][:, c * P:(c + 1) * P], xpair[i // 2][:, i % 2, c * P:(c + 1) * P], ident[:, :])
                        mm.then_inc(eT_done.sem, 1)
                    if has[1]:
                        j, i1 = s - 1, (i - 1) % ERING
                        pe.wait_ge(*w_in[i1](r, ring_count(j, i1)))
                        pe.wait_ge(*ext_ready(r, j + 1))
                        pe.wait_ge(*eh_ready(r, j - 1 if not isinstance(j, int) or j else 0))
                        for c in range(KC):
                            mm = pe.matmul(ps[2 + i1 % 2][:, 0:2 * FF], xdt[i1 % 2][:, c, :], wring[i1][:, c * 128:(c + 1) * 128],
                                           start=(c == 0), stop=(c == KC - 1))
                        mm.then_inc(egu_done.sem, 1)
                    if has[3]:
                        j, i3 = s - 3, (i - 3) % ERING
                        pe.wait_ge(*eh_ready(r, j + 1))
                        pe.wait_ge(*eht_ready(r, j))
                        pe.transpose(ps[4][:, 0:P], eh[i3 % 4], ident[:, :]).then_inc(hT_done.sem, 1)
                    if has[4]:
                        j, i4 = s - 4, (i - 4) % ERING
                        pe.wait_ge(*eht_ready(r, j + 1))
                        pe.wait_ge(*ya_ready(r, j - 1 if not isinstance(j, int) or j else 0))
                        pe.wait_ge(*yv_ready(r, j - 1 if not isinstance(j, int) or j else 0))
                        for half in range(2):
                            mm = pe.matmul(down_bank(i4, half)[:, 0:P], eht[i4 % 2][64 * half:64 * half + 64, :],
                                           wring[i4][64 * half:64 * half + 64, 256:384], start=True, stop=True)
                        mm.then_inc(ed_done.sem, 1)

                def ring_count(j, i):
                    return 16 * (j // ERING + 1) if isinstance(j, int) else (j - i + ERING) * (16 // ERING)
                pipeline(pe, NTILE, 4, ERING, expert_step)

        @block.scalar
        def _(act):
            def copy(dst, src):
                return act.activation(dst, src, ACT.Copy)

            act.wait_ge(setup_done.sem, 2)
            for r in range(2):
                barrier(act, "act")

                def project_step(s, i, has):
                    last = 2 - r
                    if has[0]:
                        act.wait_ge(*xT_done(r, s + 1))
                        act.wait_ge(*v_done(r, s))
                        copy(xt[:, :, :].rearrange("p c n -> p (c n)"), ps[0][:, :]).then_inc(xt_ready.sem, 1)
                    if has[1] and r == 0:
                        act.wait_ge(rinv_ready.sem, s - 1)
                        act.wait_ge(ss_done.sem, s)
                        act.activation(nrm, ps[4][:, 0:S], ACT.Sqrt, bias=epsu).then_inc(nrm_ready.sem, 1)
                    if has[last]:
                        n = s - last
                        k = i if r == 0 else 1 - i
                        src, part = (qf if r == 0 else qr)[k], pt[k]
                        if r == 0:
                            act.wait_ge(qf_ready.sem, n + 1)
                        else:
                            act.wait_ge(*qk_raw(r, s * 2))
                        act.wait_ge(*parts_stored[k](r, (n - (k if not isinstance(n, int) else n % 2)) * 8))
                        copy(part[:, 0, :], src).then_inc(p1_ready.sem, 1)
                    for side in range(2):
                        if has[0]:
                            if side == 0 and r == 0:
                                act.wait_ge(qn_ready.sem, before(s, 3))
                            elif side == 0:
                                act.wait_ge(*res_ready(r, before(s, 1)))
                            act.wait_ge(*qk_done(r, s * 2 + side + 1))
                            act.activation(qr[i][:, side * 512:(side + 1) * 512], ps[1 + side][:, :], ACT.Copy,
                                           scale=HD ** -0.5 if r == 1 and side == 0 else 1.0).then_inc(qk_raw.sem, 1)
                        if has[last] and side == 0:
                            act.wait_ge(*res_ready(r, n + 1))
                            copy(part[:, 1, :], res).then_inc(p2_ready.sem, 1)
                    if has[0]:
                        if r == 0:
                            act.wait_ge(*qk_raw(r, s * 2 + 2))
                            act.wait_ge(ss_done.sem, s)
                            act.activation(sq, qr[i], ACT.Square).then_inc(sq_ready.sem, 1)
                        act.wait_ge(*v_done(r, s + 1))
                        copy(v_all[:, bass.ds(s * TB, TB), :, :].rearrange("p t h d -> p (t h d)"), ps[3][:, :]).then_inc(v_out.sem, 1)

                def before(n, per):
                    return max((n - 1) * per, 0) if isinstance(n, int) else (n - 1) * per
                pipeline(act, B, 2 - r, 2, project_step)
                barrier(act, "act")

                def take_turned(s):
                    act.wait_ge(*yT_done(r, s))
                    copy(yt, ps[6][:, :]).then_inc(yt_ready.sem, 1)

                def attend_step(s, i, has):
                    if has[1]:
                        for h in range(H):
                            if h == 4 and r == 0 and not (isinstance(s, int) and s == 1):
                                take_turned(s - 1)
                            b = s - 1
                            act.wait_ge(*s2_done(r, b * H + h + 1))
                            act.wait_ge(*pv_done(r, b * H + max(h - 3, 0)))
                            n = S + P if causal(r) else 2 * S
                            act.activation(prob[h % 4][:, 0:n], ps[2 + h % 2][:, 0:n], ACT.Exp).then_inc(exp_ready.sem, 1)
                    if has[0]:
                        act.wait_ge(*mT_done(r, s + 1))
                        copy(nm[0:H, :], ps[7][0:H, 0:S]).then_inc(nm1_ready.sem, 1)
                        act.wait_ge(*rm_ready(r, s + 1))
                        copy(nm2[0:H, :], rm[0:H, :]).then_inc(nm2_ready.sem, 1)
                        copy(nm[32:32 + H, :], rm[0:H, :]).then_inc(nm3_ready.sem, 1)
                pipeline(act, B, 1, 3, attend_step)
                if r == 0:
                    take_turned(B)
                if r == 1:
                    def output_step(s, i, has):
                        if has[0]:
                            act.wait_ge(yT1_done.sem, s + 1)
                            act.wait_ge(op1_done.sem, s - 1 if not isinstance(s, int) or s else 0)
                            copy(ytb[i], ps[0][:, :]).then_inc(yt1_ready.sem, 1)
                    barrier(act, "act")
                    pipeline(act, B, 1, 2, output_step)
                barrier(act, "act")

                def route_step(s, i, has):
                    if has[0]:
                        act.wait_ge(*rT_done(r, s + 1))
                        act.wait_ge(*lg_done(r, s))
                        act.wait_ge(*rcopy_done(r, s * 2))
                        copy(xt[:, :, :].rearrange("p c n -> p (c n)"), ps[0][:, :]).then_inc(rt_ready.sem, 1)
                    if has[1]:
                        act.wait_ge(*nmx_ready(r, s))
                        for tt in range(TB):
                            ins = act.activation(ex[:, tt * E:(tt + 1) * E], ps[1 + (1 - i)][:, tt * E:(tt + 1) * E],
                                                 ACT.Exp, bias=nmx[:, tt:tt + 1])
                        ins.then_inc(ex_ready.sem, 1)
                        act.wait_ge(*rank_done(r, s))
                        copy(rank[:, bass.ds((s - 1) * TB, TB), :],
                             ps[3][:, 0:2 * E].rearrange("p (t e) -> p t e", t=TB)).then_inc(rank_out.sem, 1)
                pipeline(act, B, 1, 2, route_step)
                barrier(act, "act")

                def shared_step(s, i, has):
                    if has[0]:
                        for half in range(2):
                            act.wait_ge(*gu_done(r, s * 2 + half + 1))
                            act.wait_ge(*sga_ready(r, s * 2))
                            act.activation(sth[:, half * 512:(half + 1) * 512], ps[half][:, :], ACT.Tanh,
                                           scale=0.5).then_inc(sth_ready.sem, 1)
                pipeline(act, B, 1, 2, shared_step)
                barrier(act, "act")

                def expert_step(s, i, has):
                    if has[0]:
                        act.wait_ge(*eT_done(r, s + 1))
                        act.wait_ge(*egu_done(r, s - 1 if not isinstance(s, int) or s else 0))
                        copy(xdt[i % 2].rearrange("p c n -> p (c n)"), ps[0][:, 0:D]).then_inc(ext_ready.sem, 1)
                    if has[1]:
                        j, i1 = s - 1, (i - 1) % ERING
                        act.wait_ge(*egu_done(r, j + 1))
                        act.wait_ge(*eg_ready(r, j - 1 if not isinstance(j, int) or j else 0))
                        act.activation(eth[i1 % 2], ps[2 + i1 % 2][:, 0:FF], ACT.Tanh, scale=0.5).then_inc(eth_ready.sem, 1)
                    if has[4]:
                        j, i4 = s - 4, (i - 4) % ERING
                        act.wait_ge(*ed_done(r, j + 1))
                        act.wait_ge(*y_out[i4 // 2](r, stored_count(j, i4)))
                        copy(ypair[i4 // 2][:, i4 % 2, 0:P], down_bank(i4, 0)[:, 0:P]).then_inc(ya_ready.sem, 1)
                pipeline(act, NTILE, 4, ERING, expert_step)

        @block.vector
        def _(dve):
            dve.memset(zero[:, :], 0.0).then_inc(setup_done.sem, 1)
            dve.memset(epsu, EPS_UNIT).then_inc(setup_done.sem, 1)
            dve.wait_ge(consts_in.sem, 16 * len(CONSTS))
            dve.tensor_copy(cb[:, :], cload).then_inc(cast_done.sem, 1)
            dve.wait_ge(x_in.sem, 16)
            for i in range(NT):
                dve.bn_stats(stats[:, i % 2, :], X[:, i, :]).then_inc(stat_done.sem, 1)
                dve.wait_ge(stat_done.sem, i + 1)
                dve.bn_aggr(mv[:, i, :], stats[:, i % 2, :]).then_inc(stat_b.sem, 1)
            dve.wait_ge(stat_b.sem, NT)
            stat_at = NT

            def settle():
                dve.sem_inc(settled.sem, 1)

            def make_rstd(r, n):
                dve.tensor_scalar(ve[:, :], mv[:, :, 1], EPS_LN, None, ALU.add).then_inc(ve_ready.sem, 1)
                dve.wait_ge(*rstd_ready(r, n))

            def normalise(b, done):
                for tt in range(TB):
                    at = bass.ds(b * TB + tt, 1)
                    dve.tensor_scalar(xn[:, tt, :], X[:, at, :].rearrange("p a d -> p (a d)"),
                                      mv[:, at, 0:1].rearrange("p a o -> p (a o)"), rstd[:, at],
                                      ALU.subtract, ALU.mult).then_inc(done.sem, 1)

            for r in range(2):
                barrier(dve, "dve")
                make_rstd(r, 1)
                if r == 0:
                    dve.wait_ge(consts_in.sem, 16 * len(CONSTS))

                def project_step(s, i, has):
                    last = 2 - r
                    if has[0]:
                        dve.wait_ge(*xT_done(r, s))
                        normalise(s, xn_ready)
                    if r == 0 and has[2]:
                        roped = qf[i].rearrange("p (a n) -> p a n", a=2)[:, :, 0:S]
                        cos = cs[:, 0:1, :].broadcast_to([P, 2, S])
                        sin = cs[:, 1:2, :].broadcast_to([P, 2, S])
                        rt2 = rt.rearrange("p (a n) -> p a n", a=2)
                        dve.wait_ge(rot_done.sem, s - 1)
                        dve.tensor_tensor(rt2, ps[6][:, :].rearrange("p (a n) -> p a n", a=2), sin, ALU.mult).then_inc(rope_ready.sem, 1)
                        dve.tensor_tensor(roped, roped, cos, ALU.mult).then_inc(rope_ready.sem, 1)
                        dve.wait_ge(rope_ready.sem, (s - 1) * 2)
                        dve.tensor_tensor(roped, roped, rt2, ALU.add).then_inc(qf_ready.sem, 1)
                    if has[1] and r == 0:
                        dve.wait_ge(nrm_ready.sem, s)
                        dve.wait_ge(spread_done.sem, s - 1)
                        dve.reciprocal(rinv, nrm).then_inc(rinv_ready.sem, 1)
                    if has[last]:
                        n = s - last
                        src, part = (qf[i], pt[i]) if r == 0 else (qr[1 - i], pt[1 - i])
                        dve.wait_ge(*p1_ready(r, n + 1))
                        dve.wait_ge(*p2_ready(r, n))
                        dve.wait_ge(*p3_ready(r, n))
                        dve.tensor_tensor(res, src, part[:, 0, :], ALU.subtract).then_inc(res_ready.sem, 1)
                        dve.wait_ge(*p2_ready(r, n + 1))
                        dve.tensor_tensor(part[:, 2, :], res, part[:, 1, :], ALU.subtract).then_inc(p3_ready.sem, 1)
                    if has[1] and r == 0:
                        raw, q = qr[1 - i], qf[1 - i]
                        dve.wait_ge(spread_done.sem, s)
                        for c in range(KC):
                            dve.scalar_tensor_tensor(out=q[:, c * S:(c + 1) * S], in0=raw[:, c * S:(c + 1) * S],
                                                     scalar=gain[:, c:c + 1], in1=ps[5][:, c * S:(c + 1) * S],
                                                     op0=ALU.mult, op1=ALU.mult).then_inc(qn_ready.sem, 1)
                        dve.tensor_tensor(q[:, 512:1024], raw[:, 512:1024], ps[7][:, :], ALU.mult).then_inc(qn_ready.sem, 1)
                pipeline(dve, B, 2 - r, 2, project_step)
                barrier(dve, "dve")
                dve.memset(nm, 0.0).then_inc(nm_zero.sem, 1)
                dve.wait_ge(nm_zero.sem, r + 1)

                def group(s, g):
                    b = s - 1
                    if g == 0 and r == 0:
                        dve.wait_ge(yT_done.sem, s - 1)
                    dve.wait_ge(*oT_done(r, b * 4 + g + 1))
                    o4 = ps[6][:, 0:2 * P].rearrange("p (t j w) -> p t j w", t=TB, j=4)
                    rs3 = rs.rearrange("p (t j o) -> p t j o", t=TB, o=1)
                    dve.reciprocal(rs3, o4[:, :, :, HD:HD + 1]).then_inc(rs_ready.sem, 1)
                    dve.wait_ge(*rs_ready(r, b * 4 + g + 1))
                    if r == 0:
                        y4 = yrow.rearrange("p (t g j d) -> p t g j d", t=TB, g=4, j=4)[:, :, g, :, :]
                    else:
                        y4 = y_all.rearrange("p (b t) d -> p t b d", t=TB)[
                            :, :, (4 * g) % B:(4 * g) % B + 4, bass.ds(b * (2 * HD) + HD * (g // 2), HD)]
                    dve.tensor_tensor(y4, o4[:, :, :, 0:HD], rs3.broadcast_to([P, TB, 4, HD]), ALU.mult).then_inc(y_ready.sem, 1)

                def take_group(s, g):
                    b = s - 1
                    dve.wait_ge(*pv_done(r, b * H + 4 * g + 4))
                    dve.wait_ge(*oT_done(r, b * 4 + max(g - 1, 0)))
                    dve.tensor_copy(ot[g % 2], ps[4 + g % 2][:, 0:S]).then_inc(ot_ready.sem, 1)

                def attend_step(s, i, has):
                    if has[0]:
                        dve.wait_ge(*mT_done(r, s))
                    finish = has[1] and not (isinstance(s, int) and s == 1)
                    for h in range(H):
                        if has[0]:
                            dve.wait_ge(*s1_done(r, s * H + h + 1))
                            mx2 = mx.rearrange("p (t h) -> p t h", t=TB)[:, :, h]
                            if causal(r):
                                dve.tensor_reduce(mx[:, h:h + 1], ps[h % 2][:, 0:P], AX.X, ALU.max, negate=True)
                                ins = dve.tensor_reduce(mx[:, H + h:H + h + 1], ps[h % 2][:, S:2 * S], AX.X, ALU.max, negate=True)
                            else:
                                ins = dve.tensor_reduce(mx2, ps[h % 2][:, :].rearrange("p (t n) -> p t n", t=TB), AX.X, ALU.max, negate=True)
                            ins.then_inc(mx_ready.sem, 1)
                        if finish and h == 1:
                            group(s - 1, 3)
                        if finish and h == 8 and r == 0:
                            dve.wait_ge(op_done.sem, s - 1)
                            add_out(s - 1, x_added)
                        if has[1]:
                            if h >= 6 and (h - 6) % 4 == 0:
                                take_group(s, (h - 6) // 4)
                            if h >= 9 and (h - 9) % 4 == 0:
                                group(s, (h - 9) // 4)
                    if has[1]:
                        group(s, 2)
                        take_group(s, 3)
                    if has[0]:
                        dve.wait_ge(*nm1_ready(r, s + 1))
                        dve.tensor_tensor(rm[0:H, :], ps[7][0:H, 0:S], nm[0:H, :], ALU.subtract).then_inc(rm_ready.sem, 1)
                        dve.wait_ge(*nm2_ready(r, s + 1))
                        dve.tensor_tensor(nm[64:64 + H, :], rm[0:H, :], nm2[0:H, :], ALU.subtract).then_inc(nm_ready.sem, 1)
                def add_out(s, added):
                    b = s - 1
                    xb = X[:, bass.ds(b * TB, TB), :]
                    dve.tensor_tensor(xb, xb, ps[7][:, :].rearrange("p (t d) -> p t d", t=TB), ALU.add).then_inc(added.sem, 1)
                    dve.wait_ge(added.sem, s)
                    if r == 1:
                        dve.tensor_tensor(xb, xb, bproj[:, :].rearrange("p (a d) -> p a d", a=1).broadcast_to([P, TB, D]),
                                          ALU.add).then_inc(bias_added.sem, 1)
                        dve.wait_ge(bias_added.sem, s)
                    settle()
                    for tt in range(TB):
                        dve.bn_stats(stats[:, bass.ds(b * TB + tt, 1), :].rearrange("p a o -> p (a o)"),
                                     X[:, bass.ds(b * TB + tt, 1), :].rearrange("p a d -> p (a d)")).then_inc(stat_a.sem, 1)
                pipeline(dve, B, 1, 3, attend_step)
                group(B, 3)
                if r == 0:
                    dve.wait_ge(op_done.sem, B)
                    add_out(B, x_added)
                if r == 1:
                    def output_step(s, i, has):
                        if has[1]:
                            dve.wait_ge(op1_done.sem, s)
                            add_out(s, x1_added)
                    barrier(dve, "dve")
                    pipeline(dve, B, 1, 2, output_step)
                barrier(dve, "dve")
                dve.wait_ge(*stat_a(r, 2 * B))
                for i in range(NT):
                    dve.bn_aggr(mv[:, i, :], stats[:, i, :]).then_inc(stat_done.sem, 1)
                stat_at += NT
                dve.wait_ge(stat_done.sem, stat_at)
                make_rstd(r, 2)

                dve.memset(cum, 0.0).then_inc(cum0.sem, 1)
                dve.memset(one64, 1.0).then_inc(cum0.sem, 1)
                dve.wait_ge(cum0.sem, 2 * r + 2)
                CH = 11

                def route_step(s, i, has):
                    if has[0]:
                        dve.wait_ge(*rT_done(r, s))
                        dve.wait_ge(*rcopy_done(r, s * 2))
                        normalise(s, rn_ready)
                    if has[1]:
                        b, c0 = s - 1, (s - 1) * CH + r * (CH * B)
                        lg = ps[1 + (1 - i)][:, 0:2 * E].rearrange("p (t e) -> p t e", t=TB)
                        lb2 = lb.rearrange("p (t e) -> p t e", t=TB)
                        ohb = oh[:, bass.ds(b * TB, TB), :, :].rearrange("p t k e -> p (t k) e")
                        pr = prod[:, 0:TB * K * E]
                        dve.wait_ge(*lg_done(r, s))
                        dve.tensor_tensor(lb2, lg, rb[:, :].rearrange("p (a e) -> p a e", a=1).broadcast_to([P, TB, E]),
                                          ALU.add).then_inc(topk.sem, 1)
                        dve.tensor_reduce(nmx, lg, AX.X, ALU.max, negate=True).then_inc(nmx_ready.sem, 1)
                        dve.wait_ge(topk.sem, c0 + 1)
                        settle()
                        for tt in range(TB):
                            dve.max(m8[:, 8 * tt:8 * tt + 8], lb[:, tt * E:(tt + 1) * E]).then_inc(topk.sem, 1)
                        dve.wait_ge(topk.sem, c0 + 3)
                        settle()
                        for tt in range(TB):
                            dve.max_index(i8[:, 8 * tt:8 * tt + 8], m8[:, 8 * tt:8 * tt + 8], lb[:, tt * E:(tt + 1) * E]).then_inc(topk.sem, 1)
                        dve.wait_ge(topk.sem, c0 + 5)
                        dve.tensor_copy(idxf.rearrange("p (t k) -> p t k", t=TB),
                                        i8.rearrange("p (t k) -> p t k", t=TB)[:, :, 0:K]).then_inc(topk.sem, 1)
                        dve.wait_ge(topk.sem, c0 + 6)
                        dve.tensor_tensor(ohb, iot[:, :].rearrange("p (a e) -> p a e", a=1).broadcast_to([P, TB * K, E]),
                                          idxf.rearrange("p (a o) -> p a o", o=1).broadcast_to([P, TB * K, E]),
                                          ALU.is_equal).then_inc(topk.sem, 1)
                        dve.wait_ge(topk.sem, c0 + 7)
                        settle()
                        with nc.allow_low_precision("counts up to 4 are exact in bf16"):
                            dve.tensor_reduce(msk.rearrange("p (t e) -> p t e", t=TB),
                                              oh[:, bass.ds(b * TB, TB), :, :].rearrange("p t k e -> p t e k"),
                                              AX.X, ALU.add).then_inc(msk_ready.sem, 1)
                        dve.wait_ge(*ex_ready(r, s))
                        for tt in range(TB):
                            prt = pr[:, tt * K * E:(tt + 1) * K * E].rearrange("p (k e) -> p k e", k=K)
                            ins = dve.tensor_tensor(prt, ohb[:, tt * K:(tt + 1) * K, :],
                                                    ex[:, tt * E:(tt + 1) * E].rearrange("p (a e) -> p a e", a=1).broadcast_to([P, K, E]),
                                                    ALU.mult)
                        ins.then_inc(topk.sem, 1)
                        dve.wait_ge(topk.sem, c0 + 8)
                        dve.tensor_reduce(gk, pr.rearrange("p (a e) -> p a e", e=E), AX.X, ALU.add).then_inc(topk.sem, 1)
                        dve.wait_ge(topk.sem, c0 + 9)
                        dve.tensor_reduce(gs, gk.rearrange("p (t k) -> p t k", t=TB), AX.X, ALU.add).then_inc(topk.sem, 1)
                        dve.wait_ge(topk.sem, c0 + 10)
                        dve.reciprocal(gr, gs).then_inc(topk.sem, 1)
                        dve.wait_ge(topk.sem, c0 + 11)
                        dve.tensor_tensor(comb[:, bass.ds(b * TB, TB), :], gk.rearrange("p (t k) -> p t k", t=TB),
                                          gr.rearrange("p (t o) -> p t o", o=1).broadcast_to([P, TB, K]), ALU.mult)
                        dve.wait_ge(*rank_done(r, s))
                        dve.tensor_tensor(cum, cum, msk[:, 0:E], ALU.add).then_inc(cum_half.sem, 1)
                        dve.wait_ge(*cum_half(r, s))
                        dve.tensor_tensor(cum, cum, msk[:, E:2 * E], ALU.add).then_inc(cum_ready.sem, 1)
                pipeline(dve, B, 1, 2, route_step)

                d = [0]

                def link(ins):
                    d[0] += 1
                    ins.then_inc(disp.sem, 1)
                    dve.wait_ge(disp.sem, disp_base[0] + d[0])
                dve.wait_ge(*cnt_done(r, 1))
                link(dve.tensor_scalar(cnt_i, ps[4][:, 0:E], float(P - 1), None, ALU.add))
                link(dve.tensor_single_scalar(cnt_i, cnt_i, 7, ALU.arith_shift_right))
                link(dve.tensor_copy(ntf, cnt_i))
                link(dve.tensor_tensor_scan(incl, one64, ntf, 0.0, ALU.mult, ALU.add))
                link(dve.tensor_tensor(base, incl, ntf, ALU.subtract))
                link(dve.tensor_scalar(base, base, float(P), None, ALU.mult))
                dve.wait_ge(*rank_out(r, B))
                sm = slotmap.rearrange("p (i e) -> p i e", i=NT)
                link(dve.tensor_tensor(sm, rank[:, :, :], base.rearrange("p (a e) -> p a e", a=1).broadcast_to([P, NT, E]), ALU.add))
                for q in range(4):
                    for i in range(4):
                        ii = 4 * q + i
                        ins = dve.tensor_tensor(prod[:, i * 256:(i + 1) * 256].rearrange("p (k e) -> p k e", k=K), oh[:, ii, :, :],
                                                sm[:, ii:ii + 1, :].broadcast_to([P, K, E]), ALU.mult)
                    link(ins)
                    link(dve.tensor_reduce(slotf, prod.rearrange("p (a e) -> p a e", e=E), AX.X, ALU.add))
                    dve.tensor_copy(slot[:, 4 * q:4 * q + 4, :].rearrange("p i k -> p (i k)"), slotf).then_inc(slot_ready.sem, 1)
                    dve.wait_ge(*slot_ready(r, q + 1))
                link(dve.tensor_scalar(cmp, incl, jcol[:, 0:1], None, ALU.is_le))
                link(dve.tensor_reduce(tef, cmp, AX.X, ALU.add))
                dve.tensor_scalar(tef, tef, float(E - 1), None, ALU.min).then_inc(tef_ready.sem, 1)
                dve.wait_ge(*teT_done(r, 1))
                dve.tensor_copy(te[:, :], ps[5][0:1, 0:P]).then_inc(te_ready.sem, 1)
                disp_base[0] += d[0]
                barrier(dve, "dve")

                def shared_step(s, i, has):
                    if has[0]:
                        for half in range(2):
                            lo, hi = half * 512, (half + 1) * 512
                            dve.wait_ge(*sth_ready(r, s * 2 + half + 1))
                            dve.scalar_tensor_tensor(out=sga[:, lo:hi], in0=sth[:, lo:hi], scalar=1.0, in1=ps[half][:, :],
                                                     op0=ALU.add, op1=ALU.mult).then_inc(sga_ready.sem, 1)
                            dve.wait_ge(*sga_ready(r, s * 2 + half + 1))
                            if half == 0:
                                dve.wait_ge(*sd_done(r, s - 1 if not isinstance(s, int) or s else 0))
                            dve.scalar_tensor_tensor(out=sg[i][:, 2 * half:2 * half + 2, :].rearrange("p c n -> p (c n)"),
                                                     in0=sga[:, lo:hi], scalar=0.5, in1=ps[2 + half][:, :],
                                                     op0=ALU.mult, op1=ALU.mult).then_inc(sg_ready.sem, 1)
                    if has[1]:
                        dve.wait_ge(*sd_done(r, s))
                        xb = X[:, bass.ds((s - 1) * TB, TB), :]
                        dve.tensor_tensor(xb, xb, ps[4][:, :].rearrange("p (t d) -> p t d", t=TB), ALU.add).then_inc(sx_added.sem, 1)
                pipeline(dve, B, 1, 2, shared_step)
                barrier(dve, "dve")

                def expert_step(s, i, has):
                    if has[1]:
                        j, i1 = s - 1, (i - 1) % ERING
                        dve.wait_ge(*eth_ready(r, j + 1))
                        dve.scalar_tensor_tensor(out=eg[i1 % 2], in0=eth[i1 % 2], scalar=1.0, in1=ps[2 + i1 % 2][:, 0:FF],
                                                 op0=ALU.add, op1=ALU.mult).then_inc(eg_ready.sem, 1)
                        dve.wait_ge(*eg_ready(r, j + 1))
                        dve.wait_ge(*hT_done(r, j - 3 if not isinstance(j, int) or j > 3 else 0))
                        dve.scalar_tensor_tensor(out=eh[i1 % 4].rearrange("p (a f) -> p a f", a=2),
                                                 in0=eg[i1 % 2].rearrange("p (a f) -> p a f", a=1).broadcast_to([P, 2, FF]), scalar=0.5,
                                                 in1=ps[2 + i1 % 2][:, FF:2 * FF].rearrange("p (a f) -> p a f", a=1).broadcast_to([P, 2, FF]),
                                                 op0=ALU.mult, op1=ALU.mult).then_inc(eh_ready.sem, 1)
                    if has[3]:
                        j, i3 = s - 3, (i - 3) % ERING
                        dve.wait_ge(*hT_done(r, j + 1))
                        dve.wait_ge(*ed_done(r, j - 1 if not isinstance(j, int) or j else 0))
                        dve.tensor_copy(eht[i3 % 2], ps[4][:, 0:P]).then_inc(eht_ready.sem, 1)
                    if has[4]:
                        j, i4 = s - 4, (i - 4) % ERING
                        dve.wait_ge(*ed_done(r, j + 1))
                        dve.wait_ge(*y_out[i4 // 2](r, stored_count(j, i4)))
                        dve.tensor_copy(ypair[i4 // 2][:, i4 % 2, P:D], down_bank(i4, 1)[:, 0:P]).then_inc(yv_ready.sem, 1)
                pipeline(dve, NTILE, 4, ERING, expert_step)

                for i in range(NT):
                    for k in range(K):
                        n = i * K + k
                        dve.wait_ge(*g_in[n % GRING](r, 16 * (n // GRING + 1)))
                        if k:
                            dve.wait_ge(*g_used(r, n))
                        dve.scalar_tensor_tensor(out=X[:, i, :], in0=gring[n % GRING], scalar=comb[:, i, k:k + 1],
                                                 in1=X[:, i, :], op0=ALU.mult, op1=ALU.add).then_inc(g_used.sem, 1)
                    dve.wait_ge(*g_used(r, i * K + K))
                    dve.bn_stats(stats[:, i % 2, :], X[:, i, :]).then_inc(stat_done.sem, 1)
                    stat_at += 1
                    dve.wait_ge(stat_done.sem, stat_at)
                    dve.bn_aggr(mv[:, i, :], stats[:, i % 2, :]).then_inc(tile_final.sem, 1)
                dve.drain()


EVEN_FIRST = list(range(0, H, 2)) + list(range(1, H, 2))


def constants():
    eye = np.eye(P, dtype=np.float32)
    cload = np.zeros((P, 2048 + 5 * P), np.float32)
    sel = cload[:, 0:2048].reshape(P, H, P)
    for part in range(3):
        for h in range(H):
            sel[32 * part + h, h, :] = 1.0
    row, col = np.arange(P)[:, None], np.arange(P)[None, :]
    for i, m in enumerate((eye, np.where(col > row, -1e30, 0.0), np.where(row > col, -1e30, 0.0), row < col, np.ones((P, P)))):
        cload[:, 2048 + i * P:2048 + (i + 1) * P] = m
    half = HD // 2
    rotm = np.zeros((P, P), np.float32)
    for m in range(P):
        rotm[m + half if m % HD < half else m - half, m] = -1.0 if m % HD < half else 1.0
    inv = np.float32(10000.0) ** (-np.arange(half, dtype=np.float32) / np.float32(half))
    theta = (np.arange(S, dtype=np.float32)[:, None] * inv[None, :]).astype(np.float32)
    cs = np.stack([np.cos(theta), np.sin(theta)]).astype(np.float32)
    cs = np.ascontiguousarray(cs[:, :, np.arange(P) % half].transpose(2, 0, 1))
    headsum = np.zeros((P, 32), np.float32)
    headsum[np.arange(P), np.arange(P) // HD] = 1.0
    headsel = np.zeros((P, 2 * KC, P), np.float32)
    for c in range(2 * KC):
        headsel[32 * c + np.arange(P) // HD, c, np.arange(P)] = 1.0
    return dict(cload=cload, ident=eye, rotm=rotm, cs=cs, headsum=headsum, headsel=headsel,
                iot=np.tile(np.arange(E, dtype=np.float32), (P, 1)), jcol=np.arange(P, dtype=np.float32)[:, None])


def chunked(w):
    return w.reshape(-1, P, w.shape[1]).transpose(1, 0, 2)


def layout(v):
    g = {k: np.asarray(a) for k, a in v.items()}
    a = dict(constants())
    a["x"] = g["L0_attn_a_x"]
    w = g["L0_attn_a_w_qkv"].reshape(D, 3, H, HD)[:, :, EVEN_FIRST, :].reshape(D, 3 * D)
    a["wqk0"], a["wv0"] = chunked(w[:, :2 * D]), chunked(w[:, 2 * D:])
    a["wo0"] = chunked(g["L0_attn_a_w_out"].reshape(H, HD, D)[EVEN_FIRST].reshape(D, D))
    a["gain"] = np.repeat(g["L0_attn_a_q_gain"][EVEN_FIRST], HD).reshape(KC, P).T
    w = g["L0_attn_b_Wqkv"].reshape(H, 3, HD, D).transpose(3, 1, 0, 2).reshape(D, 3 * D)
    a["wqk1"], a["wv1"] = chunked(w[:, :2 * D]), chunked(w[:, 2 * D:])
    a["wo1"] = chunked(g["L0_attn_b_Wproj"].T)
    a["bproj"] = np.tile(g["L0_attn_b_bproj"], (P, 1))
    a["rw"], a["rb"] = chunked(g["L0_ffn_router_w"]), np.tile(g["L0_ffn_router_bias"], (P, 1))
    a["swg"] = chunked(g["L0_ffn_swg"].transpose(1, 0, 2).reshape(D, SH))
    a["swu"] = chunked(g["L0_ffn_swu"].transpose(1, 0, 2).reshape(D, SH))
    a["swd"] = chunked(g["L0_ffn_swd"].reshape(SH, D))
    gu = np.concatenate([g["L0_ffn_wg"], g["L0_ffn_wu"]], axis=2).reshape(E, KC, P, 2 * FF).transpose(0, 2, 1, 3).reshape(E, P, 4 * FF)
    wd = g["L0_ffn_wd"].reshape(E, FF, 2, P).transpose(0, 2, 1, 3).reshape(E, P, P)
    a["we"] = np.concatenate([gu, wd], axis=2)
    return {k: np.ascontiguousarray(x) for k, x in a.items()}


def kernel(**inputs):
    import concourse.bacc as bacc
    from concourse.bass_utils import run_bass_kernel_spmd

    nc = bacc.Bacc("TRN2", target_bir_lowering=False, num_devices=1)
    arrays = {f"in_{k}": a for k, a in layout(inputs).items()}
    t = {k[3:]: nc.dram_tensor(k, a.shape, F32, kind="ExternalInput").ap() for k, a in arrays.items()}
    t["out"] = nc.dram_tensor("out", (B, S, D), F32, kind="ExternalOutput").ap()
    t["parts"] = nc.dram_tensor("parts", (B, 3, 2 * D, S), BF16, kind="Internal").ap()
    t["xd"] = nc.dram_tensor("xd", (SLOTS, D), F32, kind="Internal").ap()
    t["yd"] = nc.dram_tensor("yd", (SLOTS, D), F32, kind="Internal").ap()
    build(nc, t)
    r = run_bass_kernel_spmd(nc, [arrays], core_ids=[0])
    return r.results[0]["out"]
```

```python
from contextlib import ExitStack

import numpy as np
import concourse.bass as bass
from concourse import mybir

F32 = mybir.dt.float32
BF16 = mybir.dt.bfloat16
I32 = mybir.dt.int32
U32 = mybir.dt.uint32
ALU = mybir.AluOpType
ACT = mybir.ActivationFunctionType
AX = mybir.AxisListType

P = 128
B, S, D = 8, 256, 256
NT = B * S // P
TB = S // P
KC = D // P
H, HD = 16, 16
VW = 32
E, FF, K = 64, 64, 4
SH = 512
SC = SH // P
TERMS = [(0, 0), (0, 1), (1, 0), (1, 1), (0, 2), (2, 0)]
KR = len(TERMS) * HD
NTILE = B * S * K // P + E
SLOTS = NTILE * P
EPS_LN, EPS_UNIT = 1e-5, 1e-6
GRING, ERING = 2 * TB * K, 8


class Signal:

    def __init__(self, sem, per_run):
        self.sem, self.per_run = sem, per_run

    def __call__(self, run, count):
        value = count + run * self.per_run
        return self.sem, (max(value, 0) if isinstance(value, int) else value)


def pipeline(eng, items, depth, unroll, step):
    first = 2 * depth
    loops = (items - first) // unroll
    flags = lambda s: [0 <= s - d < items for d in range(depth + 1)]
    for s in range(first):
        step(s, s % unroll, flags(s))
    with eng.Fori(0, loops) as i:
        for j in range(unroll):
            step(i * unroll + (first + j), (first + j) % unroll, [True] * (depth + 1))
    for s in range(first + loops * unroll, items + depth):
        step(s, s % unroll, flags(s))


def build(nc, t):
    with ExitStack() as ctx:
        def sb(name, shape, dt=F32):
            return ctx.enter_context(nc.sbuf_tensor(name, shape, dt))

        def signal(name, per_run=0):
            return Signal(ctx.enter_context(nc.semaphore(name)), per_run)

        X = sb("X", [P, NT, D])
        stats = sb("stats", [P, NT, 6])
        mv = sb("mv", [P, NT, 2])
        ve = sb("ve", [P, NT])
        rstd = sb("rstd", [P, NT])
        bstats = sb("bstats", [P, TB, 6])
        bmv = sb("bmv", [P, TB, 2])
        bve = sb("bve", [P, TB])
        brstd = sb("brstd", [P, TB])
        mhalf = sb("mhalf", [P, NT])
        xn = sb("xn", [P, TB, D])
        xt = sb("xt", [P, KC, S])
        ident = sb("ident", [P, P])
        cb = sb("cb", [P, 2048 + 5 * P], BF16)
        esel = cb[:, 0:2048].rearrange("p (h k) -> p h k", h=H)
        identb, mask_s, mask_t, ltri, onesb = (cb[:, 2048 + i * P:2048 + (i + 1) * P] for i in range(5))
        rotm = sb("rotm", [P, P])
        headsum = sb("headsum", [P, 32])
        headsel = sb("headsel", [P, 2 * KC, P])
        cs = sb("cs", [P, 2, S])
        gain = sb("gain", [P, KC])
        wqk = [sb(f"wqk{r}", [P, KC, 2 * D]) for r in range(2)]
        wv = [sb(f"wv{r}", [P, KC, D]) for r in range(2)]
        wo = [sb(f"wo{r}", [P, KC, D]) for r in range(2)]
        bproj = sb("bproj", [P, D])
        rw = sb("rw", [P, KC, E])
        rb = sb("rb", [P, E])
        iot = sb("iot", [P, E])
        jcol = sb("jcol", [P, 1])
        swg = sb("swg", [P, KC, SH])
        swu = sb("swu", [P, KC, SH])
        swd = sb("swd", [P, SC, D])
        oh = sb("oh", [P, NT, K, E], BF16)
        rank = sb("rank", [P, NT, E])
        comb = sb("comb", [P, NT, K])
        slot = sb("slot", [P, NT, K], I32)
        te = sb("te", [1, P], I32)

        big = sb("big", [P, 2 * NT * D])
        v_all = big[:, 0:NT * D].rearrange("p (i h d) -> p i h d", i=NT, h=H)
        xn_all = big[:, 0:NT * D].rearrange("p (i d) -> p i d", i=NT)
        xnt_all = big[:, NT * D:].rearrange("p (c n) -> p c n", c=KC)
        y_all = big[:, NT * D:].rearrange("p (i d) -> p i d", i=NT)
        arena = sb("arena", [P, 12288])
        qs = [arena[:, 4096 * i:4096 * i + 2048].bitcast(BF16).rearrange("p (h n) -> p h n", h=H) for i in range(3)]
        ks = [arena[:, 4096 * i + 2048:4096 * i + 4096].bitcast(BF16).rearrange("p (h n) -> p h n", h=H) for i in range(3)]
        cload = arena[:, 0:2048 + 5 * P]
        wring = [arena[:, 384 * i:384 * i + 384] for i in range(ERING)]
        xpair = [arena[:, 3072 + 512 * i:3584 + 512 * i].rearrange("p (t d) -> p t d", t=2) for i in range(ERING // 2)]
        ypair = [arena[:, 5120 + 512 * i:5632 + 512 * i].rearrange("p (t d) -> p t d", t=2) for i in range(ERING // 2)]
        sth = arena[:, 7680:8704]
        sga = arena[:, 8704:9728]
        sg = [arena[:, 9728 + 1024 * i:10752 + 1024 * i].rearrange("p (c n) -> p c n", c=SC) for i in range(2)]
        gring = [big[:, NT * D + D * i:NT * D + D * (i + 1)] for i in range(GRING)]
        tmp = sb("tmp", [P, 8192])
        qr = [tmp[:, 0:1024], tmp[:, 1024:2048]]
        sq = tmp[:, 2048:3072]
        nrm = tmp[:, 3072:3328]
        rinv = tmp[:, 3328:3584]
        qf = [tmp[:, 3584:4608], tmp[:, 4608:5632]]
        res = tmp[:, 5632:6656]
        rt = tmp[:, 6656:7168]
        pt = [arena[:, 8192 + 1536 * i:9728 + 1536 * i].bitcast(BF16).rearrange("p (s n) -> p s n", s=3) for i in range(2)]
        prob = [tmp[:, 512 * i:512 * i + 512] for i in range(4)]
        vb = [tmp[:, 2048 + 1024 * i:3072 + 1024 * i].rearrange("p (t h w) -> p t h w", t=TB, h=H) for i in range(3)]
        ot = [tmp[:, 5120 + 256 * i:5376 + 256 * i] for i in range(2)]
        yrow = tmp[:, 5632:6144]
        yt = tmp[:, 6144:6656]
        ybuf = [arena[:, 512 * i:512 * i + 512] for i in range(2)]
        ytb = [arena[:, 1024 + 512 * i:1536 + 512 * i] for i in range(2)]
        mx = tmp[:, 6656:6688]
        rs = tmp[:, 6688:6696]
        rm = tmp[:, 6720:6976]
        nm = [tmp[:, 7168:7296].bitcast(BF16), tmp[:, 7424:7552].bitcast(BF16)]
        nm2 = tmp[:, 7296:7424].bitcast(BF16)
        lb = tmp[:, 0:128]
        nmx = tmp[:, 128:130]
        m8 = tmp[:, 144:160]
        i8 = tmp[:, 160:176].bitcast(U32)
        idxf = tmp[:, 176:184]
        gk = tmp[:, 184:192]
        gs = tmp[:, 192:194]
        gr = tmp[:, 194:196]
        ex = tmp[:, 2304:2304 + NT * E].rearrange("p (i e) -> p i e", i=NT)
        prod = tmp[:, 512:1536]
        msk = [tmp[:, 1536:1600].bitcast(BF16), tmp[:, 256:320].bitcast(BF16)]
        cum = [tmp[:, 1600:1632].bitcast(BF16), tmp[:, 320:352].bitcast(BF16)]
        cumh = tmp[:, 352:384].bitcast(BF16)
        cnt_i = tmp[:, 1664:1728].bitcast(I32)
        ntf = tmp[:, 1728:1792]
        incl = tmp[:, 1792:1856]
        base = tmp[:, 1856:1920]
        one64 = tmp[:, 1920:1984]
        cmp = tmp[:, 1984:2048]
        tef = tmp[:, 2048:2049]
        slotf = tmp[:, 2052:2068]
        slotmap = tmp[:, 4096:5120]
        xdt = [tmp[:, 5120 + 256 * i:5376 + 256 * i].rearrange("p (c n) -> p c n", c=KC) for i in range(2)]
        eth = [tmp[:, 5632 + 64 * i:5696 + 64 * i] for i in range(2)]
        eg = [tmp[:, 5760 + 64 * i:5824 + 64 * i] for i in range(2)]
        eh = [tmp[:, 5888 + 128 * i:6016 + 128 * i] for i in range(4)]
        eht = [tmp[:, 6400 + 128 * i:6528 + 128 * i] for i in range(2)]
        zero = sb("zero", [P, D])

        ps = [ctx.enter_context(nc.psum_tensor(f"ps{i}", [P, 512], F32)) for i in range(8)]

        cload_in = signal("cload_in")
        consts_in, later_in, x_in = signal("consts_in"), signal("later_in"), [signal(f"x_in{q}") for q in range(4)]
        cast_done, setup_done = signal("cast_done"), signal("setup_done")
        phase_end = signal("phase_end")
        stat_done = signal("stat_done")
        ve_ready, rstd_ready = signal("ve_ready", 2), signal("rstd_ready", 4)
        xn_ready, xT_done, xt_ready = signal("xn_ready", 16), signal("xT_done", 8), signal("xt_ready", 8)
        qk_done, qk_raw = signal("qk_done", 16), signal("qk_raw", 16)
        v_done, v_out = signal("v_done", 8), signal("v_out", 8)
        sq_ready, ss_done, nrm_ready = signal("sq_ready"), signal("ss_done"), signal("nrm_ready")
        rinv_ready, spread_done, qn_ready, rot_done = signal("rinv_ready"), signal("spread_done"), signal("qn_ready"), signal("rot_done")
        rope_ready, qf_ready = signal("rope_ready"), signal("qf_ready")
        p1_ready, res_ready, p2_ready, p3_ready = (signal(n, 8) for n in ("p1_ready", "res_ready", "p2_ready", "p3_ready"))
        parts_stored = [signal(f"parts_stored{i}", 16 * B // 2) for i in range(2)]
        stack_in = [signal(f"stack_in{i}", 16 * len(TERMS) * 2 * (3 if i < 2 else 2)) for i in range(3)]
        vb_ready, vpad = signal("vb_ready", 8), signal("vpad", 1)
        s1_done, mx_ready, mT_done = signal("s1_done", 128), signal("mx_ready", 128), signal("mT_done", 16)
        nm3_ready = signal("nm3_ready", 16)
        nm1_ready, rm_ready, nm2_ready, nm_ready = (signal(n, 16) for n in ("nm1_ready", "rm_ready", "nm2_ready", "nm_ready"))
        s2_done, exp_ready, pv_done = signal("s2_done", 128), signal("exp_ready", 128), signal("pv_done", 128)
        ot_ready, oT_done, rs_ready, y_ready = (signal(n, 32) for n in ("ot_ready", "oT_done", "rs_ready", "y_ready"))
        yT_done, yt_ready, op_done, x_added = (signal(n) for n in ("yT_done", "yt_ready", "op_done", "x_added"))
        rn_ready, rT_done, rt_ready, rcopy_done = signal("rn_ready", 16), signal("rT_done", 8), signal("rt_ready", 8), signal("rcopy_done", 8)
        lg_read = signal("lg_read", 8)
        xnt_ready, gate = signal("xnt_ready", 8), signal("gate", 4 * B)
        lg_done, nmx_ready, ex_ready = signal("lg_done", 8), signal("nmx_ready", 8), signal("ex_ready", 8)
        topk = signal("topk")
        msk_ready, rank_done, rank_out = signal("msk_ready", 8), signal("rank_done", 8), signal("rank_out", 8)
        cum_ready, cnt_done = signal("cum_ready", 8), signal("cnt_done", 1)
        slot_ready, tef_ready, teT_done, te_ready = signal("slot_ready", 4), signal("tef_ready", 1), signal("teT_done", 1), signal("te_ready", 1)
        zeroed, scattered = signal("zeroed"), signal("scattered", 16 * NT * K)
        gu_done, sth_ready, sga_ready, sg_ready = signal("gu_done", 16), signal("sth_ready", 16), signal("sga_ready", 16), signal("sg_ready", 16)
        sd_done, sx_added = signal("sd_done", 8), signal("sx_added", 8)
        w_in = [signal(f"w_in{i}", 16 * NTILE // ERING) for i in range(ERING)]
        xd_in = [signal(f"xd_in{i}", 16 * NTILE // ERING) for i in range(ERING // 2)]
        y_out = [signal(f"y_out{i}", 16 * NTILE // ERING) for i in range(ERING // 2)]
        eT_done, ext_ready, egu_done, eth_ready = (signal(n, NTILE) for n in ("eT_done", "ext_ready", "egu_done", "eth_ready"))
        eg_ready, eh_ready, hT_done, eht_ready = (signal(n, NTILE) for n in ("eg_ready", "eh_ready", "hT_done", "eht_ready"))
        ed_done, ya_ready, yv_ready = (signal(n, NTILE) for n in ("ed_done", "ya_ready", "yv_ready"))
        g_in = [signal(f"g_in{i}", 16 * NT * K // GRING) for i in range(GRING)]
        g_used = signal("g_used", NT * K)
        bstat_done, baggr_done = signal("bstat_done"), signal("baggr_done")
        bve_ready, brstd_ready, stored = signal("bve_ready"), signal("brstd_ready"), signal("stored")

        FIRST = ("ident", "rotm", "headsum", "headsel", "cs", "gain", "wqk0", "wv0")
        CONSTS = [(cload, "cload"), (ident[:, :], "ident"), (rotm[:, :], "rotm"), (headsum[:, :], "headsum"), (headsel[:, :, :], "headsel"),
                  (cs[:, :, :], "cs"), (gain[:, :], "gain"), (bproj[:, :], "bproj"), (rw[:, :, :], "rw"),
                  (rb[:, :], "rb"), (iot[:, :], "iot"), (jcol[:, :], "jcol"), (swg[:, :, :], "swg"),
                  (swu[:, :, :], "swu"), (swd[:, :, :], "swd")]
        for r in range(2):
            CONSTS += [(wqk[r][:, :, :], f"wqk{r}"), (wv[r][:, :, :], f"wv{r}"), (wo[r][:, :, :], f"wo{r}")]
        x_tiles = t["x"].rearrange("b (t p) d -> p (b t) d", p=P)
        out_tiles = t["out"].rearrange("b (t p) d -> p (b t) d", p=P)
        parts = t["parts"]
        xd, yd = t["xd"], t["yd"]

        epsu = sb("epsu", [P, 1])[:, :]
        nm_zero, bias_added, stat_a = signal("nm_zero"), signal("bias_added"), signal("stat_a", 2 * B)
        yb_ready, yT1_done, yt1_ready, op1_done, x1_added = (signal(n) for n in ("yb_ready", "yT1_done", "yt1_ready", "op1_done", "x1_added"))
        stat_b, settled = signal("stat_b"), signal("settled")
        cum0, cum_half, disp = signal("cum0"), signal("cum_half", 8), signal("disp")
        disp_base = [0]

        block = ctx.enter_context(nc.Block())

        barriers = {}

        def barrier(e, name):
            barriers[name] = barriers.get(name, 0) + 1
            e.drain().then_inc(phase_end.sem, 1)
            e.wait_ge(phase_end.sem, 3 * barriers[name])

        def stored_count(j, i):
            return 16 * max(j // ERING, 0) if isinstance(j, int) else (j - i) * (16 // ERING)

        def down_bank(i, half):
            return ps[((5, 6), (7, 1))[i % 2][half]]

        def causal(r):
            return r == 0

        @block.sync
        def _(sp):
            for q in range(4):
                sp.dma_start(X[:, q * NT // 4:(q + 1) * NT // 4, :], x_tiles[:, q * NT // 4:(q + 1) * NT // 4, :]).then_inc(x_in[q].sem, 16)
            for dst, name in CONSTS:
                if name in FIRST:
                    sp.dma_start(dst, t[name]).then_inc(consts_in.sem, 16)
            def clear_tiles(b):
                n = NTILE // B
                sp.dma_start(xd.rearrange("(p a) d -> p a d", a=NTILE)[:, bass.ds(b * n, n), :],
                             zero[:, :].rearrange("p (a d) -> p a d", a=1).broadcast_to([P, n, D])).then_inc(zeroed.sem, 16)
            sp.wait_ge(setup_done.sem, 1)

            for r in range(2):
                def store_parts(b, j):
                    sp.wait_ge(*p3_ready(r, b + 1))
                    sp.dma_start(parts[bass.ds(b, 1)].rearrange("a s (c p) n -> p (a s) c n", p=P),
                                 pt[j].rearrange("p s (c n) -> p s c n", c=4)).then_inc(parts_stored[j].sem, 16)

                def load_stack(b, i):
                    for side, dst in ((0, qs[i]), (1, ks[i])):
                        for n, term in enumerate(TERMS):
                            src = parts[bass.ds(b, 1), term[side], side * D:(side + 1) * D, :].rearrange(
                                "a (h d) n -> d (a h) n", d=HD)
                            sp.dma_start(dst[HD * n:HD * n + HD, :, :], src).then_inc(stack_in[i].sem, 16)

                store_parts(0, 0)
                store_parts(1, 1)
                sp.wait_ge(cast_done.sem, 1)
                for b in range(2):
                    sp.wait_ge(*parts_stored[b](r, 16))
                    load_stack(b, b)
                with sp.Fori(0, B // 2 - 1) as it:
                    for j in range(2):
                        store_parts(it * 2 + (2 + j), j)
                for i in range(2):
                    sp.wait_ge(*parts_stored[i](r, 16 * B // 2))
                with sp.Fori(0, 2) as it:
                    for j in range(3):
                        b = it * 3 + (2 + j)
                        sp.wait_ge(*s2_done(r, (b - 2) * H + 1))
                        load_stack(b, (2 + j) % 3)
                        if r == 0:
                            clear_tiles(b)

                if r == 0:
                    clear_tiles(0)
                    clear_tiles(1)

                def load_weights(j, i):
                    ev = sp.value_load(te[0:1, bass.ds(j, 1)], min_val=0, max_val=E - 1)
                    sp.dma_start(wring[i], t["we"][bass.ds(ev, 1)].rearrange("a p n -> p (a n)")).then_inc(w_in[i].sem, 16)
                sp.wait_ge(*te_ready(r, 1))
                for j in range(ERING):
                    load_weights(j, j)
                with sp.Fori(0, NTILE // ERING - 1) as it:
                    for i in range(ERING):
                        j = it * ERING + (ERING + i)
                        sp.wait_ge(*ed_done(r, j - (ERING - 1)))
                        load_weights(j, i)
            for i in range(0, NT, TB):
                sp.wait_ge(*g_used(1, (i + TB) * K))
                sp.dma_start(out_tiles[:, i:i + TB, :], X[:, i:i + TB, :]).then_inc(stored.sem, 16)
            sp.wait_ge(stored.sem, 16 * NT // TB)

        @block.gpsimd
        def _(pool):
            pool.memset(mhalf[:, :], -0.5).then_inc(vpad.sem, 1)
            pool.wait_ge(vpad.sem, 1)

            def rsqrt_variance(run, n):
                pool.wait_ge(*ve_ready(run, n))
                for tiles in (slice(0, TB), slice(TB, NT)):
                    pool.tensor_tensor(rstd[:, tiles], ve[:, tiles], mhalf[:, tiles], ALU.pow).then_inc(rstd_ready.sem, 1)

            for r in range(2):
                if r == 0:
                    rsqrt_variance(r, 1)
                    pool.wait_ge(cload_in.sem, 16)
                    pool.tensor_copy(cb[:, :], cload).then_inc(cast_done.sem, 1)
                pool.wait_ge(*v_out(r, 8))
                pool.wait_ge(*p3_ready(r, B))
                for i in range(3):
                    pool.memset(vb[i][:, :, :, HD:HD + 1], 1.0)
                    pool.memset(vb[i][:, :, :, HD + 1:VW], 0.0).then_inc(vpad.sem, 1)
                pool.wait_ge(vpad.sem, 1 + 3 * (r + 1))

                def copy_v(b, i):
                    pool.tensor_copy(vb[i][:, :, :, 0:HD], v_all[:, bass.ds(b * TB, TB), :, :]).then_inc(vb_ready.sem, 1)

                copy_v(0, 0)
                copy_v(1, 1)
                with pool.Fori(0, 2) as it:
                    for j in range(3):
                        b = it * 3 + (2 + j)
                        pool.wait_ge(*pv_done(r, (b - 2) * H + 1))
                        copy_v(b, (2 + j) % 3)

                if r == 1:
                    pool.wait_ge(*y_ready(r, 32))
                    for b in range(2):
                        pool.tensor_copy(ybuf[b].rearrange("p (t d) -> p t d", t=TB), y_all[:, b * TB:b * TB + TB, :]).then_inc(yb_ready.sem, 1)
                    with pool.Fori(0, (B - 2) // 2) as it:
                        for j in range(2):
                            b = it * 2 + (2 + j)
                            pool.wait_ge(yT1_done.sem, b - 1)
                            pool.tensor_copy(ybuf[j].rearrange("p (t d) -> p t d", t=TB), y_all[:, bass.ds(b * TB, TB), :]).then_inc(yb_ready.sem, 1)
                rsqrt_variance(r, 2 - r)
                with pool.Fori(0, B) as b:
                    pool.wait_ge(*rn_ready(r, 2 * b + 2))
                    pool.tensor_copy(xn_all[:, bass.ds(b * TB, TB), :], xn[:, :, :]).then_inc(rcopy_done.sem, 1)

                pool.wait_ge(zeroed.sem, 16 * B)
                pool.wait_ge(*rcopy_done(r, B))
                for i in range(NT):
                    if i % 4 == 0:
                        pool.wait_ge(*slot_ready(r, i // 4 + 1))
                    for k in range(K):
                        pool.indirect_dma_start(xd[:, :], bass.IndirectOffsetOnAxis(ap=slot[:, i, k:k + 1], axis=0),
                                                xn_all[:, i, :], None).then_inc(scattered.sem, 16)

                PAIRS, PR = NTILE // 2, ERING // 2

                def load_rows(q, i):
                    pool.dma_start(xpair[i], xd[bass.ds(q * 2 * P, 2 * P), :].rearrange("(t p) d -> p t d", p=P)).then_inc(xd_in[i].sem, 16)

                def store_results(q, i):
                    pool.wait_ge(*ya_ready(r, q * 2 + 2))
                    pool.wait_ge(*yv_ready(r, q * 2 + 2))
                    pool.dma_start(yd[bass.ds(q * 2 * P, 2 * P), :].rearrange("(t p) d -> p t d", p=P), ypair[i]).then_inc(y_out[i].sem, 16)
                pool.wait_ge(*scattered(r, 16 * NT * K))
                for q in range(PR):
                    load_rows(q, q)
                with pool.Fori(0, PAIRS // PR - 1) as it:
                    for i in range(PR):
                        q = it * PR + i
                        pool.wait_ge(*eT_done(r, q * 2 + 2))
                        load_rows(q + PR, i)
                        store_results(q, i)
                for i in range(PR):
                    store_results(PAIRS - PR + i, i)

                for i in range(ERING // 2):
                    pool.wait_ge(*y_out[i](r, 16 * NTILE // ERING))
                def batch_rstd(b):
                    pool.wait_ge(bve_ready.sem, b + 1)
                    pool.tensor_tensor(brstd[:, :], bve[:, :], mhalf[:, 0:TB], ALU.pow).then_inc(brstd_ready.sem, 1)
                for b in range(B):
                    for m in range(TB * K):
                        n = b * TB * K + m
                        if n >= GRING:
                            pool.wait_ge(*g_used(r, n - GRING + 1))
                        pool.indirect_dma_start(gring[n % GRING], None, yd[:, :],
                                                bass.IndirectOffsetOnAxis(ap=slot[:, b * TB + m % TB, m // TB:m // TB + 1], axis=0)
                                                ).then_inc(g_in[n % GRING].sem, 16)
                    if r == 0 and b:
                        batch_rstd(b - 1)
                if r == 0:
                    batch_rstd(B - 1)

        @block.tensor
        def _(pe):
            pe.wait_ge(consts_in.sem, 16 * len(FIRST))

            for r in range(2):
                barrier(pe, "pe")

                def project_step(s, i, has):
                    if has[0]:
                        pe.wait_ge(*xn_ready(r, s * 2 + 2))
                        pe.wait_ge(*xt_ready(r, s))
                        for tt in range(TB):
                            for c in range(KC):
                                mm = pe.transpose(ps[0][:, c * S + tt * P:c * S + tt * P + P],
                                                  xn[:, tt, c * P:(c + 1) * P], ident[:, :])
                        mm.then_inc(xT_done.sem, 1)
                    if has[1] and r == 0:
                        pe.wait_ge(sq_ready.sem, s)
                        pe.wait_ge(nrm_ready.sem, s - 1)
                        for c in range(2 * KC):
                            mm = pe.matmul(ps[4][32 * c:32 * c + 32, 0:S], headsum[:, :], sq[:, c * S:(c + 1) * S],
                                           start=True, stop=True)
                        mm.then_inc(ss_done.sem, 1)
                    if has[0]:
                        pe.wait_ge(*xt_ready(r, s + 1))
                        for side in range(2):
                            pe.wait_ge(*qk_raw(r, s * 2))
                            for j in range(2):
                                col = side * D + j * P
                                for c in range(KC):
                                    mm = pe.matmul(ps[1 + side][:, j * S:(j + 1) * S], wqk[r][:, c, col:col + P],
                                                   xt[:, c, :], start=(c == 0), stop=(c == KC - 1))
                            mm.then_inc(qk_done.sem, 1)
                    if has[1] and r == 0:
                        pe.wait_ge(rinv_ready.sem, s)
                        pe.wait_ge(qn_ready.sem, (s - 1) * 3)
                        for c in range(2 * KC):
                            mm = pe.matmul(ps[5 + c // 2 * 2][:, c % 2 * S:c % 2 * S + S], headsel[:, c, :], rinv,
                                           start=True, stop=True)
                        mm.then_inc(spread_done.sem, 1)
                    if has[0]:
                        pe.wait_ge(*v_out(r, s))
                        for tt in range(TB):
                            for c in range(KC):
                                mm = pe.matmul(ps[3][:, tt * D:(tt + 1) * D], xt[:, c, tt * P:(tt + 1) * P],
                                               wv[r][:, c, :], start=(c == 0), stop=(c == KC - 1))
                        mm.then_inc(v_done.sem, 1)
                    if has[1] and r == 0:
                        pe.wait_ge(qn_ready.sem, s * 3)
                        pe.wait_ge(rope_ready.sem, (s - 1) * 2)
                        for side in range(2):
                            mm = pe.matmul(ps[6][:, side * S:(side + 1) * S], rotm[:, :],
                                           qf[1 - i][:, side * 512:side * 512 + S], start=True, stop=True)
                        mm.then_inc(rot_done.sem, 1)
                pipeline(pe, B, 2 - r, 2, project_step)
                barrier(pe, "pe")

                if r == 0:
                    pe.wait_ge(cast_done.sem, 1)
                    pe.wait_ge(later_in.sem, 16 * (len(CONSTS) - len(FIRST) - 1))

                def scores(s, i, h):
                    if h == 0:
                        n = 16 * len(TERMS) * 2
                        b3 = s // 3 if isinstance(s, int) else None
                        pe.wait_ge(*stack_in[i](r, n * (b3 + 1) if b3 is not None else stack_count(s, i, n)))
                    pe.wait_ge(*mx_ready(r, s * H + max(h - 1, 0)))
                    bank = ps[h % 2]
                    for tt in range(TB):
                        keys = (tt + 1) * P if causal(r) else S
                        pe_last = pe.matmul(bank[:, tt * S:tt * S + keys], qs[i][0:KR, h, tt * P:(tt + 1) * P],
                                            ks[i][0:KR, h, 0:keys], start=True, stop=not causal(r))
                        if causal(r):
                            pe_last = pe.matmul(bank[:, tt * S + tt * P:tt * S + (tt + 1) * P], identb, mask_s,
                                                start=False, stop=True)
                    pe_last.then_inc(s1_done.sem, 1)

                def stack_count(s, i, n):
                    return (s - i + 3) * (n // 3)

                def probs(s, i, h):
                    b = s - 1
                    if h % 8 == 0:
                        pe.wait_ge(*nm_ready(r, b * 2 + h // 8 + 1))
                        pe.wait_ge(*nm3_ready(r, b * 2 + h // 8 + 1))
                    pe.wait_ge(*exp_ready(r, b * H + max(h - 1, 0)))
                    bank = ps[2 + h % 2]
                    for kb in range(TB):
                        q0 = kb * P if causal(r) else 0
                        out = bank[:, kb * S:kb * S + S - q0]
                        pe.matmul(out, ks[i][0:KR, h, kb * P:(kb + 1) * P], qs[i][0:KR, h, q0:S],
                                  start=True, stop=False)
                        mm = pe.matmul(out, esel[0:96, h, :], nm[h // 8][0:96, q0:S], start=False, stop=not causal(r))
                        if causal(r):
                            mm = pe.matmul(bank[:, kb * S:kb * S + P], identb, mask_t, start=False, stop=True)
                    mm.then_inc(s2_done.sem, 1)

                def weigh(s, i, h):
                    b, g, j = s - 1, h // 4, h % 4
                    if h == 0:
                        pe.wait_ge(*vb_ready(r, s))
                    pe.wait_ge(*exp_ready(r, b * H + h + 1))
                    if j == 0:
                        pe.wait_ge(*ot_ready(r, b * 4 + max(g - 1, 0)))
                    bank = ps[4 + g % 2]
                    for kb in range(TB):
                        q0 = kb * P if causal(r) else 0
                        mm = pe.matmul(bank[32 * j:32 * j + VW, q0:S], vb[i][:, kb, h, :],
                                       prob[h % 4][:, kb * S:kb * S + S - q0], start=(kb == 0), stop=(kb == TB - 1))
                    mm.then_inc(pv_done.sem, 1)

                def turn_group(s, g):
                    b = s - 1
                    pe.wait_ge(*ot_ready(r, b * 4 + g + 1))
                    pe.wait_ge(*y_ready(r, b * 4 + g))
                    for tt in range(TB):
                        mm = pe.transpose(ps[6][:, tt * P:(tt + 1) * P], ot[g % 2][:, tt * P:(tt + 1) * P], ident[:, :])
                    mm.then_inc(oT_done.sem, 1)

                def turn_output(s):
                    pe.wait_ge(*y_ready(r, s * 4))
                    for tt in range(TB):
                        for c in range(KC):
                            mm = pe.transpose(ps[6][:, c * S + tt * P:c * S + tt * P + P],
                                              yrow[:, tt * D + c * P:tt * D + (c + 1) * P], ident[:, :])
                    mm.then_inc(yT_done.sem, 1)

                def output(s):
                    pe.wait_ge(*yt_ready(r, s))
                    for tt in range(TB):
                        for c in range(KC):
                            mm = pe.matmul(ps[7][:, tt * D:(tt + 1) * D], yt[:, c * S + tt * P:c * S + tt * P + P],
                                           wo[r][:, c, :], start=(c == 0), stop=(c == KC - 1))
                    mm.then_inc(op_done.sem, 1)

                def turn_maxima(s, q):
                    pe.wait_ge(*mx_ready(r, s * H + 8 * q + 8))
                    pe.wait_ge(*rm_ready(r, s * 2 + q))
                    if r == 0 and q == 0:
                        pe.wait_ge(x_added.sem, s - 1 if not isinstance(s, int) or s else 0)
                    for tt in range(TB):
                        mm = pe.transpose(ps[7][0:8, tt * P:(tt + 1) * P], mx[:, tt * H + 8 * q:tt * H + 8 * q + 8], ident[:, :])
                    mm.then_inc(mT_done.sem, 1)

                def attend_step(s, i, has):
                    iprev = (i - 1) % 3
                    finish = has[1] and not (isinstance(s, int) and s == 1)
                    for h in range(H + 2):
                        if h < H and has[0]:
                            scores(s, i, h)
                        if h == 12 and has[0]:
                            turn_maxima(s, 0)
                        if finish and h == 1:
                            turn_group(s - 1, 3)
                        if finish and h == 3 and r == 0:
                            turn_output(s - 1)
                        if finish and h == 6 and r == 0:
                            pe.wait_ge(*rm_ready(r, s * 2))
                            output(s - 1)
                        if has[1]:
                            if h < H:
                                probs(s, iprev, h)
                            if h >= 2:
                                weigh(s, iprev, h - 2)
                            if h >= 8 and h % 4 == 0:
                                turn_group(s, h // 4 - 2)
                    if has[0]:
                        turn_maxima(s, 1)
                pipeline(pe, B, 1, 3, attend_step)
                turn_group(B, 3)
                if r == 0:
                    turn_output(B)
                    output(B)
                if r == 1:
                    def output_step(s, i, has):
                        if has[0]:
                            pe.wait_ge(yb_ready.sem, s + 1)
                            pe.wait_ge(yt1_ready.sem, s)
                            for tt in range(TB):
                                for c in range(KC):
                                    mm = pe.transpose(ps[0][:, c * S + tt * P:c * S + tt * P + P],
                                                      ybuf[i][:, tt * D + c * P:tt * D + (c + 1) * P], ident[:, :])
                            mm.then_inc(yT1_done.sem, 1)
                        if has[1]:
                            pe.wait_ge(yt1_ready.sem, s)
                            pe.wait_ge(x1_added.sem, s - 2 if not isinstance(s, int) or s > 1 else 0)
                            for tt in range(TB):
                                for c in range(KC):
                                    mm = pe.matmul(ps[6 + i][:, tt * D:(tt + 1) * D], ytb[1 - i][:, c * S + tt * P:c * S + tt * P + P],
                                                   wo[r][:, c, :], start=(c == 0), stop=(c == KC - 1))
                            mm.then_inc(op1_done.sem, 1)
                    barrier(pe, "pe")
                    pipeline(pe, B, 1, 2, output_step)
                barrier(pe, "pe")

                def route_step(s, i, has):
                    if has[0]:
                        pe.wait_ge(*rn_ready(r, s * 2 + 2))
                        pe.wait_ge(*xnt_ready(r, s))
                        for tt in range(TB):
                            for c in range(KC):
                                mm = pe.transpose(ps[0][:, c * S + tt * P:c * S + tt * P + P],
                                                  xn[:, tt, c * P:(c + 1) * P], ident[:, :])
                        mm.then_inc(rT_done.sem, 1)
                        pe.wait_ge(*rt_ready(r, s + 1))
                        pe.wait_ge(*nmx_ready(r, s - 1 if not isinstance(s, int) or s else 0))
                        pe.wait_ge(*ex_ready(r, s - 1 if not isinstance(s, int) or s else 0))
                        for tt in range(TB):
                            for c in range(KC):
                                mm = pe.matmul(ps[1 + i][:, tt * E:(tt + 1) * E], xt[:, c, tt * P:(tt + 1) * P],
                                               rw[:, c, :], start=(c == 0), stop=(c == KC - 1))
                        mm.then_inc(lg_done.sem, 1)
                    if has[1]:
                        pe.wait_ge(*msk_ready(r, s))
                        pe.wait_ge(*cum_ready(r, s - 1))
                        pe.wait_ge(*rank_out(r, s - 1))
                        m, c = msk[1 - i], cum[1 - i]
                        pe.matmul(ps[3][:, 0:E], ltri, m[:, 0:E], start=True, stop=False)
                        pe.matmul(ps[3][:, 0:E], onesb, c, start=False, stop=True)
                        pe.matmul(ps[3][:, E:2 * E], ltri, m[:, E:2 * E], start=True, stop=False)
                        pe.matmul(ps[3][:, E:2 * E], onesb, m[:, 0:E], start=False, stop=False)
                        pe.matmul(ps[3][:, E:2 * E], onesb, c, start=False, stop=True).then_inc(rank_done.sem, 1)
                pipeline(pe, B, 1, 2, route_step)
                pe.wait_ge(*cum_ready(r, B))
                pe.matmul(ps[4][:, 0:E], onesb, cum[0], start=True, stop=True).then_inc(cnt_done.sem, 1)

                pe.wait_ge(*xnt_ready(r, B))
                pe.wait_ge(*ex_ready(r, B))
                pe.wait_ge(*nmx_ready(r, B))
                pe.wait_ge(*lg_read(r, B))
                pe.wait_ge(*rank_out(r, B))

                def shared_step(s, i, has):
                    for half in range(2):
                        if has[0]:
                            pe.wait_ge(*sg_ready(r, s * 2 + half if half == 0 else s * 2))
                            for w, bank in ((swg, ps[half]), (swu, ps[2 + half])):
                                for j in range(2):
                                    ch = half * 2 + j
                                    for c in range(KC):
                                        mm = pe.matmul(bank[:, j * S:(j + 1) * S], w[:, c, ch * P:(ch + 1) * P],
                                                       xnt_all[:, c, bass.ds(s * S, S)], start=(c == 0), stop=(c == KC - 1))
                            mm.then_inc(gu_done.sem, 1)
                    if isinstance(s, int) and s == 0:
                        pe.wait_ge(*tef_ready(r, 1))
                        pe.transpose(ps[5][0:1, 0:P], tef, ident[:, :]).then_inc(teT_done.sem, 1)
                    if has[1]:
                        pe.wait_ge(*sg_ready(r, s * 2))
                        pe.wait_ge(*sx_added(r, s - 1))
                        for tt in range(TB):
                            for ch in range(SC):
                                mm = pe.matmul(ps[4][:, tt * D:(tt + 1) * D], sg[1 - i][:, ch, tt * P:(tt + 1) * P],
                                               swd[:, ch, :], start=(ch == 0), stop=(ch == SC - 1))
                        mm.then_inc(sd_done.sem, 1)
                pipeline(pe, B, 1, 2, shared_step)
                barrier(pe, "pe")

                def expert_step(s, i, has):
                    i %= ERING
                    if has[0]:
                        j = s
                        pe.wait_ge(*xd_in[i // 2](r, ring_count(j, i)))
                        pe.wait_ge(*ext_ready(r, j))
                        for c in range(KC):
                            mm = pe.transpose(ps[0][:, c * P:(c + 1) * P], xpair[i // 2][:, i % 2, c * P:(c + 1) * P], ident[:, :])
                        mm.then_inc(eT_done.sem, 1)
                    if has[1]:
                        j, i1 = s - 1, (i - 1) % ERING
                        pe.wait_ge(*w_in[i1](r, ring_count(j, i1)))
                        pe.wait_ge(*ext_ready(r, j + 1))
                        pe.wait_ge(*eh_ready(r, j - 1 if not isinstance(j, int) or j else 0))
                        for c in range(KC):
                            mm = pe.matmul(ps[2 + i1 % 2][:, 0:2 * FF], xdt[i1 % 2][:, c, :], wring[i1][:, c * 128:(c + 1) * 128],
                                           start=(c == 0), stop=(c == KC - 1))
                        mm.then_inc(egu_done.sem, 1)
                    if has[3]:
                        j, i3 = s - 3, (i - 3) % ERING
                        pe.wait_ge(*eh_ready(r, j + 1))
                        pe.wait_ge(*eht_ready(r, j))
                        pe.transpose(ps[4][:, 0:P], eh[i3 % 4], ident[:, :]).then_inc(hT_done.sem, 1)
                    if has[4]:
                        j, i4 = s - 4, (i - 4) % ERING
                        pe.wait_ge(*eht_ready(r, j + 1))
                        pe.wait_ge(*ya_ready(r, j - 1 if not isinstance(j, int) or j else 0))
                        pe.wait_ge(*yv_ready(r, j - 1 if not isinstance(j, int) or j else 0))
                        for half in range(2):
                            mm = pe.matmul(down_bank(i4, half)[:, 0:P], eht[i4 % 2][64 * half:64 * half + 64, :],
                                           wring[i4][64 * half:64 * half + 64, 256:384], start=True, stop=True)
                        mm.then_inc(ed_done.sem, 1)

                def ring_count(j, i):
                    return 16 * (j // ERING + 1) if isinstance(j, int) else (j - i + ERING) * (16 // ERING)
                pipeline(pe, NTILE, 4, 2 * ERING, expert_step)

        @block.scalar
        def _(act):
            def copy(dst, src):
                return act.activation(dst, src, ACT.Copy)

            act.wait_ge(x_in[3].sem, 16)
            for dst, name in CONSTS:
                if name not in FIRST:
                    act.dma_start(dst, t[name]).then_inc((cload_in if name == "cload" else later_in).sem, 16)
            act.wait_ge(setup_done.sem, 2)
            for r in range(2):
                barrier(act, "act")

                def project_step(s, i, has):
                    last = 2 - r
                    if has[0]:
                        act.wait_ge(*xT_done(r, s + 1))
                        act.wait_ge(*v_done(r, s))
                        copy(xt[:, :, :].rearrange("p c n -> p (c n)"), ps[0][:, :]).then_inc(xt_ready.sem, 1)
                    if has[1] and r == 0:
                        act.wait_ge(rinv_ready.sem, s - 1)
                        act.wait_ge(ss_done.sem, s)
                        act.activation(nrm, ps[4][:, 0:S], ACT.Sqrt, bias=epsu).then_inc(nrm_ready.sem, 1)
                    if has[last]:
                        n = s - last
                        k = i if r == 0 else 1 - i
                    if has[last] and r == 0:
                        act.wait_ge(qf_ready.sem, n + 1)
                        first_part(n, k, qf[k])
                    if has[last] and r == 1:
                        second_part(n, k)
                    for side in range(2):
                        if has[0]:
                            if side == 0 and r == 0:
                                act.wait_ge(qn_ready.sem, before(s, 3))
                            elif side == 0:
                                act.wait_ge(*res_ready(r, before(s, 1)))
                            act.wait_ge(*qk_done(r, s * 2 + side + 1))
                            act.activation(qr[i][:, side * 512:(side + 1) * 512], ps[1 + side][:, :], ACT.Copy,
                                           scale=HD ** -0.5 if r == 1 and side == 0 else 1.0).then_inc(qk_raw.sem, 1)
                        if has[last] and side == 0 and r == 0:
                            second_part(n, k)
                    if has[0]:
                        act.wait_ge(*qk_raw(r, s * 2 + 2))
                        if r == 0:
                            act.wait_ge(ss_done.sem, s)
                            act.activation(sq, qr[i], ACT.Square).then_inc(sq_ready.sem, 1)
                        else:
                            first_part(s, i, qr[i])
                        act.wait_ge(*v_done(r, s + 1))
                        copy(v_all[:, bass.ds(s * TB, TB), :, :].rearrange("p t h d -> p (t h d)"), ps[3][:, :]).then_inc(v_out.sem, 1)

                def first_part(n, k, src):
                    act.wait_ge(*parts_stored[k](r, (n - (k if not isinstance(n, int) else n % 2)) * 8))
                    copy(pt[k][:, 0, :], src).then_inc(p1_ready.sem, 1)

                def second_part(n, k):
                    act.wait_ge(*res_ready(r, n + 1))
                    copy(pt[k][:, 1, :], res).then_inc(p2_ready.sem, 1)

                def before(n, per):
                    return max((n - 1) * per, 0) if isinstance(n, int) else (n - 1) * per
                pipeline(act, B, 2 - r, 2, project_step)
                barrier(act, "act")

                def take_turned(s):
                    act.wait_ge(*yT_done(r, s))
                    copy(yt, ps[6][:, :]).then_inc(yt_ready.sem, 1)

                def maxima_part1(b, q):
                    act.wait_ge(*mT_done(r, b * 2 + q + 1))
                    act.wait_ge(*s2_done(r, (b - 1) * H + 8 * q + 8 if not isinstance(b, int) or b else 0))
                    copy(nm[q][0:8, :], ps[7][0:8, 0:S]).then_inc(nm1_ready.sem, 1)

                def maxima_part2(b, q):
                    act.wait_ge(*rm_ready(r, b * 2 + q + 1))
                    act.wait_ge(*nm_ready(r, b * 2 + q))
                    copy(nm2[0:8, :], rm[0:8, :]).then_inc(nm2_ready.sem, 1)
                    copy(nm[q][32:40, :], rm[0:8, :]).then_inc(nm3_ready.sem, 1)

                def attend_step(s, i, has):
                    for h in range(H):
                        if has[1] and h == 1:
                            maxima_part1(s - 1, 1)
                        if has[1] and h == 2:
                            maxima_part2(s - 1, 1)
                        if has[0] and h == 13:
                            maxima_part1(s, 0)
                        if has[0] and h == 15:
                            maxima_part2(s, 0)
                        if has[1]:
                            if h == 4 and r == 0 and not (isinstance(s, int) and s == 1):
                                take_turned(s - 1)
                            b = s - 1
                            act.wait_ge(*s2_done(r, b * H + h + 1))
                            act.wait_ge(*pv_done(r, b * H + max(h - 3, 0)))
                            n = S + P if causal(r) else 2 * S
                            act.activation(prob[h % 4][:, 0:n], ps[2 + h % 2][:, 0:n], ACT.Exp).then_inc(exp_ready.sem, 1)
                pipeline(act, B, 1, 3, attend_step)
                if r == 0:
                    take_turned(B)
                if r == 1:
                    def output_step(s, i, has):
                        if has[0]:
                            act.wait_ge(yT1_done.sem, s + 1)
                            act.wait_ge(op1_done.sem, s - 1 if not isinstance(s, int) or s else 0)
                            copy(ytb[i], ps[0][:, :]).then_inc(yt1_ready.sem, 1)
                    barrier(act, "act")
                    pipeline(act, B, 1, 2, output_step)
                barrier(act, "act")

                def route_step(s, i, has):
                    if has[0]:
                        act.wait_ge(*rT_done(r, s + 1))
                        act.wait_ge(*lg_done(r, s))
                        copy(xt[:, :, :].rearrange("p c n -> p (c n)"), ps[0][:, :]).then_inc(rt_ready.sem, 1)
                        copy(xnt_all[:, :, bass.ds(s * S, S)], ps[0][:, :].rearrange("p (c n) -> p c n", c=KC)).then_inc(xnt_ready.sem, 1)
                    if has[1]:
                        act.wait_ge(*nmx_ready(r, s))
                        for tt in range(TB):
                            ins = act.activation(ex[:, bass.ds((s - 1) * TB + tt, 1), :].rearrange("p a e -> p (a e)"), ps[1 + (1 - i)][:, tt * E:(tt + 1) * E],
                                                 ACT.Exp, bias=nmx[:, tt:tt + 1])
                        ins.then_inc(ex_ready.sem, 1)
                        act.wait_ge(*rank_done(r, s))
                        copy(rank[:, bass.ds((s - 1) * TB, TB), :],
                             ps[3][:, 0:2 * E].rearrange("p (t e) -> p t e", t=TB)).then_inc(rank_out.sem, 1)
                pipeline(act, B, 1, 2, route_step)

                def shared_step(s, i, has):
                    if has[0]:
                        for half in range(2):
                            act.wait_ge(*gu_done(r, s * 2 + half + 1))
                            act.wait_ge(*sga_ready(r, s * 2))
                            act.activation(sth[:, half * 512:(half + 1) * 512], ps[half][:, :], ACT.Tanh,
                                           scale=0.5).then_inc(sth_ready.sem, 1)
                pipeline(act, B, 1, 2, shared_step)
                barrier(act, "act")

                def expert_step(s, i, has):
                    i %= ERING
                    if has[0]:
                        act.wait_ge(*eT_done(r, s + 1))
                        act.wait_ge(*egu_done(r, s - 1 if not isinstance(s, int) or s else 0))
                        copy(xdt[i % 2].rearrange("p c n -> p (c n)"), ps[0][:, 0:D]).then_inc(ext_ready.sem, 1)
                    if has[1]:
                        j, i1 = s - 1, (i - 1) % ERING
                        act.wait_ge(*egu_done(r, j + 1))
                        act.wait_ge(*eg_ready(r, j - 1 if not isinstance(j, int) or j else 0))
                        act.activation(eth[i1 % 2], ps[2 + i1 % 2][:, 0:FF], ACT.Tanh, scale=0.5).then_inc(eth_ready.sem, 1)
                    if has[4]:
                        j, i4 = s - 4, (i - 4) % ERING
                        act.wait_ge(*ed_done(r, j + 1))
                        act.wait_ge(*y_out[i4 // 2](r, stored_count(j, i4)))
                        copy(ypair[i4 // 2][:, i4 % 2, 0:P], down_bank(i4, 0)[:, 0:P]).then_inc(ya_ready.sem, 1)
                pipeline(act, NTILE, 4, 2 * ERING, expert_step)

        @block.vector
        def _(dve):
            dve.memset(zero[:, :], 0.0).then_inc(setup_done.sem, 1)
            dve.memset(epsu, EPS_UNIT).then_inc(setup_done.sem, 1)
            for i in range(NT):
                if i % (NT // 4) == 0:
                    dve.wait_ge(x_in[i // (NT // 4)].sem, 16)
                dve.bn_stats(stats[:, i, :], X[:, i, :]).then_inc(stat_b.sem, 1)
            dve.wait_ge(stat_b.sem, NT)
            for i in range(NT):
                dve.bn_aggr(mv[:, i, :], stats[:, i, :]).then_inc(stat_done.sem, 1)
            dve.wait_ge(stat_done.sem, NT)
            dve.wait_ge(consts_in.sem, 16 * len(FIRST))
            stat_at = NT

            def settle():
                dve.sem_inc(settled.sem, 1)

            def make_rstd(r, n):
                dve.tensor_scalar(ve[:, :], mv[:, :, 1], EPS_LN, None, ALU.add).then_inc(ve_ready.sem, 1)

            def wait_rstd(r, n, b):
                if isinstance(b, int) and b < 2:
                    dve.wait_ge(*rstd_ready(r, 2 * n - 1 + b))

            def normalise(b, done):
                for tt in range(TB):
                    at = bass.ds(b * TB + tt, 1)
                    dve.tensor_scalar(xn[:, tt, :], X[:, at, :].rearrange("p a d -> p (a d)"),
                                      mv[:, at, 0:1].rearrange("p a o -> p (a o)"), rstd[:, at],
                                      ALU.subtract, ALU.mult).then_inc(done.sem, 1)

            def combine(run, b, i):
                for m in range(TB * K):
                    k, tt = m // TB, m % TB
                    dve.wait_ge(*g_in[i * TB * K + m](run, 16 * (b // 2 + 1) if isinstance(b, int) else (b - i + 2) * 8))
                    if k:
                        dve.wait_ge(*g_used(run, b * TB * K + (m - 1)))
                        settle()
                    at = bass.ds(b * TB + tt, 1)
                    xr = X[:, at, :].rearrange("p a d -> p (a d)")
                    dve.scalar_tensor_tensor(out=xr, in0=gring[i * TB * K + m], scalar=comb[:, at, k:k + 1].rearrange("p a o -> p (a o)"),
                                             in1=xr, op0=ALU.mult, op1=ALU.add).then_inc(g_used.sem, 1)

            def batch_norm(b):
                dve.wait_ge(*g_used(0, (b + 1) * TB * K))
                settle()
                for tt in range(TB):
                    dve.bn_stats(bstats[:, tt, :], X[:, bass.ds(b * TB + tt, 1), :].rearrange("p a d -> p (a d)")).then_inc(bstat_done.sem, 1)
                dve.wait_ge(bstat_done.sem, (b + 1) * TB)
                settle()
                for tt in range(TB):
                    dve.bn_aggr(bmv[:, tt, :], bstats[:, tt, :]).then_inc(baggr_done.sem, 1)
                dve.wait_ge(baggr_done.sem, (b + 1) * TB)
                settle()
                dve.tensor_scalar(bve[:, :], bmv[:, :, 1], EPS_LN, None, ALU.add).then_inc(bve_ready.sem, 1)
                dve.wait_ge(brstd_ready.sem, b + 1)
                settle()
                for tt in range(TB):
                    dve.tensor_scalar(xn[:, tt, :], X[:, bass.ds(b * TB + tt, 1), :].rearrange("p a d -> p (a d)"),
                                      bmv[:, tt, 0:1], brstd[:, tt:tt + 1], ALU.subtract, ALU.mult).then_inc(xn_ready.sem, 1)

            for r in range(2):
                barrier(dve, "dve")
                if r == 0:
                    make_rstd(r, 1)

                def project_step(s, i, has):
                    last = 2 - r
                    if has[0] and r == 1:
                        combine(0, s, i)
                    if has[0]:
                        dve.wait_ge(*xT_done(r, s))
                        if r == 0:
                            wait_rstd(r, 1, s)
                            normalise(s, xn_ready)
                        else:
                            batch_norm(s)
                    if r == 0 and has[2]:
                        roped = qf[i].rearrange("p (a n) -> p a n", a=2)[:, :, 0:S]
                        cos = cs[:, 0:1, :].broadcast_to([P, 2, S])
                        sin = cs[:, 1:2, :].broadcast_to([P, 2, S])
                        rt2 = rt.rearrange("p (a n) -> p a n", a=2)
                        dve.wait_ge(rot_done.sem, s - 1)
                        dve.tensor_tensor(rt2, ps[6][:, :].rearrange("p (a n) -> p a n", a=2), sin, ALU.mult).then_inc(rope_ready.sem, 1)
                        dve.tensor_tensor(roped, roped, cos, ALU.mult).then_inc(rope_ready.sem, 1)
                        dve.wait_ge(rope_ready.sem, (s - 1) * 2)
                        dve.tensor_tensor(roped, roped, rt2, ALU.add).then_inc(qf_ready.sem, 1)
                    if has[1] and r == 0:
                        dve.wait_ge(nrm_ready.sem, s)
                        dve.wait_ge(spread_done.sem, s - 1)
                        dve.reciprocal(rinv, nrm).then_inc(rinv_ready.sem, 1)
                    if has[last]:
                        n = s - last
                        src, part = (qf[i], pt[i]) if r == 0 else (qr[1 - i], pt[1 - i])
                        dve.wait_ge(*p1_ready(r, n + 1))
                        dve.wait_ge(*p2_ready(r, n))
                        dve.wait_ge(*p3_ready(r, n))
                        dve.tensor_tensor(res, src, part[:, 0, :], ALU.subtract).then_inc(res_ready.sem, 1)
                        if r == 1:
                            xb = X[:, bass.ds((s - 1) * TB, TB), :]
                            dve.wait_ge(*xn_ready(r, s * 2))
                            dve.tensor_tensor(xb, xb, bproj[:, :].rearrange("p (a d) -> p a d", a=1).broadcast_to([P, TB, D]),
                                              ALU.add).then_inc(bias_added.sem, 1)
                        dve.wait_ge(*p2_ready(r, n + 1))
                        dve.tensor_tensor(part[:, 2, :], res, part[:, 1, :], ALU.subtract).then_inc(p3_ready.sem, 1)
                    if has[1] and r == 0:
                        raw, q = qr[1 - i], qf[1 - i]
                        dve.wait_ge(spread_done.sem, s)
                        for c in range(KC):
                            dve.scalar_tensor_tensor(out=q[:, c * S:(c + 1) * S], in0=raw[:, c * S:(c + 1) * S],
                                                     scalar=gain[:, c:c + 1], in1=ps[5][:, c * S:(c + 1) * S],
                                                     op0=ALU.mult, op1=ALU.mult).then_inc(qn_ready.sem, 1)
                        dve.tensor_tensor(q[:, 512:1024], raw[:, 512:1024], ps[7][:, :], ALU.mult).then_inc(qn_ready.sem, 1)
                pipeline(dve, B, 2 - r, 2, project_step)
                barrier(dve, "dve")
                if r == 0:
                    dve.wait_ge(later_in.sem, 16 * (len(CONSTS) - len(FIRST) - 1))
                for q in range(2):
                    dve.memset(nm[q], 0.0).then_inc(nm_zero.sem, 1)
                dve.wait_ge(nm_zero.sem, 2 * r + 2)

                def group(s, g):
                    b = s - 1
                    if g == 0 and r == 0:
                        dve.wait_ge(yT_done.sem, s - 1)
                    dve.wait_ge(*oT_done(r, b * 4 + g + 1))
                    o4 = ps[6][:, 0:2 * P].rearrange("p (t j w) -> p t j w", t=TB, j=4)
                    rs3 = rs.rearrange("p (t j o) -> p t j o", t=TB, o=1)
                    dve.reciprocal(rs3, o4[:, :, :, HD:HD + 1]).then_inc(rs_ready.sem, 1)
                    dve.wait_ge(*rs_ready(r, b * 4 + g + 1))
                    if r == 0:
                        y4 = yrow.rearrange("p (t g j d) -> p t g j d", t=TB, g=4, j=4)[:, :, g, :, :]
                    else:
                        y4 = y_all.rearrange("p (b t) d -> p t b d", t=TB)[
                            :, :, (4 * g) % B:(4 * g) % B + 4, bass.ds(b * (2 * HD) + HD * (g // 2), HD)]
                    dve.tensor_tensor(y4, o4[:, :, :, 0:HD], rs3.broadcast_to([P, TB, 4, HD]), ALU.mult).then_inc(y_ready.sem, 1)

                def take_group(s, g):
                    b = s - 1
                    dve.wait_ge(*pv_done(r, b * H + 4 * g + 4))
                    dve.wait_ge(*oT_done(r, b * 4 + max(g - 1, 0)))
                    dve.tensor_copy(ot[g % 2], ps[4 + g % 2][:, 0:S]).then_inc(ot_ready.sem, 1)

                def maxima_rest(b, q):
                    dve.wait_ge(*nm1_ready(r, b * 2 + q + 1))
                    dve.wait_ge(*nm3_ready(r, b * 2 + q))
                    dve.tensor_tensor(rm[0:8, :], ps[7][0:8, 0:S], nm[q][0:8, :], ALU.subtract).then_inc(rm_ready.sem, 1)

                def maxima_part3(b, q):
                    dve.wait_ge(*nm2_ready(r, b * 2 + q + 1))
                    dve.tensor_tensor(nm[q][64:72, :], rm[0:8, :], nm2[0:8, :], ALU.subtract).then_inc(nm_ready.sem, 1)

                def attend_step(s, i, has):
                    if has[0]:
                        dve.wait_ge(*mT_done(r, s * 2))
                    finish = has[1] and not (isinstance(s, int) and s == 1)
                    for h in range(H):
                        if has[0]:
                            dve.wait_ge(*s1_done(r, s * H + h + 1))
                            mx2 = mx.rearrange("p (t h) -> p t h", t=TB)[:, :, h]
                            if causal(r):
                                dve.tensor_reduce(mx[:, h:h + 1], ps[h % 2][:, 0:P], AX.X, ALU.max, negate=True)
                                ins = dve.tensor_reduce(mx[:, H + h:H + h + 1], ps[h % 2][:, S:2 * S], AX.X, ALU.max, negate=True)
                            else:
                                ins = dve.tensor_reduce(mx2, ps[h % 2][:, :].rearrange("p (t n) -> p t n", t=TB), AX.X, ALU.max, negate=True)
                            ins.then_inc(mx_ready.sem, 1)
                        if has[1] and h == 1:
                            maxima_rest(s - 1, 1)
                        if has[1] and h == 2:
                            maxima_part3(s - 1, 1)
                        if has[0] and h == 13:
                            maxima_rest(s, 0)
                        if has[0] and h == 15:
                            maxima_part3(s, 0)
                        if finish and h == 1:
                            group(s - 1, 3)
                        if finish and h == 8 and r == 0:
                            dve.wait_ge(op_done.sem, s - 1)
                            add_out(s - 1, x_added, ps[7])
                        if has[1]:
                            if h >= 6 and (h - 6) % 4 == 0:
                                take_group(s, (h - 6) // 4)
                            if h >= 9 and (h - 9) % 4 == 0:
                                group(s, (h - 9) // 4)
                    if has[1]:
                        group(s, 2)
                        take_group(s, 3)

                def add_out(s, added, out):
                    b = s - 1
                    xb = X[:, bass.ds(b * TB, TB), :]
                    dve.tensor_tensor(xb, xb, out[:, :].rearrange("p (t d) -> p t d", t=TB), ALU.add).then_inc(added.sem, 1)
                    dve.wait_ge(added.sem, s)
                    settle()
                    for tt in range(TB):
                        dve.bn_stats(stats[:, bass.ds(b * TB + tt, 1), :].rearrange("p a o -> p (a o)"),
                                     X[:, bass.ds(b * TB + tt, 1), :].rearrange("p a d -> p (a d)")).then_inc(stat_a.sem, 1)
                pipeline(dve, B, 1, 3, attend_step)
                group(B, 3)
                if r == 0:
                    dve.wait_ge(op_done.sem, B)
                    add_out(B, x_added, ps[7])
                if r == 1:
                    def output_step(s, i, has):
                        if has[1]:
                            dve.wait_ge(op1_done.sem, s)
                            add_out(s, x1_added, ps[6 + i])
                    barrier(dve, "dve")
                    dve.wait_ge(bias_added.sem, B)
                    pipeline(dve, B, 1, 2, output_step)
                barrier(dve, "dve")
                dve.wait_ge(*stat_a(r, 2 * B))
                for i in range(NT):
                    dve.bn_aggr(mv[:, i, :], stats[:, i, :]).then_inc(stat_done.sem, 1)
                stat_at += NT
                dve.wait_ge(stat_done.sem, stat_at)
                make_rstd(r, 2 - r)

                dve.memset(cum[0], 0.0).then_inc(cum0.sem, 1)
                dve.memset(one64, 1.0).then_inc(cum0.sem, 1)
                dve.wait_ge(cum0.sem, 2 * r + 2)
                CH = 7

                def route_step(s, i, has):
                    if has[0]:
                        dve.wait_ge(*rT_done(r, s))
                        dve.wait_ge(*rcopy_done(r, s))
                        wait_rstd(r, 2 - r, s)
                        normalise(s, rn_ready)
                    if has[1]:
                        b, c0 = s - 1, (s - 1) * CH + r * (CH * B)
                        lg = ps[1 + (1 - i)][:, 0:2 * E].rearrange("p (t e) -> p t e", t=TB)
                        lb2 = lb.rearrange("p (t e) -> p t e", t=TB)
                        ohb = oh[:, bass.ds(b * TB, TB), :, :].rearrange("p t k e -> p (t k) e")
                        dve.wait_ge(*ex_ready(r, s - 1))
                        dve.wait_ge(*rank_done(r, s - 1))
                        dve.wait_ge(*lg_done(r, s))
                        dve.tensor_tensor(lb2, lg, rb[:, :].rearrange("p (a e) -> p a e", a=1).broadcast_to([P, TB, E]),
                                          ALU.add).then_inc(topk.sem, 1)
                        dve.tensor_reduce(nmx, lg, AX.X, ALU.max, negate=True).then_inc(nmx_ready.sem, 1)
                        dve.wait_ge(topk.sem, c0 + 1)
                        settle()
                        for tt in range(TB):
                            dve.max(m8[:, 8 * tt:8 * tt + 8], lb[:, tt * E:(tt + 1) * E]).then_inc(topk.sem, 1)
                        dve.wait_ge(topk.sem, c0 + 3)
                        settle()
                        for tt in range(TB):
                            dve.max_index(i8[:, 8 * tt:8 * tt + 8], m8[:, 8 * tt:8 * tt + 8], lb[:, tt * E:(tt + 1) * E]).then_inc(topk.sem, 1)
                        dve.wait_ge(topk.sem, c0 + 5)
                        dve.tensor_copy(idxf.rearrange("p (t k) -> p t k", t=TB),
                                        i8.rearrange("p (t k) -> p t k", t=TB)[:, :, 0:K]).then_inc(topk.sem, 1)
                        dve.wait_ge(topk.sem, c0 + 6)
                        dve.tensor_tensor(ohb, iot[:, :].rearrange("p (a e) -> p a e", a=1).broadcast_to([P, TB * K, E]),
                                          idxf.rearrange("p (a o) -> p a o", o=1).broadcast_to([P, TB * K, E]),
                                          ALU.is_equal).then_inc(topk.sem, 1)
                        dve.wait_ge(topk.sem, c0 + 7)
                        settle()
                        with nc.allow_low_precision("counts up to 4 are exact in bf16"):
                            dve.tensor_reduce(msk[1 - i].rearrange("p (t e) -> p t e", t=TB),
                                              oh[:, bass.ds(b * TB, TB), :, :].rearrange("p t k e -> p t e k"),
                                              AX.X, ALU.add).then_inc(msk_ready.sem, 1)
                        dve.wait_ge(*msk_ready(r, s))
                        dve.sem_inc(lg_read.sem, 1)
                        dve.tensor_tensor(cumh, cum[1 - i], msk[1 - i][:, 0:E], ALU.add).then_inc(cum_half.sem, 1)
                        dve.wait_ge(*cum_half(r, s))
                        dve.tensor_tensor(cum[i], cumh, msk[1 - i][:, E:2 * E], ALU.add).then_inc(cum_ready.sem, 1)
                pipeline(dve, B, 1, 2, route_step)

                d = [0]

                def link(ins):
                    d[0] += 1
                    ins.then_inc(disp.sem, 1)
                    dve.wait_ge(disp.sem, disp_base[0] + d[0])
                dve.wait_ge(*cnt_done(r, 1))
                link(dve.tensor_scalar(cnt_i, ps[4][:, 0:E], float(P - 1), None, ALU.add))
                link(dve.tensor_single_scalar(cnt_i, cnt_i, 7, ALU.arith_shift_right))
                link(dve.tensor_copy(ntf, cnt_i))
                link(dve.tensor_tensor_scan(incl, one64, ntf, 0.0, ALU.mult, ALU.add))
                link(dve.tensor_tensor(base, incl, ntf, ALU.subtract))
                link(dve.tensor_scalar(base, base, float(P), None, ALU.mult))
                dve.wait_ge(*rank_out(r, B))
                sm = slotmap.rearrange("p (i e) -> p i e", i=NT)
                link(dve.tensor_tensor(sm, rank[:, :, :], base.rearrange("p (a e) -> p a e", a=1).broadcast_to([P, NT, E]), ALU.add))
                for q in range(4):
                    for i in range(4):
                        ii = 4 * q + i
                        ins = dve.tensor_tensor(prod[:, i * 256:(i + 1) * 256].rearrange("p (k e) -> p k e", k=K), oh[:, ii, :, :],
                                                sm[:, ii:ii + 1, :].broadcast_to([P, K, E]), ALU.mult)
                    link(ins)
                    link(dve.tensor_reduce(slotf, prod.rearrange("p (a e) -> p a e", e=E), AX.X, ALU.add))
                    dve.tensor_copy(slot[:, 4 * q:4 * q + 4, :].rearrange("p i k -> p (i k)"), slotf).then_inc(slot_ready.sem, 1)
                    dve.wait_ge(*slot_ready(r, q + 1))
                link(dve.tensor_scalar(cmp, incl, jcol[:, 0:1], None, ALU.is_le))
                link(dve.tensor_reduce(tef, cmp, AX.X, ALU.add))
                dve.tensor_scalar(tef, tef, float(E - 1), None, ALU.min).then_inc(tef_ready.sem, 1)
                dve.wait_ge(*teT_done(r, 1))
                dve.tensor_copy(te[:, :], ps[5][0:1, 0:P]).then_inc(te_ready.sem, 1)
                disp_base[0] += d[0]

                def gates(b):
                    c0 = b * 4 + r * (4 * B)
                    ohb = oh[:, bass.ds(b * TB, TB), :, :].rearrange("p t k e -> p (t k) e")
                    pr = prod[:, 0:TB * K * E]
                    for tt in range(TB):
                        ins = dve.tensor_tensor(pr[:, tt * K * E:(tt + 1) * K * E].rearrange("p (k e) -> p k e", k=K), ohb[:, tt * K:(tt + 1) * K, :],
                                                ex[:, bass.ds(b * TB + tt, 1), :].broadcast_to([P, K, E]), ALU.mult)
                    ins.then_inc(gate.sem, 1)
                    dve.wait_ge(gate.sem, c0 + 1)
                    dve.tensor_reduce(gk, pr.rearrange("p (a e) -> p a e", e=E), AX.X, ALU.add).then_inc(gate.sem, 1)
                    dve.wait_ge(gate.sem, c0 + 2)
                    dve.tensor_reduce(gs, gk.rearrange("p (t k) -> p t k", t=TB), AX.X, ALU.add).then_inc(gate.sem, 1)
                    dve.wait_ge(gate.sem, c0 + 3)
                    dve.reciprocal(gr, gs).then_inc(gate.sem, 1)
                    dve.wait_ge(gate.sem, c0 + 4)
                    dve.tensor_tensor(comb[:, bass.ds(b * TB, TB), :], gk.rearrange("p (t k) -> p t k", t=TB),
                                      gr.rearrange("p (t o) -> p t o", o=1).broadcast_to([P, TB, K]), ALU.mult)

                def shared_step(s, i, has):
                    if has[0]:
                        for half in range(2):
                            lo, hi = half * 512, (half + 1) * 512
                            dve.wait_ge(*sth_ready(r, s * 2 + half + 1))
                            dve.scalar_tensor_tensor(out=sga[:, lo:hi], in0=sth[:, lo:hi], scalar=1.0, in1=ps[half][:, :],
                                                     op0=ALU.add, op1=ALU.mult).then_inc(sga_ready.sem, 1)
                            dve.wait_ge(*sga_ready(r, s * 2 + half + 1))
                            if half == 0:
                                dve.wait_ge(*sd_done(r, s - 1 if not isinstance(s, int) or s else 0))
                            dve.scalar_tensor_tensor(out=sg[i][:, 2 * half:2 * half + 2, :].rearrange("p c n -> p (c n)"),
                                                     in0=sga[:, lo:hi], scalar=0.5, in1=ps[2 + half][:, :],
                                                     op0=ALU.mult, op1=ALU.mult).then_inc(sg_ready.sem, 1)
                    if has[0]:
                        gates(s)
                    if has[1]:
                        dve.wait_ge(*sd_done(r, s))
                        xb = X[:, bass.ds((s - 1) * TB, TB), :]
                        dve.tensor_tensor(xb, xb, ps[4][:, :].rearrange("p (t d) -> p t d", t=TB), ALU.add).then_inc(sx_added.sem, 1)
                pipeline(dve, B, 1, 2, shared_step)
                barrier(dve, "dve")

                def expert_step(s, i, has):
                    i %= ERING
                    if has[1]:
                        j, i1 = s - 1, (i - 1) % ERING
                        dve.wait_ge(*eth_ready(r, j + 1))
                        dve.scalar_tensor_tensor(out=eg[i1 % 2], in0=eth[i1 % 2], scalar=1.0, in1=ps[2 + i1 % 2][:, 0:FF],
                                                 op0=ALU.add, op1=ALU.mult).then_inc(eg_ready.sem, 1)
                        dve.wait_ge(*eg_ready(r, j + 1))
                        dve.wait_ge(*hT_done(r, j - 3 if not isinstance(j, int) or j > 3 else 0))
                        dve.scalar_tensor_tensor(out=eh[i1 % 4].rearrange("p (a f) -> p a f", a=2),
                                                 in0=eg[i1 % 2].rearrange("p (a f) -> p a f", a=1).broadcast_to([P, 2, FF]), scalar=0.5,
                                                 in1=ps[2 + i1 % 2][:, FF:2 * FF].rearrange("p (a f) -> p a f", a=1).broadcast_to([P, 2, FF]),
                                                 op0=ALU.mult, op1=ALU.mult).then_inc(eh_ready.sem, 1)
                    if has[3]:
                        j, i3 = s - 3, (i - 3) % ERING
                        dve.wait_ge(*hT_done(r, j + 1))
                        dve.wait_ge(*ed_done(r, j - 1 if not isinstance(j, int) or j else 0))
                        dve.tensor_copy(eht[i3 % 2], ps[4][:, 0:P]).then_inc(eht_ready.sem, 1)
                    if has[4]:
                        j, i4 = s - 4, (i - 4) % ERING
                        dve.wait_ge(*ed_done(r, j + 1))
                        dve.wait_ge(*y_out[i4 // 2](r, stored_count(j, i4)))
                        dve.tensor_copy(ypair[i4 // 2][:, i4 % 2, P:D], down_bank(i4, 1)[:, 0:P]).then_inc(yv_ready.sem, 1)
                pipeline(dve, NTILE, 4, 2 * ERING, expert_step)

                if r == 1:
                    for b in range(B):
                        combine(r, b, b % 2)
                dve.drain()


EVEN_FIRST = list(range(0, H, 2)) + list(range(1, H, 2))


def constants():
    eye = np.eye(P, dtype=np.float32)
    cload = np.zeros((P, 2048 + 5 * P), np.float32)
    sel = cload[:, 0:2048].reshape(P, H, P)
    for part in range(3):
        for h in range(H):
            sel[32 * part + h, h, :] = 1.0
    row, col = np.arange(P)[:, None], np.arange(P)[None, :]
    for i, m in enumerate((eye, np.where(col > row, -1e30, 0.0), np.where(row > col, -1e30, 0.0), row < col, np.ones((P, P)))):
        cload[:, 2048 + i * P:2048 + (i + 1) * P] = m
    half = HD // 2
    rotm = np.zeros((P, P), np.float32)
    for m in range(P):
        rotm[m + half if m % HD < half else m - half, m] = -1.0 if m % HD < half else 1.0
    inv = np.float32(10000.0) ** (-np.arange(half, dtype=np.float32) / np.float32(half))
    theta = (np.arange(S, dtype=np.float32)[:, None] * inv[None, :]).astype(np.float32)
    cs = np.stack([np.cos(theta), np.sin(theta)]).astype(np.float32)
    cs = np.ascontiguousarray(cs[:, :, np.arange(P) % half].transpose(2, 0, 1))
    headsum = np.zeros((P, 32), np.float32)
    headsum[np.arange(P), np.arange(P) // HD] = 1.0
    headsel = np.zeros((P, 2 * KC, P), np.float32)
    for c in range(2 * KC):
        headsel[32 * c + np.arange(P) // HD, c, np.arange(P)] = 1.0
    return dict(cload=cload, ident=eye, rotm=rotm, cs=cs, headsum=headsum, headsel=headsel,
                iot=np.tile(np.arange(E, dtype=np.float32), (P, 1)), jcol=np.arange(P, dtype=np.float32)[:, None])


def chunked(w):
    return w.reshape(-1, P, w.shape[1]).transpose(1, 0, 2)


def layout(v):
    g = {k: np.asarray(a) for k, a in v.items()}
    a = dict(constants())
    a["x"] = g["L0_attn_a_x"]
    w = g["L0_attn_a_w_qkv"].reshape(D, 3, H, HD)[:, :, EVEN_FIRST, :].reshape(D, 3 * D)
    a["wqk0"], a["wv0"] = chunked(w[:, :2 * D]), chunked(w[:, 2 * D:])
    a["wo0"] = chunked(g["L0_attn_a_w_out"].reshape(H, HD, D)[EVEN_FIRST].reshape(D, D))
    a["gain"] = np.repeat(g["L0_attn_a_q_gain"][EVEN_FIRST], HD).reshape(KC, P).T
    w = g["L0_attn_b_Wqkv"].reshape(H, 3, HD, D).transpose(3, 1, 0, 2).reshape(D, 3 * D)
    a["wqk1"], a["wv1"] = chunked(w[:, :2 * D]), chunked(w[:, 2 * D:])
    a["wo1"] = chunked(g["L0_attn_b_Wproj"].T)
    a["bproj"] = np.tile(g["L0_attn_b_bproj"], (P, 1))
    a["rw"], a["rb"] = chunked(g["L0_ffn_router_w"]), np.tile(g["L0_ffn_router_bias"], (P, 1))
    a["swg"] = chunked(g["L0_ffn_swg"].transpose(1, 0, 2).reshape(D, SH))
    a["swu"] = chunked(g["L0_ffn_swu"].transpose(1, 0, 2).reshape(D, SH))
    a["swd"] = chunked(g["L0_ffn_swd"].reshape(SH, D))
    gu = np.concatenate([g["L0_ffn_wg"], g["L0_ffn_wu"]], axis=2).reshape(E, KC, P, 2 * FF).transpose(0, 2, 1, 3).reshape(E, P, 4 * FF)
    wd = g["L0_ffn_wd"].reshape(E, FF, 2, P).transpose(0, 2, 1, 3).reshape(E, P, P)
    a["we"] = np.concatenate([gu, wd], axis=2)
    return {k: np.ascontiguousarray(x) for k, x in a.items()}


def kernel(**inputs):
    import concourse.bacc as bacc
    from concourse.bass_utils import run_bass_kernel_spmd

    nc = bacc.Bacc("TRN2", target_bir_lowering=False, num_devices=1)
    arrays = {f"in_{k}": a for k, a in layout(inputs).items()}
    t = {k[3:]: nc.dram_tensor(k, a.shape, F32, kind="ExternalInput").ap() for k, a in arrays.items()}
    t["out"] = nc.dram_tensor("out", (B, S, D), F32, kind="ExternalOutput").ap()
    t["parts"] = nc.dram_tensor("parts", (B, 3, 2 * D, S), BF16, kind="Internal").ap()
    t["xd"] = nc.dram_tensor("xd", (SLOTS, D), F32, kind="Internal").ap()
    t["yd"] = nc.dram_tensor("yd", (SLOTS, D), F32, kind="Internal").ap()
    build(nc, t)
    r = run_bass_kernel_spmd(nc, [arrays], core_ids=[0])
    return r.results[0]["out"]
```
